# Optimizing a Trainium2 kernel written in Bass

```python
import numpy as np
import jax
import jax.numpy as jnp

def _softmax(x, axis=-1):
    return jax.nn.softmax(x, axis=axis)

def _gelu(x):
    return jax.nn.gelu(x, approximate=True)

def _silu(x):
    return jax.nn.silu(x)

def _sigmoid(x):
    return jax.nn.sigmoid(x)

def _layernorm(x, axis=-1, eps=1e-05):
    m = jnp.mean(x, axis=axis, keepdims=True)
    v = jnp.var(x, axis=axis, keepdims=True)
    return (x - m) / jnp.sqrt(v + eps)

def _scatter_add(tgt, idx, src, axis=0):
    return tgt.at[idx].add(src)

def _segment_sum(src, seg, n):
    return jax.ops.segment_sum(src, seg, n)
kernel_name = 'mk_decoder_preln_d1_seqx_r8_5eba38'

def setup_inputs(seed: int=0):
    np.random.seed(seed)
    _w = jnp.asarray

    def _rec_inputs():
        import jax
        import jax.numpy as jnp
        _rk = jax.random.key(seed)
        x = -0.000125 + 0.9999 * jax.random.normal(jax.random.fold_in(_rk, 1), (2, 256, 512), jnp.float32)
        _lenS = 256 - jax.random.randint(jax.random.fold_in(_rk, 7), (2,), 0, max(1, 256 // 4) + 1, jnp.int32)
        _lenS2 = 512 - jax.random.randint(jax.random.fold_in(_rk, 8), (2,), 0, max(1, 512 // 4) + 1, jnp.int32)
        _ctx_4096P = jax.random.normal(jax.random.fold_in(_rk, 11), (2, 16, 512), jnp.float32)
        _ctx_4096c = jax.random.dirichlet(jax.random.fold_in(_rk, 511), 0.3 * jnp.ones((16,), jnp.float32), (2, 512))
        _ctx_4096t = jnp.einsum('bsk,bkd->bsd', _ctx_4096c, _ctx_4096P)
        _ctx_4096t = _ctx_4096t * jax.lax.rsqrt(jnp.mean(jnp.square(_ctx_4096t)) + 1e-12) * 0.953939
        ctx_4096 = -5.72187e-05 + 0.999849 * (_ctx_4096t + 0.3 * jax.random.normal(jax.random.fold_in(_rk, 611), (2, 512, 512), jnp.float32))
        return (x, ctx_4096)
    x, ctx_4096 = _rec_inputs()

    def _L0_attn_setup():
        import jax, jax.numpy as jnp
        import numpy as np
        H_M, P_M, G_M, N_M, K_CONV, CHUNK = (128, 64, 8, 128, 4, 128)
        D_MODEL = 512
        D_INNER = H_M * P_M
        CONV_DIM = D_INNER + 2 * G_M * N_M
        PROJ_DIM = D_INNER + CONV_DIM + H_M
        EPS = 1e-05

        def segsum(x):
            l = x.shape[-1]
            xe = jnp.broadcast_to(x[..., None], x.shape + (l,))
            m1 = jnp.tril(jnp.ones((l, l), dtype=bool), -1)
            s = jnp.cumsum(jnp.where(m1, xe, 0.0), axis=-2)
            m2 = jnp.tril(jnp.ones((l, l), dtype=bool), 0)
            return jnp.where(m2, s, -jnp.inf)

        def causal_conv(x, w, bconv):
            k = w.shape[1]
            s = x.shape[1]
            xp = jnp.pad(x, ((0, 0), (k - 1, 0), (0, 0)))
            y = sum((xp[:, i:i + s, :] * w[:, i] for i in range(k)))
            return y + bconv
        key = jax.random.key(seed)
        ks = jax.random.split(key, 8)
        B_, S = (1, 256)
        sc = 0.02
        return {'x': jax.random.normal(ks[0], (B_, S, D_MODEL), dtype=jnp.float32), 'norm_w': jnp.ones((D_MODEL,), dtype=jnp.float32), 'in_proj_w': jax.random.normal(ks[1], (PROJ_DIM, D_MODEL), dtype=jnp.float32) * sc, 'conv_w': jax.random.normal(ks[2], (CONV_DIM, K_CONV), dtype=jnp.float32) * 0.2, 'conv_b': jnp.zeros((CONV_DIM,), dtype=jnp.float32), 'dt_bias': jax.random.uniform(ks[3], (H_M,), dtype=jnp.float32) * 0.1, 'A_log': jnp.log(1.0 + 15.0 * jax.random.uniform(ks[4], (H_M,), dtype=jnp.float32)), 'Dp': jnp.ones((H_M,), dtype=jnp.float32), 'gnorm_w': jnp.ones((D_INNER,), dtype=jnp.float32), 'out_proj_w': jax.random.normal(ks[5], (D_MODEL, D_INNER), dtype=jnp.float32) * sc}
    _L0_attn_all = _L0_attn_setup()
    _L0_attn_in = {k: v for k, v in _L0_attn_all.items() if k in ('norm_w', 'in_proj_w', 'conv_w', 'conv_b', 'dt_bias', 'A_log', 'Dp', 'gnorm_w', 'out_proj_w')}
    del _L0_attn_all

    def _L0_xattn_setup():
        import jax, jax.numpy as jnp
        import numpy as np
        QMIN = 0.0
        QMAX = 255.0

        def fake_quant(x, scale, zp):
            s = scale.reshape(())
            z = zp.reshape(())
            q = jnp.clip(jnp.round(x / s + z), QMIN, QMAX)
            return (q - z) * s
        key = jax.random.key(seed)
        k1, k2 = jax.random.split(key)
        B, M, K, N = (4, 256, 512, 512)
        x1 = jax.random.normal(k1, (B, M, K), dtype=jnp.float32)
        x2 = jax.random.normal(k2, (B, K, N), dtype=jnp.float32)
        x1_scale = jnp.full((1,), 8.0 / 255.0, dtype=jnp.float32)
        x1_zp = jnp.full((1,), 128.0, dtype=jnp.float32)
        x2_scale = jnp.full((1,), 8.0 / 255.0, dtype=jnp.float32)
        x2_zp = jnp.full((1,), 128.0, dtype=jnp.float32)
        return {'x1': x1, 'x2': x2, 'x1_scale': x1_scale, 'x1_zp': x1_zp, 'x2_scale': x2_scale, 'x2_zp': x2_zp}
    _L0_xattn_all = _L0_xattn_setup()
    _L0_xattn_in = {k: v for k, v in _L0_xattn_all.items() if k in ('x1_scale', 'x1_zp', 'x2_scale', 'x2_zp')}
    del _L0_xattn_all

    def _L0_ffn_setup():
        import jax, jax.numpy as jnp
        import numpy as np
        NUM_EXPERTS = 8
        RANK = 32
        ALPHA = 16.0
        TOP_K = 2
        TEMPERATURE = 1.0
        GAMMA = 0.5
        SOFT_TOPK_TEMP = 0.5
        N_GRAM = 2
        EPS = 1e-06
        key = jax.random.key(seed)
        ks = jax.random.split(key, 6)
        d_in, d_out = (512, 512)
        Bsz, T = (4, 256)
        x = jax.random.normal(ks[0], (Bsz, T, d_in), dtype=jnp.float32)
        W = jax.random.normal(ks[1], (d_out, d_in), dtype=jnp.float32) / np.sqrt(d_in)
        b = jax.random.normal(ks[2], (d_out,), dtype=jnp.float32) * 0.01
        A = jax.random.normal(ks[3], (d_in, RANK), dtype=jnp.float32) / np.sqrt(d_in)
        Bmat = jax.random.normal(ks[4], (RANK, d_out), dtype=jnp.float32) * 0.01
        LiMEs = jax.random.normal(ks[5], (NUM_EXPERTS, RANK), dtype=jnp.float32) * 0.1
        return {'x': x, 'W': W, 'b': b, 'A': A, 'Bmat': Bmat, 'LiMEs': LiMEs}
    _L0_ffn_all = _L0_ffn_setup()
    _L0_ffn_in = {k: v for k, v in _L0_ffn_all.items() if k in ('W', 'b', 'A', 'Bmat', 'LiMEs')}
    del _L0_ffn_all
    return {'x': x, 'ctx_4096': ctx_4096, 'L0_attn_norm_w': _L0_attn_in['norm_w'], 'L0_attn_in_proj_w': _L0_attn_in['in_proj_w'], 'L0_attn_conv_w': _L0_attn_in['conv_w'], 'L0_attn_conv_b': _L0_attn_in['conv_b'], 'L0_attn_dt_bias': _L0_attn_in['dt_bias'], 'L0_attn_A_log': _L0_attn_in['A_log'], 'L0_attn_Dp': _L0_attn_in['Dp'], 'L0_attn_gnorm_w': _L0_attn_in['gnorm_w'], 'L0_attn_out_proj_w': _L0_attn_in['out_proj_w'], 'L0_xattn_x1_scale': _L0_xattn_in['x1_scale'], 'L0_xattn_x1_zp': _L0_xattn_in['x1_zp'], 'L0_xattn_x2_scale': _L0_xattn_in['x2_scale'], 'L0_xattn_x2_zp': _L0_xattn_in['x2_zp'], 'L0_ffn_W': _L0_ffn_in['W'], 'L0_ffn_b': _L0_ffn_in['b'], 'L0_ffn_A': _L0_ffn_in['A'], 'L0_ffn_Bmat': _L0_ffn_in['Bmat'], 'L0_ffn_LiMEs': _L0_ffn_in['LiMEs']}

def reference(x, ctx_4096, L0_attn_norm_w, L0_attn_in_proj_w, L0_attn_conv_w, L0_attn_conv_b, L0_attn_dt_bias, L0_attn_A_log, L0_attn_Dp, L0_attn_gnorm_w, L0_attn_out_proj_w, L0_xattn_x1_scale, L0_xattn_x1_zp, L0_xattn_x2_scale, L0_xattn_x2_zp, L0_ffn_W, L0_ffn_b, L0_ffn_A, L0_ffn_Bmat, L0_ffn_LiMEs):
    import jax
    import jax.numpy as jnp

    def _L0_attn_ref(x, norm_w, in_proj_w, conv_w, conv_b, dt_bias, A_log, Dp, gnorm_w, out_proj_w):
        import jax, jax.numpy as jnp
        import numpy as np
        H_M, P_M, G_M, N_M, K_CONV, CHUNK = (128, 64, 8, 128, 4, 128)
        D_MODEL = 512
        D_INNER = H_M * P_M
        CONV_DIM = D_INNER + 2 * G_M * N_M
        PROJ_DIM = D_INNER + CONV_DIM + H_M
        EPS = 1e-05

        def segsum(x):
            l = x.shape[-1]
            xe = jnp.broadcast_to(x[..., None], x.shape + (l,))
            m1 = jnp.tril(jnp.ones((l, l), dtype=bool), -1)
            s = jnp.cumsum(jnp.where(m1, xe, 0.0), axis=-2)
            m2 = jnp.tril(jnp.ones((l, l), dtype=bool), 0)
            return jnp.where(m2, s, -jnp.inf)

        def causal_conv(x, w, bconv):
            k = w.shape[1]
            s = x.shape[1]
            xp = jnp.pad(x, ((0, 0), (k - 1, 0), (0, 0)))
            y = sum((xp[:, i:i + s, :] * w[:, i] for i in range(k)))
            return y + bconv
        b, s, _ = x.shape
        residual = x
        h = x * jax.lax.rsqrt(jnp.mean(x * x, axis=-1, keepdims=True) + EPS) * norm_w
        proj = jnp.einsum('bsd,od->bso', h, in_proj_w)
        gate = proj[..., :D_INNER]
        hBC = proj[..., D_INNER:D_INNER + CONV_DIM]
        dt = proj[..., D_INNER + CONV_DIM:]
        hBC = jax.nn.silu(causal_conv(hBC, conv_w, conv_b))
        hid = hBC[..., :D_INNER].reshape(b, s, H_M, P_M)
        B = hBC[..., D_INNER:D_INNER + G_M * N_M].reshape(b, s, G_M, N_M)
        C = hBC[..., D_INNER + G_M * N_M:].reshape(b, s, G_M, N_M)
        dt = jax.nn.softplus(dt + dt_bias)
        A = -jnp.exp(A_log)
        pad = -s % CHUNK
        D_res = Dp[None, None, :, None] * hid
        hid_dt = hid * dt[..., None]
        A_full = A[None, None, :] * dt

        def padseq(t):
            return jnp.pad(t, [(0, 0), (0, pad)] + [(0, 0)] * (t.ndim - 2))
        hid_dt, A_full, Bp, Cp = (padseq(hid_dt), padseq(A_full), padseq(B), padseq(C))
        S = s + pad
        c, l = (S // CHUNK, CHUNK)
        hc = hid_dt.reshape(b, c, l, H_M, P_M)
        Ac = A_full.reshape(b, c, l, H_M).transpose(0, 3, 1, 2)
        rep = H_M // G_M
        Bh = jnp.repeat(Bp.reshape(b, c, l, G_M, N_M), rep, axis=3)
        Ch = jnp.repeat(Cp.reshape(b, c, l, G_M, N_M), rep, axis=3)
        A_cs = jnp.cumsum(Ac, axis=-1)
        L = jnp.exp(segsum(Ac))
        M = jnp.einsum('bcihn,bcjhn->bcijh', Ch, Bh) * jnp.transpose(L, (0, 2, 3, 4, 1))
        Y_diag = jnp.einsum('bcijh,bcjhp->bcihp', M, hc)
        decay_states = jnp.exp(A_cs[..., -1:] - A_cs)
        states = jnp.einsum('bclhn,bhcl,bclhp->bchpn', Bh, decay_states, hc)
        A_last = jnp.pad(A_cs[..., -1], ((0, 0), (0, 0), (1, 0)))
        decay_chunk = jnp.exp(segsum(A_last))
        states_cat = jnp.concatenate([jnp.zeros_like(states[:, :1]), states], axis=1)
        prev_states = jnp.einsum('bhij,bjhpn->bihpn', decay_chunk, states_cat)[:, :-1]
        Y_off = jnp.einsum('bclhn,bchpn,bhcl->bclhp', Ch, prev_states, jnp.exp(A_cs))
        y = (Y_diag + Y_off).reshape(b, S, H_M, P_M)[:, :s] + D_res
        y = y.reshape(b, s, D_INNER)
        yg = y * jax.nn.silu(gate)
        gsz = D_INNER // G_M
        ygr = yg.reshape(b, s, G_M, gsz)
        ygr = ygr * jax.lax.rsqrt(jnp.mean(ygr * ygr, axis=-1, keepdims=True) + EPS)
        y = ygr.reshape(b, s, D_INNER) * gnorm_w
        out = jnp.einsum('bsd,od->bso', y, out_proj_w)
        return residual + out

    def _L0_xattn_ref(x1, x2, x1_scale, x1_zp, x2_scale, x2_zp):
        import jax, jax.numpy as jnp
        import numpy as np
        QMIN = 0.0
        QMAX = 255.0

        def fake_quant(x, scale, zp):
            s = scale.reshape(())
            z = zp.reshape(())
            q = jnp.clip(jnp.round(x / s + z), QMIN, QMAX)
            return (q - z) * s
        q1 = fake_quant(x1, x1_scale, x1_zp)
        q2 = fake_quant(x2, x2_scale, x2_zp)
        return jnp.matmul(q1, q2)

    def _L0_ffn_ref(x, W, b, A, Bmat, LiMEs):
        import jax, jax.numpy as jnp
        import numpy as np
        NUM_EXPERTS = 8
        RANK = 32
        ALPHA = 16.0
        TOP_K = 2
        TEMPERATURE = 1.0
        GAMMA = 0.5
        SOFT_TOPK_TEMP = 0.5
        N_GRAM = 2
        EPS = 1e-06
        Bsz, T, d_in = x.shape
        E = LiMEs.shape[0]
        scaling = ALPHA / RANK
        H = jnp.einsum('btd,od->bto', x, W) + b
        z = jnp.einsum('btd,dr->btr', x, A)
        anchors = jnp.arange(N_GRAM - 1, T, N_GRAM)
        H_slice = H[:, anchors, :E]
        delta_slice = jnp.einsum('bar,er->bae', z[:, anchors], LiMEs)
        H_scale = jnp.maximum(jnp.max(jnp.abs(H_slice)), EPS)
        d_scale = jnp.maximum(jnp.max(jnp.abs(delta_slice)), EPS)
        logits = ((1.0 - GAMMA) * (H_slice / H_scale) + GAMMA * (delta_slice / d_scale)) / TEMPERATURE
        probs = jax.nn.softmax(logits, axis=-1)
        topk_vals, _ = jax.lax.top_k(probs, TOP_K)
        thresh = topk_vals[..., -1:]
        mask = jax.nn.sigmoid((probs - thresh) / SOFT_TOPK_TEMP)
        weights = probs * mask
        weights = weights / (jnp.sum(weights, axis=-1, keepdims=True) + 1e-09)
        weights_full = jnp.repeat(weights, N_GRAM, axis=1)
        p_mix = jnp.einsum('bte,er->btr', weights_full, LiMEs)
        delta = jnp.einsum('btr,ro->bto', z * p_mix, Bmat) * scaling
        return H + delta
    x = x + _L0_attn_ref(_layernorm(x, axis=-1), L0_attn_norm_w, L0_attn_in_proj_w, L0_attn_conv_w, L0_attn_conv_b, L0_attn_dt_bias, L0_attn_A_log, L0_attn_Dp, L0_attn_gnorm_w, L0_attn_out_proj_w)
    x = x + _L0_xattn_ref(_layernorm(x, axis=-1), ctx_4096, L0_xattn_x1_scale, L0_xattn_x1_zp, L0_xattn_x2_scale, L0_xattn_x2_zp)
    x = x + _L0_ffn_ref(_layernorm(x, axis=-1), L0_ffn_W, L0_ffn_b, L0_ffn_A, L0_ffn_Bmat, L0_ffn_LiMEs)
    return x

_drawn_inputs = setup_inputs


def setup_inputs(seed=0):
    import zlib

    import numpy as np

    out = dict(_drawn_inputs(seed))
    spreads = {'L0_attn_norm_w': (1.0, 0.2),
     'L0_attn_conv_b': (0.0, 0.1),
     'L0_attn_Dp': (1.0, 0.2),
     'L0_attn_gnorm_w': (1.0, 0.2)}
    factors = {'L0_attn_dt_bias': 8.0,
     'L0_attn_A_log': 4.63,
     'L0_ffn_b': 8.0,
     'L0_ffn_A': 8.0,
     'L0_ffn_Bmat': 8.0,
     'L0_ffn_LiMEs': 8.0}
    for name, (base, spread) in spreads.items():
        noise = np.random.default_rng([zlib.crc32(name.encode()), seed]).standard_normal(out[name].shape)
        drawn = base * np.exp(spread * noise) if base else spread * noise
        out[name] = jnp.asarray(drawn.astype(out[name].dtype))
    for name, factor in factors.items():
        out[name] = (out[name] * factor).astype(out[name].dtype)
    return out
```

```python
import concourse.bass as bass
from concourse import mybir
from contextlib import ExitStack

D = 512
B, S = 2, 256
T = B * S
P = 128
TT = T // P
KT = D // P
HEADS, HD, GROUPS = 128, 64, 8
INNER = HEADS * HD
PAIRS = INNER // P
PPG = PAIRS // GROUPS
TAPS = 4
W_IN = 2 * KT * P
W_ALL = W_IN + D
N_PAR = 8
W_ROW = W_ALL + N_PAR
BC_W = 2 * KT * P
BC_ROW = BC_W + 2 * (TAPS + 1)
CTX = 512
EXPERTS, RANK = 8, 32
MJ = S + P
EPS, EPS_G = 1e-5, 1e-5
ROUND = 1.5 * 2.0 ** 23
OUT_SCALE = 16.0 / RANK


def late(count):
    return not isinstance(count, int) or count > 0


def build(nc, x_d, ctx_d, wdt_d, dtpar_d, normw_d, wmain_d, wbc_d, quant_d, wffn_d, ffnb_d,
          ffna_d, bmat_d, limes_d, limest_d, out_d):
    f32, f32r = mybir.dt.float32, mybir.dt.float32r
    ALU, ACT, AX = mybir.AluOpType, mybir.ActivationFunctionType, mybir.AxisListType
    ds = bass.ds

    with ExitStack() as ctx:
        def sb(name, shape, dt=f32):
            return ctx.enter_context(nc.sbuf_tensor(name, shape, dt))

        def sem(name):
            return ctx.enter_context(nc.semaphore(name))

        cs_dram = nc.dram_tensor("cs_rows", [HEADS, T], f32).ap()

        acc = sb("acc", [P, TT, D])
        hT_hi = sb("hT_hi", [P, KT, T], f32r)
        hT_lo = sb("hT_lo", [P, KT, T], f32r)
        dt_tok = sb("dt_tok", [P, TT, HEADS])
        cs_tok = sb("cs_tok", [P, TT, HEADS])
        w_raw = sb("w_raw", [P, 4, W_ROW])
        win_hi = sb("win_hi", [P, 2, W_IN], f32r)
        win_lo = sb("win_lo", [P, 2, W_IN], f32r)
        wout_hi = sb("wout_hi", [P, 4, D], f32r)
        wout_lo = sb("wout_lo", [P, 4, D], f32r)
        bc_raw = sb("bc_raw", [P, BC_ROW])
        wbc_hi = sb("wbc_hi", [P, BC_W], f32r)
        wbc_lo = sb("wbc_lo", [P, BC_W], f32r)
        csb = sb("csb", [P, 4, 2, T])
        decay = sb("decay", [P, 2, B, 2, MJ])
        cs_own = sb("cs_own", [P, 2, TT, 2])
        cbm = sb("cbm", [P, B, MJ])
        conv = sb("conv", [P, T])
        conv_bc = sb("conv_bc", [P, T])
        hidT = sb("hidT", [P, 2, T])
        gate = sb("gate", [P, 2, T])
        bcT = sb("bcT", [P, 2, T])
        hid_dt = sb("hid_dt", [P, 2, TT, P])
        v = sb("v", [P, T])
        yg = sb("yg", [P, 2, T])
        y_hi = sb("y_hi", [P, 2, T], f32r)
        y_lo = sb("y_lo", [P, 2, T], f32r)
        sq = sb("sq", [P, 2, T])
        sqacc = sb("sqacc", [P, T])
        ms = sb("ms", [P, TT])
        rstd = sb("rstd", [P, TT])
        ident = sb("ident", [P, P])
        causal = sb("causal", [P, MJ])
        ones = sb("ones", [P, P])
        eps_in = sb("eps_in", [P, TT])
        half_neg = sb("half_neg", [P, TT])
        dtpar = sb("dtpar", [P, 2])
        negA = sb("negA", [P, 1])
        normw = sb("normw", [P, KT])
        stats = sb("stats", [P, TT, 6])
        mv = sb("mv", [P, TT, 2])
        qpar = sb("qpar", [P, 4])
        qinv = sb("qinv", [P, 2])
        ctxq = sb("ctxq", [P, B, CTX // P, D])
        normed = decay[:].rearrange("p r b h m -> p (r b h m)")[:, 0:TT * D].rearrange("p (t d) -> p t d", t=TT)
        wdt = csb[:, 0].rearrange("p h t -> p (h t)")[:, 0:KT * P]
        dtT = csb[:, 1, 0, :]
        csT = csb[:, 1, 1, :]
        tmpA = csb[:, 2, 0, :]
        tmpB = csb[:, 2, 1, :]
        tmpC = csb[:, 3, 0, :]
        onesT = csb[:, 3, 1, :]
        wffn = w_raw[:].rearrange("p r w -> p (r w)")[:, 0:KT * D].rearrange("p (k n) -> p k n", k=KT)
        actT = csb[:].rearrange("p r h t -> p (r h t)")[:, 0:KT * T].rearrange("p (k t) -> p k t", k=KT)
        ffn_small = sb("ffn_small", [P, 9, TT, EXPERTS])
        ffn_one = sb("ffn_one", [P, 8, TT])
        odd = sb("odd", [P, 1])
        ffnb = sb("ffnb", [1, D])
        ffna = sb("ffna", [P, KT, RANK])
        bmat = sb("bmat", [RANK, D])
        limes = sb("limes", [EXPERTS, RANK])
        limesT = sb("limesT", [RANK, EXPERTS])
        zT = sb("zT", [RANK, T])
        zp = sb("zp", [RANK, T])
        wT = sb("wT", [EXPERTS, T])

        ps_out = ctx.enter_context(nc.psum_tensor("ps_out", [P, TT, D], f32))
        ps_h = ctx.enter_context(nc.psum_tensor("ps_h", [P, T], f32))
        ps_z = ctx.enter_context(nc.psum_tensor("ps_z", [P, T], f32))
        ps_y = ctx.enter_context(nc.psum_tensor("ps_y", [P, T], f32))
        ps_t = ctx.enter_context(nc.psum_tensor("ps_t", [P, T], f32))

        x_in, pre_in, ctx_in, cs_out = sem("x_in"), sem("pre_in"), sem("ctx_in"), sem("cs_out")
        w_in = [sem(f"w_in{i}") for i in range(4)]
        csb_in = [sem(f"csb_in{i}") for i in range(4)]
        bc_in, ffn_in, stored = sem("bc_in"), sem("ffn_in"), sem("stored")
        pre_dve, pre_act, pre_pool, pre_pe = sem("pre_dve"), sem("pre_act"), sem("pre_pool"), sem("pre_pe")
        pe_hid, pe_gate, pe_bc, pe_cb = sem("pe_hid"), sem("pe_gate"), sem("pe_bc"), sem("pe_cb")
        pe_tr, pe_y, pe_out, pe_ss = sem("pe_tr"), sem("pe_y"), sem("pe_out"), sem("pe_ss")
        act_tap, act_hid, act_gate = sem("act_tap"), sem("act_hid"), sem("act_gate")
        act_tapbc, act_bc, act_exp = sem("act_tapbc"), sem("act_bc"), sem("act_exp")
        act_yhi, act_sq = sem("act_yhi"), sem("act_sq")
        dve_conv, dve_convbc, dve_hiddt = sem("dve_conv"), sem("dve_convbc"), sem("dve_hiddt")
        low_win, low_wout, low_wbc, dve_cb = sem("low_win"), sem("low_wout"), sem("low_wbc"), sem("dve_cb")
        dve_m, dve_v, dve_yg, dve_ylo = sem("dve_m"), sem("dve_v"), sem("dve_yg"), sem("dve_ylo")
        dve_ms, dve_acc, dve_sub = sem("dve_ms"), sem("dve_acc"), sem("dve_sub")
        pool_win, pool_wout, pool_wbc = sem("pool_win"), sem("pool_wout"), sem("pool_wbc")
        pool_own, pool_sq, pool_rstd = sem("pool_own"), sem("pool_sq"), sem("pool_rstd")
        fin_dve, fin_act, fin_pool, fin_pe = sem("fin_dve"), sem("fin_act"), sem("fin_pool"), sem("fin_pe")

        def slots(eng, slot):
            for k in range(PPG):
                slot(eng, k, 0, k, True, False)
            with eng.Fori(1, GROUPS - 1) as g:
                for k in range(PPG):
                    slot(eng, PPG * g + k, g, k, False, False)
            for k in range(PPG):
                slot(eng, PPG * (GROUPS - 1) + k, GROUPS - 1, k, False, True)

        block = ctx.enter_context(nc.Block())

        @block.sync
        def _(eng):
            eng.dma_start(acc[:], x_d.rearrange("b (h p) d -> p (b h) d", p=P)).then_inc(x_in, 16)
            eng.dma_start(normw[:], normw_d).then_inc(pre_in, 16)
            eng.dma_start(wdt, wdt_d).then_inc(pre_in, 16)
            eng.dma_start(dtpar[:], dtpar_d).then_inc(pre_in, 16)
            eng.dma_start(bc_raw[:], wbc_d[0]).then_inc(bc_in, 16)
            eng.dma_start(qpar[:], quant_d.rearrange("a n -> (a n)").partition_broadcast(P)).then_inc(pre_in, 16)
            eng.dma_start(w_raw[:, 0, :], wmain_d[0]).then_inc(w_in[0], 16)
            eng.dma_start(w_raw[:, 1, :], wmain_d[1]).then_inc(w_in[1], 16)
            eng.dma_start(ctxq[:], ctx_d.rearrange("b (k p) d -> p b k d", p=P)).then_inc(ctx_in, 16)
            eng.dma_start(ffnb[:], ffnb_d).then_inc(ffn_in, 16)
            eng.dma_start(ffna[:], ffna_d).then_inc(ffn_in, 16)
            eng.dma_start(bmat[:], bmat_d).then_inc(ffn_in, 16)
            eng.dma_start(limes[:], limes_d).then_inc(ffn_in, 16)
            eng.dma_start(limesT[:], limest_d).then_inc(ffn_in, 16)
            eng.wait_ge(pre_dve, DVE_CS)
            eng.dma_start(cs_dram, csT).then_inc(cs_out, 16)
            eng.wait_ge(cs_out, 16)
            eng.wait_ge(pre_pe, PE_TOK)

            def slot(eng, s, g, k, first, last):
                r = k % 4
                if not (first and k < 2):
                    if late(s - 3):
                        eng.wait_ge(dve_ylo, s - 3)
                    eng.dma_start(w_raw[:, r, :], wmain_d[s]).then_inc(w_in[r], 16)
                if late(s - 3):
                    eng.wait_ge(dve_sub, 8 * s - 24)
                eng.dma_start(csb[:, r].rearrange("p h t -> p (h t)"),
                              cs_dram[ds(2 * s, 2), :].rearrange("h t -> (h t)").partition_broadcast(P)
                              ).then_inc(csb_in[r], 16)
                if k == 1 and not last:
                    eng.wait_ge(act_bc, 2 * g + 2)
                    eng.dma_start(bc_raw[:], wbc_d[g + 1]).then_inc(bc_in, 16)

            slots(eng, slot)
            eng.wait_ge(dve_ylo, PAIRS)
            eng.dma_start(wffn, wffn_d).then_inc(ffn_in, 16)
            for t in range(TT):
                eng.wait_ge(fin_dve, FIN_DONE + t + 1)
                eng.dma_start(out_d[t // 2, (t % 2) * P:(t % 2 + 1) * P, :], acc[:, t, :]).then_inc(stored, 16)
            eng.wait_ge(stored, 16 * TT)

        @block.gpsimd
        def _(eng):
            eng.memset(ident[:], 0.0).then_inc(pre_pool, 1)
            eng.memset(causal[:], 1.0).then_inc(pre_pool, 1)
            eng.memset(eps_in[:], EPS).then_inc(pre_pool, 1)
            eng.memset(half_neg[:], -0.5).then_inc(pre_pool, 1)
            eng.memset(ones[:], 1.0).then_inc(pre_pool, 1)
            eng.wait_ge(pre_pool, 5)
            eng.affine_select(out=ident[:], in_=ident[:], compare_op=ALU.not_equal, fill=1.0, base=0,
                              pattern=[[-1, P]], channel_multiplier=1).then_inc(pre_pool, 1)
            eng.affine_select(out=causal[:, 0:P], in_=causal[:, 0:P], compare_op=ALU.is_ge, fill=0.0,
                              base=0, pattern=[[1, P]], channel_multiplier=-1).then_inc(pre_pool, 1)
            eng.affine_select(out=causal[:, S:S + P], in_=causal[:, S:S + P], compare_op=ALU.is_ge, fill=0.0,
                              base=0, pattern=[[1, P]], channel_multiplier=-1).then_inc(pre_pool, 1)
            eng.wait_ge(pre_dve, DVE_VAR)
            eng.tensor_tensor(rstd[:], ms[:], half_neg[:], ALU.pow).then_inc(pre_pool, 1)
            eng.wait_ge(pre_dve, DVE_MS)
            eng.tensor_tensor(rstd[:], ms[:], half_neg[:], ALU.pow).then_inc(pre_pool, 1)

            def split_in(r4, r2):
                eng.tensor_scalar(win_hi[:, r2, :], w_raw[:, r4, 0:W_IN], 1.0, 0.0, ALU.mult,
                                  ALU.add).then_inc(pool_win, 1)

            def split_out(r4):
                eng.tensor_scalar(wout_hi[:, r4, :], w_raw[:, r4, W_IN:W_ALL], 1.0, 0.0,
                                  ALU.mult, ALU.add).then_inc(pool_wout, 1)

            def lower_in(r4, r2, n):
                eng.wait_ge(pool_win, n)
                eng.tensor_tensor(win_lo[:, r2, :], w_raw[:, r4, 0:W_IN], win_hi[:, r2, :].bitcast(f32),
                                  ALU.subtract).then_inc(low_win, 1)

            def lower_out(r4, n):
                eng.wait_ge(pool_wout, n)
                eng.tensor_tensor(wout_lo[:, r4, :], w_raw[:, r4, W_IN:W_ALL], wout_hi[:, r4, :].bitcast(f32),
                                  ALU.subtract).then_inc(low_wout, 1)

            def lower_bc(n):
                eng.wait_ge(pool_wbc, n)
                eng.tensor_tensor(wbc_lo[:], bc_raw[:, 0:BC_W], wbc_hi[:].bitcast(f32),
                                  ALU.subtract).then_inc(low_wbc, 1)

            eng.wait_ge(bc_in, 16)
            eng.tensor_scalar(wbc_hi[:], bc_raw[:, 0:BC_W], 1.0, 0.0, ALU.mult, ALU.add).then_inc(pool_wbc, 1)
            eng.wait_ge(w_in[0], 16)
            split_in(0, 0)
            split_out(0)
            lower_bc(1)
            lower_in(0, 0, 1)
            lower_out(0, 1)

            eng.wait_ge(pre_act, ACT_TOK)

            def own_sums(s, r2):
                eng.tensor_copy(cs_own[:, r2], cs_tok[:, :, ds(2 * s, 2)]).then_inc(pool_own, 1)

            own_sums(0, 0)

            def slot(eng, s, g, k, first, last):
                r2, r4 = k % 2, k % 4
                n4 = (k + 1) % 4
                if not (last and k == PPG - 1):
                    eng.wait_ge(w_in[n4], 16 * (2 * g + (k + 1) // 4 + 1))
                    if first and 0 < k < 3:
                        eng.wait_ge(pe_gate, s)
                    if late(s - 2):
                        eng.wait_ge(pe_out, s - 2)
                if k == 4 and not last:
                    eng.wait_ge(bc_in, 16 * (g + 2))
                    eng.wait_ge(pe_bc, 2 * g + 2)
                if not (last and k == PPG - 1):
                    if late(s):
                        eng.wait_ge(dve_sub, 8 * s)
                    own_sums(s + 1, 1 - r2)
                if not (last and k == PPG - 1):
                    split_in(n4, (k + 1) % 2)
                    split_out(n4)
                    lower_in(n4, (k + 1) % 2, s + 2)
                    lower_out(n4, s + 2)
                if k == 4 and not last:
                    eng.tensor_scalar(wbc_hi[:], bc_raw[:, 0:BC_W], 1.0, 0.0, ALU.mult, ALU.add).then_inc(pool_wbc, 1)
                    lower_bc(g + 2)
                sum_squares(s, g, k, first)
                if k == 1 and not first:
                    eng.wait_ge(dve_ms, g)
                    eng.tensor_tensor(rstd[:], ms[:], half_neg[:], ALU.pow).then_inc(pool_rstd, 1)

            def sum_squares(s, g, k, first):
                if k == 1 or (first and k == 0):
                    return
                eng.wait_ge(act_sq, s)
                if k == 2:
                    if late(g):
                        eng.wait_ge(pe_ss, g)
                    eng.tensor_tensor(sqacc[:], sq[:, 0, :], sq[:, 1, :], ALU.add).then_inc(pool_sq, 1)
                else:
                    eng.wait_ge(pool_sq, (PPG - 1) * g + k - 2 if k else (PPG - 1) * (g - 1) + PPG - 2)
                    eng.tensor_tensor(sqacc[:], sqacc[:], sq[:, (k - 1) % 2, :], ALU.add).then_inc(pool_sq, 1)

            slots(eng, slot)
            sum_squares(PAIRS, GROUPS, 0, False)
            eng.wait_ge(dve_ms, GROUPS)
            eng.tensor_tensor(rstd[:], ms[:], half_neg[:], ALU.pow).then_inc(pool_rstd, 1)
            eng.wait_ge(fin_dve, FIN_VAR1)
            eng.tensor_tensor(rstd[:], ms[:], half_neg[:], ALU.pow).then_inc(fin_pool, 1)
            eng.wait_ge(fin_dve, FIN_VAR2)
            eng.tensor_tensor(rstd[:], ms[:], half_neg[:], ALU.pow).then_inc(fin_pool, 1)
            eng.wait_ge(fin_dve, FIN_ABS)
            eng.partition_all_reduce(ffn_one[:, 1, 0:2], ffn_one[:, 0, 0:2], P,
                                     bass.bass_isa.ReduceOp.max).then_inc(fin_pool, 1)

        @block.scalar
        def _(eng):
            for t in range(TT):
                eng.wait_ge(pre_dve, DVE_LN + t)
                eng.activation(v[:], normed[:, t, :], ACT.Square, accum_out=ffn_one[:, 0, t:t + 1]).then_inc(pre_act, 1)
                eng.wait_ge(pre_act, t + 1)
            eng.wait_ge(pre_in, 64)
            for k in range(KT):
                eng.wait_ge(pre_pe, k + 1)
                eng.activation(hT_hi[:, k, :], ps_out[:, k, :], ACT.Identity, scale=normw[:, k:k + 1]).then_inc(pre_act, 1)
            eng.wait_ge(pre_dve, DVE_ABS)
            eng.activation(tmpA, tmpA, ACT.Exp, scale=-1.0).then_inc(pre_act, 1)
            eng.activation(negA[:], dtpar[:, 1:2], ACT.Exp).then_inc(pre_act, 1)
            eng.wait_ge(pre_dve, DVE_ONEP)
            eng.activation(tmpC, tmpB, ACT.Ln).then_inc(pre_act, 1)
            eng.wait_ge(pre_pe, PE_TOK - 1)
            eng.activation(dt_tok[:].rearrange("p t h -> p (t h)"), ps_y[:], ACT.Copy).then_inc(pre_act, 1)
            eng.wait_ge(pre_pe, PE_TOK)
            eng.activation(cs_tok[:].rearrange("p t h -> p (t h)"), ps_t[:], ACT.Copy).then_inc(pre_act, 1)

            def tap_bc(which, g):
                base = BC_W + which * (TAPS + 1)
                eng.wait_ge(pe_bc, 2 * g + which + 1)
                if late(2 * g + which):
                    eng.wait_ge(act_bc, 2 * g + which)
                eng.activation(conv_bc[:], ps_z[:], ACT.Identity, bias=bc_raw[:, base + TAPS:base + TAPS + 1],
                               scale=bc_raw[:, base + TAPS - 1:base + TAPS]).then_inc(act_tapbc, 1)

            def silu_bc(which, g):
                eng.wait_ge(dve_convbc, 6 * g + 3 * which + 3)
                if late(2 * g):
                    eng.wait_ge(pe_cb, 2 * g)
                eng.activation(bcT[:, which, :], conv_bc[:], ACT.Silu).then_inc(act_bc, 1)

            tap_bc(0, 0)
            silu_bc(0, 0)

            def slot(eng, s, g, k, first, last):
                r2, r4, q2 = k % 2, k % 4, (k - 1) % 2
                if k == 0:
                    tap_bc(1, g)
                    silu_bc(1, g)
                if k == PPG - 1 and not last:
                    tap_bc(0, g + 1)
                    silu_bc(0, g + 1)
                eng.wait_ge(pe_hid, s + 1)
                eng.wait_ge(w_in[r4], 16 * (2 * g + k // 4 + 1))
                if late(s):
                    eng.wait_ge(act_hid, s)
                eng.activation(conv[:], ps_h[:], ACT.Identity, bias=w_raw[:, r4, W_ALL + 4:W_ALL + 5],
                               scale=w_raw[:, r4, W_ALL + 3:W_ALL + 4]).then_inc(act_tap, 1)
                eng.wait_ge(dve_sub, 8 * s + 8)
                eng.activation(decay[:, r2].rearrange("p b h m -> p (b h m)"),
                               decay[:, r2].rearrange("p b h m -> p (b h m)"), ACT.Exp).then_inc(act_exp, 1)
                eng.wait_ge(dve_conv, 3 * s + 3)
                if late(s - 1):
                    eng.wait_ge(dve_v, s - 1)
                eng.activation(hidT[:, r2, :], conv[:], ACT.Silu).then_inc(act_hid, 1)
                eng.wait_ge(pe_gate, s + 1)
                if late(s - 1):
                    eng.wait_ge(dve_yg, s - 1)
                eng.activation(gate[:, r2, :], ps_z[:], ACT.Silu).then_inc(act_gate, 1)
                if not (first and k == 0):
                    finish_y(s, g, k, first)

            def finish_y(s, g, k, first):
                q2, q4 = (k - 1) % 2, (k - 1) % 4
                eng.wait_ge(dve_yg, s)
                if late(s - 2):
                    eng.wait_ge(pe_out, s - 2)
                eng.activation(y_hi[:, q2, :], yg[:, q2, :], ACT.Copy,
                               scale=w_raw[:, q4, W_ALL + 6:W_ALL + 7]).then_inc(act_yhi, 1)
                if not (first and k < 3):
                    gs, ks = (g, k - 3) if k >= 3 else (g - 1, k - 3 + PPG)
                    eng.wait_ge(pool_sq, (PPG - 1) * gs + max(ks, 1))
                eng.activation(sq[:, q2, :], yg[:, q2, :], ACT.Square).then_inc(act_sq, 1)

            slots(eng, slot)
            finish_y(PAIRS, GROUPS, 0, False)

            for k in range(KT):
                eng.wait_ge(fin_pe, FPE_T1 + k)
                eng.activation(actT[:, k, :], ps_out[:, k, :], ACT.Copy).then_inc(fin_act, 1)
            for k in range(KT):
                eng.wait_ge(fin_pe, FPE_T2 + k)
                eng.activation(actT[:, k, :], ps_out[:, k, :], ACT.Copy).then_inc(fin_act, 1)
            eng.wait_ge(fin_pe, FPE_Z)
            eng.activation(zT[:], ps_h[0:RANK, :], ACT.Copy).then_inc(fin_act, 1)
            eng.wait_ge(fin_dve, FIN_LOGITS)
            eng.activation(ffn_small[:, 3], ffn_small[:, 2], ACT.Exp).then_inc(fin_act, 1)
            eng.wait_ge(fin_dve, FIN_THRESH)
            eng.activation(ffn_small[:, 6], ffn_small[:, 5], ACT.Exp, scale=-2.0).then_inc(fin_act, 1)
            eng.wait_ge(fin_pe, FPE_WT)
            eng.activation(wT[:], ps_y[0:EXPERTS, :], ACT.Copy).then_inc(fin_act, 1)

        @block.vector
        def _(eng):
            n_pre = [0]

            def pre(ins):
                n_pre[0] += 1
                ins.then_inc(pre_dve, 1)

            eng.wait_ge(x_in, 16)
            for t in range(TT):
                pre(eng.bn_stats(stats[:, t, :], acc[:, t, :]))
            for t in range(TT):
                eng.wait_ge(pre_dve, t + 1)
                pre(eng.bn_aggr(mv[:, t, :], stats[:, t, :]))
            eng.wait_ge(pre_dve, n_pre[0])
            pre(eng.tensor_scalar(ms[:], mv[:, :, 1], EPS, None, ALU.add))
            assert n_pre[0] == DVE_VAR
            eng.wait_ge(pre_pool, 9)
            for t in range(TT):
                pre(eng.tensor_scalar(normed[:, t, :], acc[:, t, :], mv[:, t, 0:1], rstd[:, t:t + 1],
                                      ALU.subtract, ALU.mult))
            assert n_pre[0] == DVE_LN + TT - 1
            eng.wait_ge(pre_dve, n_pre[0])
            pre(eng.tensor_tensor(acc[:], acc[:], normed, ALU.add))
            eng.wait_ge(pre_act, TT)
            pre(eng.tensor_scalar(ms[:], ffn_one[:, 0, :], 1.0 / D, EPS, ALU.mult, ALU.add))
            assert n_pre[0] == DVE_MS
            eng.wait_ge(pre_pool, 10)
            eng.wait_ge(pre_dve, n_pre[0])
            for t in range(TT):
                pre(eng.tensor_scalar(normed[:, t, :], normed[:, t, :], rstd[:, t:t + 1], None, ALU.mult))
            assert n_pre[0] == DVE_H
            for k in range(KT):
                eng.wait_ge(pre_act, TT + k + 1)
                pre(eng.scalar_tensor_tensor(out=hT_lo[:, k, :], in0=ps_out[:, k, :], scalar=normw[:, k:k + 1],
                                             in1=hT_hi[:, k, :].bitcast(f32), op0=ALU.mult, op1=ALU.subtract))
            assert n_pre[0] == DVE_HT
            eng.wait_ge(pre_pe, PE_DT)
            pre(eng.tensor_scalar(dtT, ps_h[:], dtpar[:, 0:1], None, ALU.add))
            eng.wait_ge(pre_dve, n_pre[0])
            pre(eng.scalar_tensor_tensor(out=tmpA, in0=dtT, scalar=-1.0, in1=dtT, op0=ALU.mult, op1=ALU.max))
            assert n_pre[0] == DVE_ABS
            pre(eng.memset(onesT, 1.0))
            eng.wait_ge(pre_act, 9)
            pre(eng.tensor_scalar(tmpB, tmpA, 1.0, None, ALU.add))
            assert n_pre[0] == DVE_ONEP
            eng.wait_ge(pre_dve, n_pre[0])
            pre(eng.scalar_tensor_tensor(out=tmpA, in0=tmpB, scalar=-1.0, in1=tmpA, op0=ALU.add, op1=ALU.subtract))
            eng.wait_ge(pre_act, 11)
            pre(eng.reciprocal(tmpB, tmpB))
            eng.wait_ge(pre_dve, n_pre[0])
            pre(eng.tensor_tensor(tmpA, tmpA, tmpB, ALU.mult))
            eng.wait_ge(pre_dve, n_pre[0])
            pre(eng.tensor_tensor(tmpC, tmpC, tmpA, ALU.subtract))
            eng.wait_ge(pre_dve, n_pre[0])
            pre(eng.scalar_tensor_tensor(out=dtT, in0=dtT, scalar=0.0, in1=tmpC, op0=ALU.max, op1=ALU.add))
            eng.wait_ge(pre_dve, n_pre[0])
            eng.wait_ge(pre_act, 10)
            pre(eng.tensor_scalar(tmpA, dtT, negA[:], -1.0, ALU.mult, ALU.mult))
            eng.wait_ge(pre_dve, n_pre[0])
            for b in range(B):
                pre(eng.tensor_tensor_scan(csT[:, b * S:(b + 1) * S], onesT[:, b * S:(b + 1) * S],
                                           tmpA[:, b * S:(b + 1) * S], 0.0, ALU.mult, ALU.add))
            assert n_pre[0] == DVE_CS

            def convolve(out, acc_in, src, w, done, count):
                src_b = src.rearrange("p (b t) -> p b t", b=B)
                out_b = out.rearrange("p (b t) -> p b t", b=B)
                for n, back in enumerate((1, 2, 3)):
                    if n:
                        eng.wait_ge(done, count + n)
                    eng.scalar_tensor_tensor(out=out_b[:, :, back:], in0=src_b[:, :, 0:S - back],
                                             scalar=w[:, TAPS - 1 - back:TAPS - back], in1=out_b[:, :, back:],
                                             op0=ALU.mult, op1=ALU.add).then_inc(done, 1)

            def conv_group(which, g):
                base = BC_W + which * (TAPS + 1)
                eng.wait_ge(act_tapbc, 2 * g + which + 1)
                convolve(conv_bc[:], None, ps_z[:], bc_raw[:, base:base + TAPS], dve_convbc, 6 * g + 3 * which)

            conv_group(0, 0)

            def slot(eng, s, g, k, first, last):
                r2, r4 = k % 2, k % 4
                if not (first and k == 0):
                    scale_hidden(s, k)
                if k == 2 and not first:
                    add_group(g - 1)
                if k == PPG - 1 and not last:
                    conv_group(0, g + 1)
                if k == 0:
                    conv_group(1, g)
                exponents(s, g, k)
                if k == 0:
                    if late(s):
                        eng.wait_ge(dve_m, s)
                    eng.wait_ge(pe_cb, 2 * g + 1)
                    eng.tensor_tensor(cbm[:, 1, :], ps_z[:, 0:MJ], causal[:], ALU.mult).then_inc(dve_cb, 1)
                    eng.wait_ge(pe_cb, 2 * g + 2)
                    eng.tensor_tensor(cbm[:, 0, :], ps_t[:, 0:MJ], causal[:], ALU.mult).then_inc(dve_cb, 1)
                eng.wait_ge(act_tap, s + 1)
                convolve(conv[:], None, ps_h[:], w_raw[:, r4, W_ALL:W_ALL + TAPS], dve_conv, 3 * s)
                if k == 1 and not first:
                    mean_squares(g - 1)
                if not (first and k == 0):
                    combine(s, k)
                eng.wait_ge(act_exp, s + 1)
                if k == 0:
                    eng.wait_ge(dve_cb, 2 * g + 2)
                eng.tensor_tensor(decay[:, r2], decay[:, r2], cbm[:].unsqueeze(2).broadcast_to([P, B, 2, MJ]),
                                  ALU.mult).then_inc(dve_m, 1)
                if not (first and k == 0):
                    lower_y(s, k)

            def exponents(s, g, k):
                r2, r4 = k % 2, k % 4
                eng.wait_ge(csb_in[r4], 16 * (2 * g + k // 4 + 1))
                eng.wait_ge(pool_own, s + 1)
                if late(s - 1):
                    eng.wait_ge(pe_y, s - 1)
                for b in range(B):
                    for h in range(2):
                        for j, (lo, n) in enumerate(((0, S), (S, P))):
                            eng.tensor_scalar(decay[:, r2, b, h, lo:lo + n],
                                              csb[:, r4, h, (b + 1) * S - n:(b + 1) * S],
                                              cs_own[:, r2, 2 * b + j, h:h + 1], 0.0,
                                              ALU.subtract, ALU.min).then_inc(dve_sub, 1)

            def scale_hidden(s, k):
                q2 = (k - 1) % 2
                eng.wait_ge(pe_tr, s)
                if late(s - 2):
                    eng.wait_ge(pe_y, s - 2)
                own = dt_tok[:, :, ds(2 * (s - 1), 2)].unsqueeze(3).broadcast_to([P, TT, 2, HD])
                eng.tensor_tensor(hid_dt[:, q2].rearrange("p t (h c) -> p t h c", h=2),
                                  ps_t[:].rearrange("p (t h c) -> p t h c", t=TT, h=2), own,
                                  ALU.mult).then_inc(dve_hiddt, 1)

            def combine(s, k):
                q2, q4 = (k - 1) % 2, (k - 1) % 4
                eng.wait_ge(pe_y, s)
                eng.wait_ge(act_hid, s)
                if late(s - 1):
                    eng.wait_ge(dve_yg, s - 1)
                eng.scalar_tensor_tensor(out=v[:], in0=hidT[:, q2, :], scalar=w_raw[:, q4, W_ALL + 5:W_ALL + 6],
                                         in1=ps_y[:], op0=ALU.mult, op1=ALU.add).then_inc(dve_v, 1)
                eng.wait_ge(act_gate, s)
                if late(s - 2):
                    eng.wait_ge(dve_ylo, s - 2)
                eng.wait_ge(dve_v, s)
                eng.tensor_tensor(yg[:, q2, :], v[:], gate[:, q2, :], ALU.mult).then_inc(dve_yg, 1)

            def lower_y(s, k):
                q2, q4 = (k - 1) % 2, (k - 1) % 4
                eng.wait_ge(act_yhi, s)
                eng.scalar_tensor_tensor(out=y_lo[:, q2, :], in0=yg[:, q2, :],
                                         scalar=w_raw[:, q4, W_ALL + 6:W_ALL + 7],
                                         in1=y_hi[:, q2, :].bitcast(f32), op0=ALU.mult,
                                         op1=ALU.subtract).then_inc(dve_ylo, 1)

            def mean_squares(g):
                eng.wait_ge(pe_ss, g + 1)
                eng.tensor_scalar(ms[:], ps_t[:, 0:TT], 1.0 / (INNER // GROUPS), EPS_G, ALU.mult,
                                  ALU.add).then_inc(dve_ms, 1)

            def add_group(g):
                eng.wait_ge(pool_rstd, g + 1)
                eng.wait_ge(pe_out, PPG * (g + 1))
                for t in range(TT):
                    eng.scalar_tensor_tensor(out=acc[:, t, :], in0=ps_out[:, t, :], scalar=rstd[:, t:t + 1],
                                             in1=acc[:, t, :], op0=ALU.mult, op1=ALU.add).then_inc(dve_acc, 1)

            slots(eng, slot)
            scale_hidden(PAIRS, 0)
            combine(PAIRS, 0)
            lower_y(PAIRS, 0)
            mean_squares(GROUPS - 1)
            n_fin = [0]

            def fin(ins):
                n_fin[0] += 1
                ins.then_inc(fin_dve, 1)

            def settle():
                eng.wait_ge(fin_dve, n_fin[0])

            def fake_quant(x, inv, scale, zero):
                fin(eng.tensor_scalar(x, x, inv, zero, ALU.mult, ALU.add))
                settle()
                fin(eng.tensor_scalar(x, x, 0.0, 255.0, ALU.max, ALU.min))
                settle()
                fin(eng.tensor_scalar(x, x, ROUND, -ROUND, ALU.add, ALU.add))
                settle()
                fin(eng.tensor_scalar(x, x, zero, scale, ALU.subtract, ALU.mult))
                settle()

            for n in range(2):
                fin(eng.reciprocal(qinv[:, n:n + 1], qpar[:, 2 * n:2 * n + 1]))
            settle()
            eng.wait_ge(ctx_in, 16)
            fake_quant(ctxq[:].rearrange("p b k d -> p (b k d)"), qinv[:, 1:2], qpar[:, 2:3], qpar[:, 3:4])
            assert n_fin[0] == FIN_CTX
            add_group(GROUPS - 1)
            eng.wait_ge(dve_acc, TT * GROUPS)

            def layernorm(norms):
                for t in range(TT):
                    fin(eng.bn_stats(stats[:, t, :], acc[:, t, :]))
                settle()
                for t in range(TT):
                    fin(eng.bn_aggr(mv[:, t, :], stats[:, t, :]))
                settle()
                fin(eng.tensor_scalar(ms[:], mv[:, :, 1], EPS, None, ALU.add))
                eng.wait_ge(fin_pool, norms)
                for t in range(TT):
                    fin(eng.tensor_scalar(normed[:, t, :], acc[:, t, :], mv[:, t, 0:1], rstd[:, t:t + 1],
                                          ALU.subtract, ALU.mult))
                settle()

            layernorm(1)
            fake_quant(normed, qinv[:, 0:1], qpar[:, 0:1], qpar[:, 1:2])
            assert n_fin[0] == FIN_Q
            for t in range(TT):
                eng.wait_ge(fin_pe, FPE_X + t)
                fin(eng.tensor_tensor(acc[:, t, :], acc[:, t, :], ps_out[:, t, :], ALU.add))
            settle()
            layernorm(2)
            assert n_fin[0] == FIN_LN2
            hs, dl, lg, ex, pr, df, sg, wt, ab = (ffn_small[:, i] for i in range(9))
            fin(eng.tensor_reduce(odd[:], ident[:].rearrange("p (n two) -> p n two", two=2)[:, :, 1], AX.X, ALU.add))
            eng.wait_ge(fin_pe, FPE_DS)
            fin(eng.tensor_copy(hs, ps_out[:, :, 0:EXPERTS]))
            fin(eng.tensor_copy(dl, ps_z[:, 0:TT * EXPERTS].rearrange("p (t e) -> p t e", t=TT)))
            settle()
            for n, src in enumerate((hs, dl)):
                fin(eng.scalar_tensor_tensor(out=ab, in0=src, scalar=-1.0, in1=src, op0=ALU.mult, op1=ALU.max))
                settle()
                fin(eng.tensor_reduce(ffn_one[:, 2, n:n + 1], ab, AX.XY, ALU.max))
                settle()
            fin(eng.tensor_scalar(ffn_one[:, 0, 0:2], ffn_one[:, 2, 0:2], odd[:], None, ALU.mult))
            assert n_fin[0] == FIN_ABS
            eng.wait_ge(fin_pool, 3)
            fin(eng.tensor_scalar(ffn_one[:, 3, 0:2], ffn_one[:, 1, 0:2], 1e-6, None, ALU.max))
            settle()
            fin(eng.reciprocal(ffn_one[:, 4, 0:2], ffn_one[:, 3, 0:2]))
            settle()
            fin(eng.tensor_scalar(hs, hs, ffn_one[:, 4, 0:1], 0.5, ALU.mult, ALU.mult))
            fin(eng.tensor_scalar(dl, dl, ffn_one[:, 4, 1:2], 0.5, ALU.mult, ALU.mult))
            settle()
            fin(eng.tensor_tensor(hs, hs, dl, ALU.add))
            settle()
            fin(eng.tensor_reduce(ffn_one[:, 5, :], hs, AX.X, ALU.max))
            settle()
            fin(eng.tensor_tensor(lg, hs, ffn_one[:, 5, :].unsqueeze(2).broadcast_to([P, TT, EXPERTS]), ALU.subtract))
            assert n_fin[0] == FIN_LOGITS
            eng.wait_ge(fin_act, 10)
            fin(eng.tensor_reduce(ffn_one[:, 6, :], ex, AX.X, ALU.add))
            settle()
            fin(eng.reciprocal(ffn_one[:, 7, :], ffn_one[:, 6, :]))
            settle()
            fin(eng.tensor_tensor(pr, ex, ffn_one[:, 7, :].unsqueeze(2).broadcast_to([P, TT, EXPERTS]), ALU.mult))
            settle()
            for t in range(TT):
                fin(eng.max(ab[:, t, :], pr[:, t, :]))
            settle()
            fin(eng.tensor_tensor(df, pr, ab[:, :, 1:2].broadcast_to([P, TT, EXPERTS]), ALU.subtract))
            assert n_fin[0] == FIN_THRESH
            eng.wait_ge(fin_act, 11)
            fin(eng.tensor_scalar(sg, sg, 1.0, None, ALU.add))
            settle()
            fin(eng.reciprocal(sg, sg))
            settle()
            fin(eng.tensor_tensor(wt, pr, sg, ALU.mult))
            settle()
            fin(eng.tensor_reduce(ffn_one[:, 5, :], wt, AX.X, ALU.add))
            settle()
            fin(eng.tensor_scalar(ffn_one[:, 5, :], ffn_one[:, 5, :], 1e-9, None, ALU.add))
            settle()
            fin(eng.reciprocal(ffn_one[:, 6, :], ffn_one[:, 5, :]))
            settle()
            fin(eng.tensor_tensor(wt, wt, ffn_one[:, 6, :].unsqueeze(2).broadcast_to([P, TT, EXPERTS]), ALU.mult))
            assert n_fin[0] == FIN_WT
            eng.wait_ge(fin_pe, FPE_MIX)
            fin(eng.scalar_tensor_tensor(out=zp[:], in0=zT[:], scalar=OUT_SCALE, in1=ps_t[0:RANK, :],
                                         op0=ALU.mult, op1=ALU.mult))
            assert n_fin[0] == FIN_DONE
            for t in range(TT):
                eng.wait_ge(fin_pe, FPE_END + t)
                fin(eng.tensor_tensor(acc[:, t, :], acc[:, t, :], ps_out[:, t, :], ALU.add))

        @block.tensor
        def _(eng):
            mm = nc.tensor.matmul

            def tr(out, src, n=P):
                return nc.tensor.transpose(out, src, ident[:n, :n])

            eng.wait_ge(pre_pool, 8)
            eng.wait_ge(pre_dve, DVE_H)
            for k in range(KT):
                for t in range(TT):
                    last = tr(ps_out[:, k, t * P:(t + 1) * P], normed[:, t, k * P:(k + 1) * P])
                last.then_inc(pre_pe, 1)
            eng.wait_ge(pre_dve, DVE_HT)
            for k in range(KT):
                last = mm(ps_h[:], wdt[:, k * P:(k + 1) * P], hT_hi[:, k, :].bitcast(f32), start=k == 0, stop=False)
            for k in range(KT):
                last = mm(ps_h[:], wdt[:, k * P:(k + 1) * P], hT_lo[:, k, :].bitcast(f32), start=False, stop=k == KT - 1)
            last.then_inc(pre_pe, 1)

            def project(out, w_hi, w_lo, done):
                n = 0
                for w, h in ((w_hi, hT_hi), (w_hi, hT_lo), (w_lo, hT_hi)):
                    for k in range(KT):
                        last = mm(out, w[:, k * P:(k + 1) * P], h[:, k, :], start=n == 0, stop=n == 3 * KT - 1)
                        n += 1
                last.then_inc(done, 1)

            eng.wait_ge(low_wbc, 1)
            project(ps_z[:], wbc_hi[:, 0:KT * P], wbc_lo[:, 0:KT * P], pe_bc)
            eng.wait_ge(pre_dve, DVE_CS)
            for src, out in ((dtT, ps_y), (csT, ps_t)):
                for t in range(TT):
                    last = tr(out[:, t * P:(t + 1) * P], src[:, t * P:(t + 1) * P])
                last.then_inc(pre_pe, 1)
            eng.wait_ge(dve_convbc, 3)
            project(ps_z[:], wbc_hi[:, KT * P:], wbc_lo[:, KT * P:], pe_bc)
            eng.wait_ge(pre_act, ACT_TOK)

            def slot(eng, s, g, k, first, last):
                r2 = k % 2
                eng.wait_ge(low_win, s + 1)
                if late(3 * s):
                    eng.wait_ge(dve_conv, 3 * s)
                project(ps_h[:], win_hi[:, r2, 0:KT * P], win_lo[:, r2, 0:KT * P], pe_hid)
                if not (first and k == 0):
                    scan_heads(s, k)
                if k == 0:
                    eng.wait_ge(act_bc, 2 * g + 2)
                    if late(s):
                        eng.wait_ge(act_gate, s)
                    for b, bank in ((1, ps_z), (0, ps_t)):
                        q = b * S
                        mm(bank[:, 0:S], bcT[:, 0, q:q + P], bcT[:, 1, q:q + S], start=True, stop=True)
                        mm(bank[:, S:MJ], bcT[:, 0, q + P:q + S], bcT[:, 1, q + P:q + S], start=True,
                           stop=True).then_inc(pe_cb, 1)
                if k == 1 and not first:
                    sum_channels(g - 1)
                if late(s):
                    eng.wait_ge(act_gate, s)
                if k == 0:
                    eng.wait_ge(dve_cb, 2 * g + 1)
                if k == PPG - 1 and not last:
                    eng.wait_ge(dve_convbc, 6 * (g + 1) + 3)
                project(ps_z[:], win_hi[:, r2, KT * P:], win_lo[:, r2, KT * P:], pe_gate)
                if not (first and k < 2):
                    project_out(s, g, k)
                eng.wait_ge(act_hid, s + 1)
                if k == 0:
                    eng.wait_ge(dve_cb, 2 * g + 2)
                if k == 1 and not first:
                    eng.wait_ge(dve_ms, g)
                for t in range(TT):
                    done = tr(ps_t[:, t * P:(t + 1) * P], hidT[:, r2, t * P:(t + 1) * P])
                done.then_inc(pe_tr, 1)
                if k >= PPG - 2 and not last:
                    which = k - (PPG - 2)
                    eng.wait_ge(low_wbc, g + 2)
                    eng.wait_ge(act_gate, s + 1)
                    project(ps_z[:], wbc_hi[:, which * KT * P:(which + 1) * KT * P],
                            wbc_lo[:, which * KT * P:(which + 1) * KT * P], pe_bc)

            def scan_heads(s, k):
                q2 = (k - 1) % 2
                eng.wait_ge(dve_hiddt, s)
                eng.wait_ge(dve_m, s)
                if late(s - 1):
                    eng.wait_ge(dve_v, s - 1)
                for h in range(2):
                    for b in range(B):
                        out = ps_y[h * HD:(h + 1) * HD, b * S:(b + 1) * S]
                        mm(out, hid_dt[:, q2, 2 * b, h * HD:(h + 1) * HD], decay[:, q2, b, h, 0:S],
                           start=True, stop=False)
                        done = mm(out[:, P:S], hid_dt[:, q2, 2 * b + 1, h * HD:(h + 1) * HD],
                                  decay[:, q2, b, h, S:MJ], start=False, stop=True)
                done.then_inc(pe_y, 1)

            def project_out(s, g, k):
                pair, q2, q4 = (k - 2) % PPG, (k - 2) % 2, (k - 2) % 4
                eng.wait_ge(dve_ylo, s - 1)
                for t in range(TT):
                    if k == 2 and late(TT * g):
                        eng.wait_ge(dve_acc, TT * (g - 1) + t + 1)
                    for n, (y, w) in enumerate(((y_hi, wout_hi), (y_hi, wout_lo), (y_lo, wout_hi))):
                        done = mm(ps_out[:, t, :], y[:, q2, t * P:(t + 1) * P], w[:, q4, :],
                                  start=pair == 0 and n == 0, stop=pair == PPG - 1 and n == 2)
                done.then_inc(pe_out, 1)

            def sum_channels(g):
                eng.wait_ge(pool_sq, (PPG - 1) * (g + 1))
                for t in range(TT):
                    done = mm(ps_t[:, t:t + 1], sqacc[:, t * P:(t + 1) * P], ones[:, 0:1], start=True, stop=True)
                done.then_inc(pe_ss, 1)

            slots(eng, slot)
            scan_heads(PAIRS, 0)
            project_out(PAIRS, GROUPS, 0)
            sum_channels(GROUPS - 1)
            project_out(PAIRS + 1, GROUPS, 1)

            def transposed(base):
                for k in range(KT):
                    for t in range(TT):
                        done = tr(ps_out[:, k, t * P:(t + 1) * P], normed[:, t, k * P:(k + 1) * P])
                    done.then_inc(fin_pe, 1)

            eng.wait_ge(fin_dve, FIN_Q)
            eng.wait_ge(dve_acc, TT * GROUPS)
            transposed(1)
            eng.wait_ge(fin_act, KT)
            for t in range(TT):
                for k in range(KT):
                    done = mm(ps_out[:, t, :], actT[:, k, t * P:(t + 1) * P], ctxq[:, t // 2, k, :],
                              start=k == 0, stop=k == KT - 1)
                done.then_inc(fin_pe, 1)
            eng.wait_ge(fin_dve, FIN_LN2)
            transposed(2)
            eng.wait_ge(fin_act, 2 * KT)
            eng.wait_ge(ffn_in, 96)
            for k in range(KT):
                done = mm(ps_h[0:RANK, :], ffna[:, k, :], actT[:, k, :], start=k == 0, stop=k == KT - 1)
            done.then_inc(fin_pe, 1)
            for t in range(TT):
                for k in range(KT):
                    mm(ps_out[:, t, :], actT[:, k, t * P:(t + 1) * P], wffn[:, k, :], start=k == 0, stop=False)
                mm(ps_out[:, t, :], ones[0:1, 0:P], ffnb[:], start=False, stop=True)
            eng.wait_ge(fin_act, 9)
            for t in range(TT):
                done = mm(ps_z[:, t * EXPERTS:(t + 1) * EXPERTS], zT[:, t * P:(t + 1) * P], limesT[:],
                          start=True, stop=True)
            done.then_inc(fin_pe, 1)
            eng.wait_ge(fin_dve, FIN_WT)
            for t in range(TT):
                done = tr(ps_y[0:EXPERTS, t * P:(t + 1) * P], ffn_small[:, 7, t, :])
            done.then_inc(fin_pe, 1)
            eng.wait_ge(fin_act, 12)
            anchors = wT[:].rearrange("e (a two) -> e a two", two=2)[:, :, 1:2].broadcast_to([EXPERTS, T // 2, 2])
            mm(ps_t[0:RANK, :], limes[:], anchors, start=True, stop=True).then_inc(fin_pe, 1)
            eng.wait_ge(fin_dve, FIN_DONE)
            for t in range(TT):
                mm(ps_out[:, t, :], zp[:, t * P:(t + 1) * P], bmat[:], start=False, stop=True,
                   skip_group_check=True).then_inc(fin_pe, 1)


DVE_VAR = 2 * TT + 1
DVE_LN = DVE_VAR + 1
DVE_MS = DVE_VAR + TT + 2
DVE_H = DVE_MS + TT
DVE_HT = DVE_H + KT
DVE_ABS = DVE_HT + 2
DVE_ONEP = DVE_ABS + 2
DVE_CS = DVE_ONEP + 6 + B
PE_DT = KT + 1
PE_TOK = PE_DT + 2
ACT_TOK = TT + KT + 5
FIN_CTX = 6
FIN_VAR1 = FIN_CTX + 2 * TT + 1
FIN_Q = FIN_VAR1 + TT + 4
FIN_VAR2 = FIN_Q + TT + 2 * TT + 1
FIN_LN2 = FIN_VAR2 + TT
FIN_ABS = FIN_LN2 + 8
FIN_LOGITS = FIN_ABS + 7
FIN_THRESH = FIN_LOGITS + 3 + TT + 1
FIN_WT = FIN_THRESH + 7
FIN_DONE = FIN_WT + 1
FPE_T1 = 1
FPE_X = KT + 1
FPE_T2 = KT + TT + 1
FPE_Z = 2 * KT + TT + 1
FPE_DS = FPE_Z + 1
FPE_WT = FPE_DS + 1
FPE_MIX = FPE_WT + 1
FPE_END = FPE_MIX + 1


def lay_out(i):
    import numpy as np

    a = {k: np.asarray(x) for k, x in i.items()}

    def by_width(w):
        return w.T.reshape(KT, P, -1).transpose(1, 0, 2)

    win, conv_w, conv_b = a["L0_attn_in_proj_w"], a["L0_attn_conv_w"], a["L0_attn_conv_b"]
    gates, hidden = win[:INNER], win[INNER:2 * INNER]
    gn = GROUPS * P
    rows_b, rows_c = win[2 * INNER:2 * INNER + gn], win[2 * INNER + gn:2 * INNER + 2 * gn]
    rows_dt = win[2 * INNER + 2 * gn:]
    wout = a["L0_attn_out_proj_w"].T
    d_ch = np.repeat(a["L0_attn_Dp"], HD)
    gnorm = a["L0_attn_gnorm_w"]
    wmain = np.zeros((PAIRS, P, W_ROW), np.float32)
    for s in range(PAIRS):
        c = slice(s * P, (s + 1) * P)
        wmain[s, :, 0:KT * P] = by_width(hidden[c]).reshape(P, -1)
        wmain[s, :, KT * P:W_IN] = by_width(gates[c]).reshape(P, -1)
        wmain[s, :, W_IN:W_ALL] = wout[c]
        wmain[s, :, W_ALL:W_ALL + TAPS] = conv_w[c]
        wmain[s, :, W_ALL + 4] = conv_b[c]
        wmain[s, :, W_ALL + 5] = d_ch[c]
        wmain[s, :, W_ALL + 6] = gnorm[c]
    wbc = np.zeros((GROUPS, P, BC_ROW), np.float32)
    for g in range(GROUPS):
        c = slice(g * P, (g + 1) * P)
        for n, rows in enumerate((rows_b, rows_c)):
            at = BC_W + n * (TAPS + 1)
            cc = slice(INNER + n * gn + g * P, INNER + n * gn + (g + 1) * P)
            wbc[g, :, n * KT * P:(n + 1) * KT * P] = by_width(rows[c]).reshape(P, -1)
            wbc[g, :, at:at + TAPS] = conv_w[cc]
            wbc[g, :, at + TAPS] = conv_b[cc]
    return {
        "x": a["x"], "ctx": a["ctx_4096"],
        "wdt": by_width(rows_dt).reshape(P, -1),
        "dtpar": np.stack([a["L0_attn_dt_bias"], a["L0_attn_A_log"]], 1),
        "normw": a["L0_attn_norm_w"].reshape(KT, P).T,
        "wmain": wmain, "wbc": wbc,
        "quant": np.stack([a["L0_xattn_x1_scale"], a["L0_xattn_x1_zp"], a["L0_xattn_x2_scale"],
                           a["L0_xattn_x2_zp"]], 0),
        "wffn": by_width(a["L0_ffn_W"]), "ffnb": a["L0_ffn_b"].reshape(1, D),
        "ffna": a["L0_ffn_A"].reshape(KT, P, RANK).transpose(1, 0, 2),
        "bmat": a["L0_ffn_Bmat"], "limes": a["L0_ffn_LiMEs"], "limest": a["L0_ffn_LiMEs"].T,
    }


def kernel(**inputs):
    import numpy as np
    import concourse.bacc as bacc
    from concourse import mybir as mb
    from concourse.bass_utils import run_bass_kernel_spmd

    nc = bacc.Bacc("TRN2", target_bir_lowering=False, num_devices=1)
    arrays, args = {}, []
    for name, a in lay_out(inputs).items():
        a = np.ascontiguousarray(a)
        arrays[f"in_{name}"] = a
        args.append(nc.dram_tensor(f"in_{name}", a.shape, mb.dt.from_np(a.dtype), kind="ExternalInput").ap())
    args.append(nc.dram_tensor("out_x", (B, S, D), mb.dt.float32, kind="ExternalOutput").ap())
    build(nc, *args)
    r = run_bass_kernel_spmd(nc, [arrays], core_ids=[0])
    return r.results[0]["out_x"]
```

```python
import concourse.bass as bass
from concourse import mybir
from contextlib import ExitStack

D = 512
B, S = 2, 256
T = B * S
P = 128
TT = T // P
KT = D // P
HEADS, HD, GROUPS = 128, 64, 8
INNER = HEADS * HD
PAIRS = INNER // P
PPG = PAIRS // GROUPS
TAPS = 4
W_IN = 2 * KT * P
W_ALL = W_IN + D
N_PAR = 8
W_ROW = W_ALL + N_PAR
BC_W = 2 * KT * P
BC_ROW = BC_W + 2 * (TAPS + 1)
CTX = 512
EXPERTS, RANK = 8, 32
GATE = RANK + EXPERTS
CHUNK = B * CTX * D // P // PPG
MJ = S + P
EPS, EPS_G = 1e-5, 1e-5
ROUND = 1.5 * 2.0 ** 23
OUT_SCALE = 16.0 / RANK


def late(count):
    return not isinstance(count, int) or count > 0


def build(nc, x_d, ctx_d, wdt_d, dtpar_d, normw_d, wmain_d, wbc_d, quant_d, wffn_d, ffnb_d,
          gate_d, bmat_d, limes_d, limest_d, out_d):
    f32, f32r, bf16 = mybir.dt.float32, mybir.dt.float32r, mybir.dt.bfloat16
    ALU, ACT, AX = mybir.AluOpType, mybir.ActivationFunctionType, mybir.AxisListType
    ds = bass.ds

    with ExitStack() as ctx:
        def sb(name, shape, dt=f32):
            return ctx.enter_context(nc.sbuf_tensor(name, shape, dt))

        def sem(name):
            return ctx.enter_context(nc.semaphore(name))

        cs_dram = nc.dram_tensor("cs_rows", [HEADS, T], f32).ap()

        acc = sb("acc", [P, TT, D])
        hT_hi = sb("hT_hi", [P, KT, T], f32r)
        hT_lo = sb("hT_lo", [P, KT, T], f32r)
        dt_tok = sb("dt_tok", [P, TT, HEADS])
        cs_tok = sb("cs_tok", [P, TT, HEADS])
        w_raw = sb("w_raw", [P, 4, W_ROW])
        win_hi = sb("win_hi", [P, 2, W_IN], f32r)
        win_lo = sb("win_lo", [P, 2, W_IN], f32r)
        wout_hi = sb("wout_hi", [P, 4, D], f32r)
        wout_lo = sb("wout_lo", [P, 4, D], f32r)
        bc_raw = sb("bc_raw", [P, BC_ROW])
        wbc_hi = sb("wbc_hi", [P, BC_W], f32r)
        wbc_lo = sb("wbc_lo", [P, BC_W], f32r)
        csb = sb("csb", [P, 4, 2, T])
        decay = sb("decay", [P, 2, B, 2, MJ])
        cs_own = sb("cs_own", [P, 2, TT, 2])
        cbm = sb("cbm", [P, B, MJ])
        conv = sb("conv", [P, T])
        conv_bc = sb("conv_bc", [P, T])
        hidT = sb("hidT", [P, 2, T])
        gate = sb("gate", [P, 2, T])
        bcT = sb("bcT", [P, 2, T])
        hid_dt = sb("hid_dt", [P, 2, TT, P])
        v = sb("v", [P, T])
        yg = sb("yg", [P, 2, T])
        y_hi = sb("y_hi", [P, 2, T], f32r)
        y_lo = sb("y_lo", [P, 2, T], f32r)
        sq = sb("sq", [P, 2, T])
        sqacc = sb("sqacc", [P, T])
        ms = sb("ms", [P, TT])
        rstd = sb("rstd", [P, TT])
        ident = sb("ident", [P, P])
        causal = sb("causal", [P, MJ])
        ones = sb("ones", [P, P])
        eps_in = sb("eps_in", [P, TT])
        half_neg = sb("half_neg", [P, TT])
        dtpar = sb("dtpar", [P, 2])
        negA = sb("negA", [P, 1])
        normw = sb("normw", [P, KT])
        stats = sb("stats", [P, TT, 6])
        mv = sb("mv", [P, TT, 2])
        qpar = sb("qpar", [P, 4])
        qinv = sb("qinv", [P, 2])
        ctxq = sb("ctxq", [P, B, CTX // P, D])
        wffn_hi = sb("wffn_hi", [P, 2 * D], f32r)
        wffn_lo = sb("wffn_lo", [P, 2 * D], f32r)
        gate_raw = sb("gate_raw", [P, KT, GATE])
        gate_hi = sb("gate_hi", [P, KT, GATE], f32r)
        gate_lo = sb("gate_lo", [P, KT, GATE], f32r)
        lnv = sb("lnv", [P, 2, TT])
        lnr = sb("lnr", [P, 2, TT])
        biasb = sb("biasb", [P, D])
        odd = sb("odd", [P, 1])
        limes = sb("limes", [EXPERTS, RANK])
        limesT = sb("limesT", [RANK, EXPERTS])
        ffn_small = sb("ffn_small", [P, 9, TT, EXPERTS])
        ffn_one = sb("ffn_one", [P, 8, TT])

        normed = decay[:].rearrange("p r b h m -> p (r b h m)")[:, 0:TT * D].rearrange("p (t d) -> p t d", t=TT)
        hnorm = w_raw[:, 2:4].rearrange("p r w -> p (r w)")[:, 0:TT * D].rearrange("p (t d) -> p t d", t=TT)
        wdt = csb[:, 0].rearrange("p h t -> p (h t)")[:, 0:KT * P]
        wdt_hi, wdt_lo = y_hi[:, 0, :], y_lo[:, 0, :]
        dtT, csT = csb[:, 1, 0, :], csb[:, 1, 1, :]
        tmpA, tmpB, tmpC, onesT = csb[:, 2, 0, :], csb[:, 2, 1, :], csb[:, 3, 0, :], csb[:, 3, 1, :]
        ctx_hi = (hT_hi, hT_lo)
        ctx_lo = (win_hi[:].rearrange("p r w -> p (r w)").rearrange("p (k d) -> p k d", k=KT),
                  win_lo[:].rearrange("p r w -> p (r w)").rearrange("p (k d) -> p k d", k=KT))
        qscaled = csb[:].rearrange("p r h t -> p (r h t)")[:, 0:TT * D].rearrange("p (t d) -> p t d", t=TT)
        qvalue = csb[:].rearrange("p r h t -> p (r h t)")[:, TT * D:].rearrange("p (t d) -> p t d", t=TT)
        qround = gate[:].rearrange("p r t -> p (r t)").bitcast(bf16).rearrange("p (t d) -> p t d", t=TT)
        identb = sb("identb", [P, P], bf16)
        xT_hi, xT_lo = wout_hi, wout_lo
        zh = v[0:GATE, :]
        zp = conv[0:RANK, :]
        wT = conv_bc[0:EXPERTS, :]
        bmat = sqacc[0:RANK, :]
        zst = y_hi[0:3 * RANK, 0, :]
        bst = y_lo[0:3 * RANK, 0, :]

        def wffn(k, lower):
            if k < 2:
                return (wbc_lo if lower else wbc_hi)[:, k * D:(k + 1) * D]
            return (wffn_lo if lower else wffn_hi)[:, (k - 2) * D:(k - 1) * D]

        ps_out = ctx.enter_context(nc.psum_tensor("ps_out", [P, TT, D], f32))
        ps_h = ctx.enter_context(nc.psum_tensor("ps_h", [P, T], f32))
        ps_z = ctx.enter_context(nc.psum_tensor("ps_z", [P, T], f32))
        ps_y = ctx.enter_context(nc.psum_tensor("ps_y", [P, T], f32))
        ps_t = ctx.enter_context(nc.psum_tensor("ps_t", [P, T], f32))
        work = (ps_h, ps_z, ps_y, ps_t)

        x_in = [sem(f"x_in{t}") for t in range(TT)]
        wdt_in, pre_in, ctx_in, cs_out = sem("wdt_in"), sem("pre_in"), sem("ctx_in"), sem("cs_out")
        w_in = [sem(f"w_in{i}") for i in range(4)]
        csb_in = [sem(f"csb_in{i}") for i in range(4)]
        bc_in, ffn_in, bmat_in, stored = sem("bc_in"), sem("ffn_in"), sem("bmat_in"), sem("stored")
        pre_dve, pre_act, pre_pool, pre_pe = sem("pre_dve"), sem("pre_act"), sem("pre_pool"), sem("pre_pe")
        pe_hid, pe_gate, pe_bc, pe_cb = sem("pe_hid"), sem("pe_gate"), sem("pe_bc"), sem("pe_cb")
        pe_tr, pe_y, pe_out, pe_ss = sem("pe_tr"), sem("pe_y"), sem("pe_out"), sem("pe_ss")
        act_tap, act_hid, act_gate = sem("act_tap"), sem("act_hid"), sem("act_gate")
        act_tapbc, act_bc, act_exp = sem("act_tapbc"), sem("act_bc"), sem("act_exp")
        act_yhi, act_sq = sem("act_yhi"), sem("act_sq")
        dve_conv, dve_convbc, dve_hiddt = sem("dve_conv"), sem("dve_convbc"), sem("dve_hiddt")
        low_win, low_wout, low_wbc, dve_cb = sem("low_win"), sem("low_wout"), sem("low_wbc"), sem("dve_cb")
        dve_m, dve_v, dve_yg, dve_ylo = sem("dve_m"), sem("dve_v"), sem("dve_yg"), sem("dve_ylo")
        dve_ms, dve_acc, dve_sub = sem("dve_ms"), sem("dve_acc"), sem("dve_sub")
        pool_win, pool_wout, pool_wbc = sem("pool_win"), sem("pool_wout"), sem("pool_wbc")
        pool_own, pool_sq, pool_rstd = sem("pool_own"), sem("pool_sq"), sem("pool_rstd")
        dve_ctx, dve_half = sem("dve_ctx"), sem("dve_half")
        ctxhi_done, ctxlo_done, ctxlo1_done = sem("ctxhi_done"), sem("ctxlo_done"), sem("ctxlo1_done")
        bst_done, bstlo_done, gate_split, gate_low = sem("bst_done"), sem("bstlo_done"), sem("gate_split"), sem("gate_low")
        ln_step, ln_var, ln_root, ln_out = sem("ln_step"), sem("ln_var"), sem("ln_root"), sem("ln_out")
        q_scaled, q_step, q_round = sem("q_scaled"), sem("q_step"), sem("q_round")
        q_tr, q_value, q_hi, q_lo = sem("q_tr"), sem("q_value"), sem("q_hi"), sem("q_lo")
        x_mm, x_add, n_tr, n_hi, n_lo = sem("x_mm"), sem("x_add"), sem("n_tr"), sem("n_hi"), sem("n_lo")
        g_mm, g_copy, h_mm, bias_add = sem("g_mm"), sem("g_copy"), sem("h_mm"), sem("bias_add")
        mix_dve, mix_act, mix_pool, mix_pe = sem("mix_dve"), sem("mix_act"), sem("mix_pool"), sem("mix_pe")
        d_mm, y_done, h_turned = sem("d_mm"), sem("y_done"), sem("h_turned")

        def slots(eng, slot):
            for k in range(PPG):
                slot(eng, k, 0, k, True, False)
            with eng.Fori(1, GROUPS - 1) as g:
                for k in range(PPG):
                    slot(eng, PPG * g + k, g, k, False, False)
            for k in range(PPG):
                slot(eng, PPG * (GROUPS - 1) + k, GROUPS - 1, k, False, True)

        block = ctx.enter_context(nc.Block())

        @block.sync
        def _(eng):
            for t in range(TT):
                eng.dma_start(acc[:, t, :], x_d[t // 2, (t % 2) * P:(t % 2 + 1) * P, :]).then_inc(x_in[t], 16)
            eng.dma_start(wdt, wdt_d).then_inc(wdt_in, 16)
            eng.dma_start(bc_raw[:], wbc_d[0]).then_inc(bc_in, 16)
            eng.dma_start(normw[:], normw_d).then_inc(pre_in, 16)
            eng.dma_start(dtpar[:], dtpar_d).then_inc(pre_in, 16)
            eng.dma_start(w_raw[:, 0, :], wmain_d[0]).then_inc(w_in[0], 16)
            eng.dma_start(w_raw[:, 1, :], wmain_d[1]).then_inc(w_in[1], 16)
            eng.dma_start(qpar[:], quant_d.rearrange("a n -> (a n)").partition_broadcast(P)).then_inc(pre_in, 16)
            eng.dma_start(ctxq[:], ctx_d.rearrange("b (k p) d -> p b k d", p=P)).then_inc(ctx_in, 16)
            eng.dma_start(biasb[:], ffnb_d.rearrange("a n -> (a n)").partition_broadcast(P)).then_inc(ffn_in, 16)
            eng.dma_start(gate_raw[:], gate_d).then_inc(ffn_in, 16)
            eng.dma_start(limes[:], limes_d).then_inc(ffn_in, 16)
            eng.dma_start(limesT[:], limest_d).then_inc(ffn_in, 16)
            eng.wait_ge(pre_dve, DVE_CS)
            eng.dma_start(cs_dram, csT).then_inc(cs_out, 16)
            eng.wait_ge(cs_out, 16)

            def slot(eng, s, g, k, first, last):
                r = k % 4
                if not (first and k < 2):
                    if late(s - 3):
                        eng.wait_ge(dve_ylo, s - 3)
                    eng.dma_start(w_raw[:, r, :], wmain_d[s]).then_inc(w_in[r], 16)
                if first and k == 1:
                    eng.wait_ge(pre_pe, PE_TOK)
                if late(s - 3):
                    eng.wait_ge(dve_sub, 8 * s - 24)
                eng.dma_start(csb[:, r].rearrange("p h t -> p (h t)"),
                              cs_dram[ds(2 * s, 2), :].rearrange("h t -> (h t)").partition_broadcast(P)
                              ).then_inc(csb_in[r], 16)
                if k == 1:
                    eng.wait_ge(act_bc, 2 * g + 2)
                    if last:
                        eng.dma_start(bc_raw[:, 0:BC_W], wffn_d[:, 0:2 * D]).then_inc(bc_in, 16)
                    else:
                        eng.dma_start(bc_raw[:], wbc_d[g + 1]).then_inc(bc_in, 16)
                if last and k == 6:
                    eng.wait_ge(low_wbc, GROUPS + 1)
                    eng.dma_start(bc_raw[:, 0:BC_W], wffn_d[:, 2 * D:]).then_inc(bc_in, 16)

            slots(eng, slot)
            eng.wait_ge(pe_ss, GROUPS)
            eng.dma_start(bmat, bmat_d).then_inc(bmat_in, 16)
            for t in range(TT):
                eng.wait_ge(y_done, t + 1)
                eng.dma_start(out_d[t // 2, (t % 2) * P:(t % 2 + 1) * P, :], acc[:, t, :]).then_inc(stored, 16)
            eng.wait_ge(stored, 16 * TT)

        @block.gpsimd
        def _(eng):
            eng.memset(ident[:], 0.0).then_inc(pre_pool, 1)
            eng.memset(causal[:], 1.0).then_inc(pre_pool, 1)
            eng.memset(eps_in[:], EPS).then_inc(pre_pool, 1)
            eng.memset(half_neg[:], -0.5).then_inc(pre_pool, 1)
            eng.memset(ones[:], 1.0).then_inc(pre_pool, 1)
            eng.wait_ge(pre_pool, 5)
            eng.affine_select(out=ident[:], in_=ident[:], compare_op=ALU.not_equal, fill=1.0, base=0,
                              pattern=[[-1, P]], channel_multiplier=1).then_inc(pre_pool, 1)
            eng.affine_select(out=causal[:, 0:P], in_=causal[:, 0:P], compare_op=ALU.is_ge, fill=0.0,
                              base=0, pattern=[[1, P]], channel_multiplier=-1).then_inc(pre_pool, 1)
            eng.affine_select(out=causal[:, S:S + P], in_=causal[:, S:S + P], compare_op=ALU.is_ge, fill=0.0,
                              base=0, pattern=[[1, P]], channel_multiplier=-1).then_inc(pre_pool, 1)
            eng.wait_ge(pre_pool, 8)
            eng.tensor_scalar(identb[:], ident[:], 1.0, 0.0, ALU.mult, ALU.add).then_inc(pre_pool, 1)
            eng.wait_ge(pre_dve, DVE_VAR)
            eng.tensor_tensor(rstd[:], ms[:], half_neg[:], ALU.pow).then_inc(pre_pool, 1)
            eng.wait_ge(pre_dve, DVE_MS)
            eng.tensor_tensor(lnr[:, 0, :], lnv[:, 0, :], half_neg[:], ALU.pow).then_inc(pre_pool, 1)

            def split_in(r4, r2):
                eng.tensor_scalar(win_hi[:, r2, :], w_raw[:, r4, 0:W_IN], 1.0, 0.0, ALU.mult,
                                  ALU.add).then_inc(pool_win, 1)

            def split_out(r4):
                eng.tensor_scalar(wout_hi[:, r4, :], w_raw[:, r4, W_IN:W_ALL], 1.0, 0.0,
                                  ALU.mult, ALU.add).then_inc(pool_wout, 1)

            def lower_in(r4, r2, n):
                eng.wait_ge(pool_win, n)
                eng.tensor_tensor(win_lo[:, r2, :], w_raw[:, r4, 0:W_IN], win_hi[:, r2, :].bitcast(f32),
                                  ALU.subtract).then_inc(low_win, 1)

            def lower_out(r4, n):
                eng.wait_ge(pool_wout, n)
                eng.tensor_tensor(wout_lo[:, r4, :], w_raw[:, r4, W_IN:W_ALL], wout_hi[:, r4, :].bitcast(f32),
                                  ALU.subtract).then_inc(low_wout, 1)

            def lower_bc(n):
                eng.wait_ge(pool_wbc, n)
                eng.tensor_tensor(wbc_lo[:], bc_raw[:, 0:BC_W], wbc_hi[:].bitcast(f32),
                                  ALU.subtract).then_inc(low_wbc, 1)

            eng.wait_ge(bc_in, 16)
            eng.tensor_scalar(wbc_hi[:], bc_raw[:, 0:BC_W], 1.0, 0.0, ALU.mult, ALU.add).then_inc(pool_wbc, 1)
            eng.wait_ge(w_in[0], 16)
            split_in(0, 0)
            split_out(0)
            lower_bc(1)
            lower_in(0, 0, 1)
            lower_out(0, 1)

            eng.wait_ge(pre_act, ACT_TOK)

            def own_sums(s, r2):
                eng.tensor_copy(cs_own[:, r2], cs_tok[:, :, ds(2 * s, 2)]).then_inc(pool_own, 1)

            own_sums(0, 0)

            def slot(eng, s, g, k, first, last):
                r2, r4 = k % 2, k % 4
                n4 = (k + 1) % 4
                if not (last and k == PPG - 1):
                    eng.wait_ge(w_in[n4], 16 * (2 * g + (k + 1) // 4 + 1))
                    if first and 0 < k < 3:
                        eng.wait_ge(pe_gate, s)
                    if late(s - 2):
                        eng.wait_ge(pe_out, s - 2)
                if k == 4:
                    eng.wait_ge(bc_in, 16 * (g + 2))
                    eng.wait_ge(pe_bc, 2 * g + 2)
                if not (last and k == PPG - 1):
                    if late(s):
                        eng.wait_ge(dve_sub, 8 * s)
                    own_sums(s + 1, 1 - r2)
                if not (last and k == PPG - 1):
                    split_in(n4, (k + 1) % 2)
                    split_out(n4)
                    lower_in(n4, (k + 1) % 2, s + 2)
                    lower_out(n4, s + 2)
                if k == 4:
                    eng.tensor_scalar(wbc_hi[:], bc_raw[:, 0:BC_W], 1.0, 0.0, ALU.mult, ALU.add).then_inc(pool_wbc, 1)
                    lower_bc(g + 2)
                sum_squares(s, g, k, first)
                if k == 1 and not first:
                    eng.wait_ge(dve_ms, g)
                    eng.tensor_tensor(rstd[:], ms[:], half_neg[:], ALU.pow).then_inc(pool_rstd, 1)

            def sum_squares(s, g, k, first):
                if k == 1 or (first and k == 0):
                    return
                eng.wait_ge(act_sq, s)
                if k == 2:
                    if late(g):
                        eng.wait_ge(pe_ss, g)
                    eng.tensor_tensor(sqacc[:], sq[:, 0, :], sq[:, 1, :], ALU.add).then_inc(pool_sq, 1)
                else:
                    eng.wait_ge(pool_sq, (PPG - 1) * g + k - 2 if k else (PPG - 1) * (g - 1) + PPG - 2)
                    eng.tensor_tensor(sqacc[:], sqacc[:], sq[:, (k - 1) % 2, :], ALU.add).then_inc(pool_sq, 1)

            slots(eng, slot)
            sum_squares(PAIRS, GROUPS, 0, False)
            eng.wait_ge(bc_in, 16 * (GROUPS + 2))
            eng.tensor_scalar(wffn_hi[:], bc_raw[:, 0:BC_W], 1.0, 0.0, ALU.mult, ALU.add).then_inc(pool_wbc, 1)
            eng.wait_ge(dve_ms, GROUPS)
            eng.tensor_tensor(rstd[:], ms[:], half_neg[:], ALU.pow).then_inc(pool_rstd, 1)
            eng.wait_ge(pool_wbc, GROUPS + 2)
            eng.tensor_tensor(wffn_lo[:], bc_raw[:, 0:BC_W], wffn_hi[:].bitcast(f32), ALU.subtract).then_inc(low_wbc, 1)

            def root(r, t):
                eng.wait_ge(ln_var, TT * r + t + 1)
                eng.tensor_tensor(lnr[:, r, t:t + 1], lnv[:, r, t:t + 1], half_neg[:, 0:1],
                                  ALU.pow).then_inc(ln_root, 1)

            for t in range(TT):
                root(0, t)
            eng.wait_ge(ctxhi_done, 2)
            for k in range(KT):
                eng.tensor_tensor(ctx_lo[1][:, k, :], ctxq[:, 1, k, :], ctx_hi[1][:, k, :].bitcast(f32),
                                  ALU.subtract).then_inc(ctxlo1_done, 1)
                if k == KT // 2:
                    root(1, 0)
            for t in range(TT):
                if t:
                    root(1, t)
                eng.wait_ge(ffn_in, 64)
                eng.wait_ge(ln_out, TT + t + 1)
                eng.tensor_tensor(acc[:, t, :], acc[:, t, :], biasb[:], ALU.add).then_inc(bias_add, 1)
            eng.wait_ge(mix_dve, MIX_ABS)
            eng.partition_all_reduce(ffn_one[:, 1, 0:2], ffn_one[:, 0, 0:2], P,
                                     bass.bass_isa.ReduceOp.max).then_inc(mix_pool, 1)

        @block.scalar
        def _(eng):
            eng.wait_ge(wdt_in, 16)
            eng.activation(wdt_hi, wdt, ACT.Copy).then_inc(pre_act, 1)
            eng.wait_ge(pre_in, 48)
            for k in range(KT):
                eng.wait_ge(pre_pe, k + 1)
                eng.activation(hT_hi[:, k, :], ps_out[:, k, :], ACT.Identity, scale=normw[:, k:k + 1]).then_inc(pre_act, 1)
            eng.wait_ge(pre_dve, DVE_ABS)
            eng.activation(tmpA, tmpA, ACT.Exp, scale=-1.0).then_inc(pre_act, 1)
            eng.activation(negA[:], dtpar[:, 1:2], ACT.Exp).then_inc(pre_act, 1)

            def tap_bc(which, g):
                base = BC_W + which * (TAPS + 1)
                eng.wait_ge(pe_bc, 2 * g + which + 1)
                if late(2 * g + which):
                    eng.wait_ge(act_bc, 2 * g + which)
                eng.activation(conv_bc[:], ps_z[:], ACT.Identity, bias=bc_raw[:, base + TAPS:base + TAPS + 1],
                               scale=bc_raw[:, base + TAPS - 1:base + TAPS]).then_inc(act_tapbc, 1)

            def silu_bc(which, g):
                eng.wait_ge(dve_convbc, 6 * g + 3 * which + 3)
                if late(2 * g):
                    eng.wait_ge(pe_cb, 2 * g)
                eng.activation(bcT[:, which, :], conv_bc[:], ACT.Silu).then_inc(act_bc, 1)

            tap_bc(0, 0)
            eng.wait_ge(pre_dve, DVE_ONEP)
            eng.activation(tmpC, tmpB, ACT.Ln).then_inc(pre_act, 1)
            silu_bc(0, 0)

            def slot(eng, s, g, k, first, last):
                r2, r4, q2 = k % 2, k % 4, (k - 1) % 2
                if k == 0:
                    tap_bc(1, g)
                    if first:
                        eng.wait_ge(pre_pe, PE_TOK - 1)
                        eng.activation(dt_tok[:].rearrange("p t h -> p (t h)"), ps_y[:], ACT.Copy).then_inc(pre_act, 1)
                        eng.wait_ge(pre_pe, PE_TOK)
                        eng.activation(cs_tok[:].rearrange("p t h -> p (t h)"), ps_t[:], ACT.Copy).then_inc(pre_act, 1)
                    silu_bc(1, g)
                if k == PPG - 1 and not last:
                    tap_bc(0, g + 1)
                    silu_bc(0, g + 1)
                eng.wait_ge(pe_hid, s + 1)
                eng.wait_ge(w_in[r4], 16 * (2 * g + k // 4 + 1))
                if late(s):
                    eng.wait_ge(act_hid, s)
                eng.activation(conv[:], ps_h[:], ACT.Identity, bias=w_raw[:, r4, W_ALL + 4:W_ALL + 5],
                               scale=w_raw[:, r4, W_ALL + 3:W_ALL + 4]).then_inc(act_tap, 1)
                eng.wait_ge(dve_sub, 8 * s + 8)
                eng.activation(decay[:, r2].rearrange("p b h m -> p (b h m)"),
                               decay[:, r2].rearrange("p b h m -> p (b h m)"), ACT.Exp).then_inc(act_exp, 1)
                eng.wait_ge(dve_conv, 3 * s + 3)
                if late(s - 1):
                    eng.wait_ge(dve_v, s - 1)
                eng.activation(hidT[:, r2, :], conv[:], ACT.Silu).then_inc(act_hid, 1)
                eng.wait_ge(pe_gate, s + 1)
                if late(s - 1):
                    eng.wait_ge(dve_yg, s - 1)
                eng.activation(gate[:, r2, :], ps_z[:], ACT.Silu).then_inc(act_gate, 1)
                if not (first and k == 0):
                    finish_y(s, g, k, first)

            def finish_y(s, g, k, first):
                q2, q4 = (k - 1) % 2, (k - 1) % 4
                eng.wait_ge(dve_yg, s)
                if late(s - 2):
                    eng.wait_ge(pe_out, s - 2)
                eng.activation(y_hi[:, q2, :], yg[:, q2, :], ACT.Copy,
                               scale=w_raw[:, q4, W_ALL + 6:W_ALL + 7]).then_inc(act_yhi, 1)
                if not (first and k < 3):
                    gs, ks = (g, k - 3) if k >= 3 else (g - 1, k - 3 + PPG)
                    eng.wait_ge(pool_sq, (PPG - 1) * gs + max(ks, 1))
                eng.activation(sq[:, q2, :], yg[:, q2, :], ACT.Square).then_inc(act_sq, 1)

            slots(eng, slot)
            finish_y(PAIRS, GROUPS, 0, False)

            eng.wait_ge(pe_gate, PAIRS)
            eng.wait_ge(dve_ctx, 4 * PPG)
            for b in range(B):
                eng.activation(ctx_hi[b][:].rearrange("p k d -> p (k d)"), ctxq[:, b].rearrange("p k d -> p (k d)"),
                               ACT.Copy).then_inc(ctxhi_done, 1)
            eng.wait_ge(ffn_in, 64)
            eng.activation(gate_hi[:], gate_raw[:], ACT.Copy).then_inc(gate_split, 1)

            def scaled(t):
                eng.wait_ge(ln_out, t + 1)
                eng.wait_ge(dve_sub, 8 * PAIRS)
                eng.activation(qscaled[:, t, :], normed[:, t, :], ACT.Identity, bias=qpar[:, 1:2],
                               scale=qinv[:, 0:1]).then_inc(q_scaled, 1)

            def q_upper(t):
                eng.wait_ge(q_value, t + 1)
                eng.wait_ge(pe_out, PAIRS)
                eng.activation(xT_hi[:, t, :], qvalue[:, t, :], ACT.Copy).then_inc(q_hi, 1)

            for t in range(TT):
                scaled(t)
                if t >= 2:
                    q_upper(t - 2)
            q_upper(TT - 2)
            q_upper(TT - 1)
            eng.wait_ge(bmat_in, 16)
            eng.wait_ge(dve_ylo, PAIRS)
            eng.wait_ge(pe_out, PAIRS)
            eng.activation(bst[0:RANK, :], bmat, ACT.Copy).then_inc(bst_done, 1)
            eng.activation(bst[2 * RANK:3 * RANK, :], bmat, ACT.Copy).then_inc(bst_done, 1)

            def gate_copy(t):
                eng.wait_ge(g_mm, t + 1)
                eng.activation(zh[:, t * P:(t + 1) * P], ps_out[0:GATE, t, 0:P], ACT.Copy).then_inc(g_copy, 1)

            for t in range(TT):
                eng.wait_ge(n_tr, t + 1)
                eng.wait_ge(x_mm, t + 1)
                eng.activation(xT_hi[:, t, :], ps_out[:, t, :], ACT.Copy).then_inc(n_hi, 1)
                if t:
                    gate_copy(t - 1)
            gate_copy(TT - 1)
            eng.wait_ge(mix_dve, MIX_LOGITS)
            eng.activation(ffn_small[:, 3], ffn_small[:, 2], ACT.Exp).then_inc(mix_act, 1)
            eng.wait_ge(mix_dve, MIX_THRESH)
            eng.activation(ffn_small[:, 6], ffn_small[:, 5], ACT.Exp, scale=-2.0).then_inc(mix_act, 1)
            eng.wait_ge(mix_pe, 2)
            eng.activation(wT, ps_y[0:EXPERTS, :], ACT.Copy).then_inc(mix_act, 1)
            eng.wait_ge(mix_dve, MIX_ZP)
            eng.activation(zst[0:RANK, :], zp, ACT.Copy).then_inc(mix_act, 1)
            eng.activation(zst[RANK:2 * RANK, :], zp, ACT.Copy).then_inc(mix_act, 1)

        @block.vector
        def _(eng):
            n_pre = [0]

            def pre(ins):
                n_pre[0] += 1
                ins.then_inc(pre_dve, 1)

            for t in range(TT):
                eng.wait_ge(x_in[t], 16)
                pre(eng.bn_stats(stats[:, t, :], acc[:, t, :]))
            for t in range(TT):
                eng.wait_ge(pre_dve, t + 1)
                pre(eng.bn_aggr(mv[:, t, :], stats[:, t, :]))
            eng.wait_ge(pre_dve, n_pre[0])
            pre(eng.tensor_scalar(ms[:], mv[:, :, 1], EPS, None, ALU.add))
            assert n_pre[0] == DVE_VAR
            eng.wait_ge(pre_act, 1)
            pre(eng.tensor_tensor(wdt_lo, wdt, wdt_hi.bitcast(f32), ALU.subtract))
            eng.wait_ge(pre_pool, 10)
            pre(eng.tensor_tensor(lnv[:, 1, :], rstd[:], rstd[:], ALU.mult))
            eng.wait_ge(pre_dve, n_pre[0])
            pre(eng.tensor_tensor(lnv[:, 0, :], lnv[:, 1, :], mv[:, :, 1], ALU.mult))
            eng.wait_ge(pre_dve, n_pre[0])
            pre(eng.tensor_scalar(lnv[:, 0, :], lnv[:, 0, :], EPS, None, ALU.add))
            assert n_pre[0] == DVE_MS
            for t in range(TT):
                pre(eng.tensor_scalar(normed[:, t, :], acc[:, t, :], mv[:, t, 0:1], rstd[:, t:t + 1],
                                      ALU.subtract, ALU.mult))
            eng.wait_ge(pre_pool, 11)
            for t in range(TT):
                eng.wait_ge(pre_dve, DVE_MS + t + 1)
                pre(eng.tensor_scalar(hnorm[:, t, :], normed[:, t, :], lnr[:, 0, t:t + 1], None, ALU.mult))
            assert n_pre[0] == DVE_H
            for k in range(KT):
                eng.wait_ge(pre_act, 2 + k)
                pre(eng.scalar_tensor_tensor(out=hT_lo[:, k, :], in0=ps_out[:, k, :], scalar=normw[:, k:k + 1],
                                             in1=hT_hi[:, k, :].bitcast(f32), op0=ALU.mult, op1=ALU.subtract))
            assert n_pre[0] == DVE_HT
            pre(eng.tensor_tensor(acc[:], acc[:], normed, ALU.add))
            eng.wait_ge(pre_pe, PE_DT)
            pre(eng.tensor_scalar(dtT, ps_h[:], dtpar[:, 0:1], None, ALU.add))
            assert n_pre[0] == DVE_V
            eng.wait_ge(pre_dve, n_pre[0])
            pre(eng.scalar_tensor_tensor(out=tmpA, in0=dtT, scalar=-1.0, in1=dtT, op0=ALU.mult, op1=ALU.max))
            assert n_pre[0] == DVE_ABS
            pre(eng.memset(onesT, 1.0))
            eng.wait_ge(pre_act, 6)
            pre(eng.tensor_scalar(tmpB, tmpA, 1.0, None, ALU.add))
            assert n_pre[0] == DVE_ONEP
            eng.wait_ge(pre_dve, n_pre[0])
            pre(eng.scalar_tensor_tensor(out=tmpA, in0=tmpB, scalar=-1.0, in1=tmpA, op0=ALU.add, op1=ALU.subtract))

            def convolve(out, acc_in, src, w, done, count):
                src_b = src.rearrange("p (b t) -> p b t", b=B)
                out_b = out.rearrange("p (b t) -> p b t", b=B)
                for n, back in enumerate((1, 2, 3)):
                    if n:
                        eng.wait_ge(done, count + n)
                    eng.scalar_tensor_tensor(out=out_b[:, :, back:], in0=src_b[:, :, 0:S - back],
                                             scalar=w[:, TAPS - 1 - back:TAPS - back], in1=out_b[:, :, back:],
                                             op0=ALU.mult, op1=ALU.add).then_inc(done, 1)

            def conv_group(which, g):
                base = BC_W + which * (TAPS + 1)
                eng.wait_ge(act_tapbc, 2 * g + which + 1)
                convolve(conv_bc[:], None, ps_z[:], bc_raw[:, base:base + TAPS], dve_convbc, 6 * g + 3 * which)

            conv_group(0, 0)
            eng.wait_ge(pre_act, 8)
            eng.wait_ge(pre_dve, n_pre[0])
            pre(eng.tensor_tensor(tmpC, tmpC, tmpA, ALU.subtract))
            eng.wait_ge(pre_dve, n_pre[0])
            pre(eng.scalar_tensor_tensor(out=dtT, in0=dtT, scalar=0.0, in1=tmpC, op0=ALU.max, op1=ALU.add))
            eng.wait_ge(pre_dve, n_pre[0])
            eng.wait_ge(pre_act, 7)
            pre(eng.tensor_scalar(tmpA, dtT, negA[:], -1.0, ALU.mult, ALU.mult))
            eng.wait_ge(pre_dve, n_pre[0])
            for b in range(B):
                pre(eng.tensor_tensor_scan(csT[:, b * S:(b + 1) * S], onesT[:, b * S:(b + 1) * S],
                                           tmpA[:, b * S:(b + 1) * S], 0.0, ALU.mult, ALU.add))
            assert n_pre[0] == DVE_CS

            def slot(eng, s, g, k, first, last):
                r2, r4 = k % 2, k % 4
                if not (first and k == 0):
                    scale_hidden(s, k)
                if k == 2 and not first:
                    add_group(g - 1)
                if k == PPG - 1 and not last:
                    conv_group(0, g + 1)
                if k == 0:
                    conv_group(1, g)
                exponents(s, g, k)
                if k == 0:
                    if late(s):
                        eng.wait_ge(dve_m, s)
                    eng.wait_ge(pe_cb, 2 * g + 1)
                    eng.tensor_tensor(cbm[:, 1, :], ps_z[:, 0:MJ], causal[:], ALU.mult).then_inc(dve_cb, 1)
                    eng.wait_ge(pe_cb, 2 * g + 2)
                    eng.tensor_tensor(cbm[:, 0, :], ps_t[:, 0:MJ], causal[:], ALU.mult).then_inc(dve_cb, 1)
                eng.wait_ge(act_tap, s + 1)
                convolve(conv[:], None, ps_h[:], w_raw[:, r4, W_ALL:W_ALL + TAPS], dve_conv, 3 * s)
                if k == 1 and not first:
                    mean_squares(g - 1)
                if not (first and k == 0):
                    combine(s, k)
                eng.wait_ge(act_exp, s + 1)
                if k == 0:
                    eng.wait_ge(dve_cb, 2 * g + 2)
                eng.tensor_tensor(decay[:, r2], decay[:, r2], cbm[:].unsqueeze(2).broadcast_to([P, B, 2, MJ]),
                                  ALU.mult).then_inc(dve_m, 1)
                if not (first and k == 0):
                    lower_y(s, k)
                if first:
                    quantise_context(k)

            def quantise_context(k):
                x = ctxq[:].rearrange("p b k d -> p (b k d)")[:, k * CHUNK:(k + 1) * CHUNK]
                if k == 0:
                    eng.wait_ge(pre_in, 48)
                    for n in range(2):
                        eng.reciprocal(qinv[:, n:n + 1], qpar[:, 2 * n:2 * n + 1]).then_inc(dve_half, 1)
                    eng.wait_ge(dve_half, 2)
                    eng.wait_ge(ctx_in, 16)
                for n, (a, b, op0, op1) in enumerate((
                        (qinv[:, 1:2], qpar[:, 3:4], ALU.mult, ALU.add), (0.0, 255.0, ALU.max, ALU.min),
                        (ROUND, -ROUND, ALU.add, ALU.add), (qpar[:, 3:4], qpar[:, 2:3], ALU.subtract, ALU.mult))):
                    if n:
                        eng.wait_ge(dve_ctx, 4 * k + n)
                    eng.tensor_scalar(x, x, a, b, op0, op1).then_inc(dve_ctx, 1)

            def exponents(s, g, k):
                r2, r4 = k % 2, k % 4
                eng.wait_ge(csb_in[r4], 16 * (2 * g + k // 4 + 1))
                eng.wait_ge(pool_own, s + 1)
                if late(s - 1):
                    eng.wait_ge(pe_y, s - 1)
                for b in range(B):
                    for h in range(2):
                        for j, (lo, n) in enumerate(((0, S), (S, P))):
                            eng.tensor_scalar(decay[:, r2, b, h, lo:lo + n],
                                              csb[:, r4, h, (b + 1) * S - n:(b + 1) * S],
                                              cs_own[:, r2, 2 * b + j, h:h + 1], 0.0,
                                              ALU.subtract, ALU.min).then_inc(dve_sub, 1)

            def scale_hidden(s, k):
                q2 = (k - 1) % 2
                eng.wait_ge(pe_tr, s)
                if late(s - 2):
                    eng.wait_ge(pe_y, s - 2)
                own = dt_tok[:, :, ds(2 * (s - 1), 2)].unsqueeze(3).broadcast_to([P, TT, 2, HD])
                eng.tensor_tensor(hid_dt[:, q2].rearrange("p t (h c) -> p t h c", h=2),
                                  ps_t[:].rearrange("p (t h c) -> p t h c", t=TT, h=2), own,
                                  ALU.mult).then_inc(dve_hiddt, 1)

            def combine(s, k):
                q2, q4 = (k - 1) % 2, (k - 1) % 4
                eng.wait_ge(pe_y, s)
                eng.wait_ge(act_hid, s)
                if late(s - 1):
                    eng.wait_ge(dve_yg, s - 1)
                eng.scalar_tensor_tensor(out=v[:], in0=hidT[:, q2, :], scalar=w_raw[:, q4, W_ALL + 5:W_ALL + 6],
                                         in1=ps_y[:], op0=ALU.mult, op1=ALU.add).then_inc(dve_v, 1)
                eng.wait_ge(act_gate, s)
                if late(s - 2):
                    eng.wait_ge(dve_ylo, s - 2)
                eng.wait_ge(dve_v, s)
                eng.tensor_tensor(yg[:, q2, :], v[:], gate[:, q2, :], ALU.mult).then_inc(dve_yg, 1)

            def lower_y(s, k):
                q2, q4 = (k - 1) % 2, (k - 1) % 4
                eng.wait_ge(act_yhi, s)
                eng.scalar_tensor_tensor(out=y_lo[:, q2, :], in0=yg[:, q2, :],
                                         scalar=w_raw[:, q4, W_ALL + 6:W_ALL + 7],
                                         in1=y_hi[:, q2, :].bitcast(f32), op0=ALU.mult,
                                         op1=ALU.subtract).then_inc(dve_ylo, 1)

            def mean_squares(g):
                eng.wait_ge(pe_ss, g + 1)
                eng.tensor_scalar(ms[:], ps_t[:, 0:TT], 1.0 / (INNER // GROUPS), EPS_G, ALU.mult,
                                  ALU.add).then_inc(dve_ms, 1)

            def add_group(g):
                eng.wait_ge(pool_rstd, g + 1)
                eng.wait_ge(pe_out, PPG * (g + 1))
                for t in range(TT):
                    add_tile(t)

            def add_tile(t):
                eng.scalar_tensor_tensor(out=acc[:, t, :], in0=ps_out[:, t, :], scalar=rstd[:, t:t + 1],
                                         in1=acc[:, t, :], op0=ALU.mult, op1=ALU.add).then_inc(dve_acc, 1)

            slots(eng, slot)
            scale_hidden(PAIRS, 0)
            combine(PAIRS, 0)
            lower_y(PAIRS, 0)
            mean_squares(GROUPS - 1)
            eng.wait_ge(ctxhi_done, 1)
            eng.tensor_tensor(ctx_lo[0].rearrange("p k d -> p (k d)"), ctxq[:, 0].rearrange("p k d -> p (k d)"),
                              ctx_hi[0][:].rearrange("p k d -> p (k d)").bitcast(f32),
                              ALU.subtract).then_inc(ctxlo_done, 1)
            eng.wait_ge(gate_split, 1)
            eng.tensor_tensor(gate_lo[:], gate_raw[:], gate_hi[:].bitcast(f32), ALU.subtract).then_inc(gate_low, 1)
            eng.tensor_reduce(odd[:], ident[:].rearrange("p (n two) -> p n two", two=2)[:, :, 1], AX.X,
                              ALU.add).then_inc(dve_half, 1)
            eng.wait_ge(pool_rstd, GROUPS)
            eng.wait_ge(pe_out, PAIRS)

            def variance(r, t):
                eng.bn_stats(stats[:, t, :], acc[:, t, :]).then_inc(ln_step, 1)
                eng.wait_ge(ln_step, 2 * (TT * r + t) + 1)
                eng.bn_aggr(mv[:, t, :], stats[:, t, :]).then_inc(ln_step, 1)
                eng.wait_ge(ln_step, 2 * (TT * r + t) + 2)
                eng.tensor_scalar(lnv[:, r, t:t + 1], mv[:, t, 1:2], EPS, None, ALU.add).then_inc(ln_var, 1)

            def norm(r, t):
                eng.wait_ge(ln_root, TT * r + t + 1)
                if r:
                    eng.wait_ge(q_scaled, t + 1)
                eng.tensor_scalar(normed[:, t, :], acc[:, t, :], mv[:, t, 0:1], lnr[:, r, t:t + 1],
                                  ALU.subtract, ALU.mult).then_inc(ln_out, 1)

            def last_group(t):
                add_tile(t)
                eng.wait_ge(dve_acc, TT * (GROUPS - 1) + t + 1)
                variance(0, t)

            def quantise(t):
                eng.wait_ge(q_scaled, t + 1)
                eng.tensor_scalar(qscaled[:, t, :], qscaled[:, t, :], 0.0, 255.0, ALU.max, ALU.min).then_inc(q_step, 1)
                eng.wait_ge(q_step, t + 1)
                eng.tensor_scalar(qround[:, t, :], qscaled[:, t, :], ROUND, -ROUND, ALU.add, ALU.add).then_inc(q_round, 1)

            def values(t):
                eng.wait_ge(q_tr, t + 1)
                eng.tensor_scalar(qvalue[:, t, :], ps_out[:, t, :].bitcast(bf16)[:, 0:D], qpar[:, 1:2], qpar[:, 0:1],
                                  ALU.subtract, ALU.mult).then_inc(q_value, 1)

            def q_lower(t):
                eng.wait_ge(q_hi, t + 1)
                eng.tensor_tensor(xT_lo[:, t, :], qvalue[:, t, :], xT_hi[:, t, :].bitcast(f32),
                                  ALU.subtract).then_inc(q_lo, 1)

            def cross(t):
                eng.wait_ge(x_mm, t + 1)
                eng.tensor_tensor(acc[:, t, :], acc[:, t, :], work[t][:], ALU.add).then_inc(x_add, 1)
                eng.wait_ge(x_add, t + 1)
                variance(1, t)

            def n_lower(t):
                eng.wait_ge(n_hi, t + 1)
                eng.tensor_tensor(xT_lo[:, t, :], ps_out[:, t, :], xT_hi[:, t, :].bitcast(f32),
                                  ALU.subtract).then_inc(n_lo, 1)

            last_group(0)
            last_group(1)
            norm(0, 0)
            last_group(2)
            norm(0, 1)
            quantise(0)
            last_group(3)
            norm(0, 2)
            quantise(1)
            values(0)
            norm(0, 3)
            quantise(2)
            values(1)
            q_lower(0)
            quantise(3)
            values(2)
            q_lower(1)
            cross(0)
            values(3)
            q_lower(2)
            norm(1, 0)
            cross(1)
            q_lower(3)
            norm(1, 1)
            n_lower(0)
            cross(2)
            norm(1, 2)
            n_lower(1)
            cross(3)
            n_lower(2)
            norm(1, 3)
            eng.wait_ge(bst_done, 1)
            eng.tensor_tensor(bst[RANK:2 * RANK, :], bmat, bst[0:RANK, :].bitcast(f32), ALU.subtract).then_inc(bstlo_done, 1)
            n_lower(3)

            n_mix = [0]

            def mix(ins):
                n_mix[0] += 1
                ins.then_inc(mix_dve, 1)

            def settle():
                eng.wait_ge(mix_dve, n_mix[0])

            hs, dl, lg, ex, pr, df, sg, wt, ab = (ffn_small[:, i] for i in range(9))
            wide = [P, TT, EXPERTS]
            eng.wait_ge(mix_pe, 1)
            mix(eng.tensor_tensor(hs, ps_t[:, 0:TT * EXPERTS].rearrange("p (t e) -> p t e", t=TT),
                                  biasb[:, 0:EXPERTS].unsqueeze(1).broadcast_to(wide), ALU.add))
            mix(eng.tensor_copy(dl, ps_t[:, 64:64 + TT * EXPERTS].rearrange("p (t e) -> p t e", t=TT)))
            settle()
            for n, src in enumerate((hs, dl)):
                mix(eng.scalar_tensor_tensor(out=(ab, wt)[n], in0=src, scalar=-1.0, in1=src, op0=ALU.mult, op1=ALU.max))
            settle()
            for n in range(2):
                mix(eng.tensor_reduce(ffn_one[:, 2, n:n + 1], (ab, wt)[n], AX.XY, ALU.max))
            settle()
            eng.wait_ge(dve_half, 3)
            mix(eng.tensor_scalar(ffn_one[:, 0, 0:2], ffn_one[:, 2, 0:2], odd[:], None, ALU.mult))
            assert n_mix[0] == MIX_ABS
            eng.wait_ge(mix_pool, 1)
            mix(eng.tensor_scalar(ffn_one[:, 3, 0:2], ffn_one[:, 1, 0:2], 1e-6, None, ALU.max))
            settle()
            mix(eng.reciprocal(ffn_one[:, 4, 0:2], ffn_one[:, 3, 0:2]))
            settle()
            mix(eng.tensor_scalar(hs, hs, ffn_one[:, 4, 0:1], 0.5, ALU.mult, ALU.mult))
            mix(eng.tensor_scalar(dl, dl, ffn_one[:, 4, 1:2], 0.5, ALU.mult, ALU.mult))
            settle()
            mix(eng.tensor_tensor(hs, hs, dl, ALU.add))
            settle()
            mix(eng.tensor_reduce(ffn_one[:, 5, :], hs, AX.X, ALU.max))
            settle()
            mix(eng.tensor_tensor(lg, hs, ffn_one[:, 5, :].unsqueeze(2).broadcast_to(wide), ALU.subtract))
            assert n_mix[0] == MIX_LOGITS
            eng.wait_ge(mix_act, 1)
            mix(eng.tensor_reduce(ffn_one[:, 6, :], ex, AX.X, ALU.add))
            settle()
            mix(eng.reciprocal(ffn_one[:, 7, :], ffn_one[:, 6, :]))
            settle()
            mix(eng.tensor_tensor(pr, ex, ffn_one[:, 7, :].unsqueeze(2).broadcast_to(wide), ALU.mult))
            settle()
            for t in range(TT):
                mix(eng.max(ab[:, t, :], pr[:, t, :]))
            settle()
            mix(eng.tensor_tensor(df, pr, ab[:, :, 1:2].broadcast_to(wide), ALU.subtract))
            assert n_mix[0] == MIX_THRESH
            eng.wait_ge(mix_act, 2)
            mix(eng.tensor_scalar(sg, sg, 1.0, None, ALU.add))
            settle()
            mix(eng.reciprocal(sg, sg))
            settle()
            mix(eng.tensor_tensor(wt, pr, sg, ALU.mult))
            settle()
            mix(eng.tensor_reduce(ffn_one[:, 5, :], wt, AX.X, ALU.add))
            settle()
            mix(eng.tensor_scalar(ffn_one[:, 5, :], ffn_one[:, 5, :], 1e-9, None, ALU.add))
            settle()
            mix(eng.reciprocal(ffn_one[:, 6, :], ffn_one[:, 5, :]))
            settle()
            mix(eng.tensor_tensor(wt, wt, ffn_one[:, 6, :].unsqueeze(2).broadcast_to(wide), ALU.mult))
            assert n_mix[0] == MIX_WT
            eng.wait_ge(mix_pe, 3)
            mix(eng.scalar_tensor_tensor(out=zp, in0=zh[0:RANK, :], scalar=OUT_SCALE, in1=ps_out[0:RANK, 0, :],
                                         op0=ALU.mult, op1=ALU.mult))
            assert n_mix[0] == MIX_ZP
            eng.wait_ge(mix_act, 4)
            mix(eng.tensor_tensor(zst[2 * RANK:3 * RANK, :], zp, zst[0:RANK, :].bitcast(f32), ALU.subtract))
            for t in range(TT):
                eng.wait_ge(d_mm, t + 1)
                eng.wait_ge(bias_add, t + 1)
                eng.tensor_tensor(acc[:, t, :], acc[:, t, :], work[t][:], ALU.add).then_inc(y_done, 1)

        @block.tensor
        def _(eng):
            mm = nc.tensor.matmul

            def tr(out, src, n=P):
                return nc.tensor.transpose(out, src, ident[:n, :n])

            eng.wait_ge(pre_pool, 8)
            eng.wait_ge(pre_dve, DVE_H)
            for k in range(KT):
                for t in range(TT):
                    last = tr(ps_out[:, k, t * P:(t + 1) * P], hnorm[:, t, k * P:(k + 1) * P])
                last.then_inc(pre_pe, 1)
            eng.wait_ge(pre_dve, DVE_HT)
            def project(out, w_hi, w_lo, done):
                n = 0
                for w, h in ((w_hi, hT_hi), (w_hi, hT_lo), (w_lo, hT_hi)):
                    for k in range(KT):
                        last = mm(out, w[:, k * P:(k + 1) * P], h[:, k, :], start=n == 0, stop=n == 3 * KT - 1)
                        n += 1
                last.then_inc(done, 1)

            project(ps_h[:], wdt_hi, wdt_lo, pre_pe)
            eng.wait_ge(low_wbc, 1)
            project(ps_z[:], wbc_hi[:, 0:KT * P], wbc_lo[:, 0:KT * P], pe_bc)

            def start_up():
                eng.wait_ge(dve_convbc, 3)
                project(ps_z[:], wbc_hi[:, KT * P:], wbc_lo[:, KT * P:], pe_bc)
                eng.wait_ge(pre_dve, DVE_CS)
                for src, out in ((dtT, ps_y), (csT, ps_t)):
                    for t in range(TT):
                        last = tr(out[:, t * P:(t + 1) * P], src[:, t * P:(t + 1) * P])
                    last.then_inc(pre_pe, 1)
                eng.wait_ge(pre_act, ACT_TOK)

            def slot(eng, s, g, k, first, last):
                r2 = k % 2
                eng.wait_ge(low_win, s + 1)
                if late(3 * s):
                    eng.wait_ge(dve_conv, 3 * s)
                if first and k == 0:
                    eng.wait_ge(pre_dve, DVE_V)
                project(ps_h[:], win_hi[:, r2, 0:KT * P], win_lo[:, r2, 0:KT * P], pe_hid)
                if first and k == 0:
                    start_up()
                if not (first and k == 0):
                    scan_heads(s, k)
                if k == 0:
                    eng.wait_ge(act_bc, 2 * g + 2)
                    if late(s):
                        eng.wait_ge(act_gate, s)
                    for b, bank in ((1, ps_z), (0, ps_t)):
                        q = b * S
                        mm(bank[:, 0:S], bcT[:, 0, q:q + P], bcT[:, 1, q:q + S], start=True, stop=True)
                        mm(bank[:, S:MJ], bcT[:, 0, q + P:q + S], bcT[:, 1, q + P:q + S], start=True,
                           stop=True).then_inc(pe_cb, 1)
                if k == 1 and not first:
                    sum_channels(g - 1)
                if late(s):
                    eng.wait_ge(act_gate, s)
                if k == 0:
                    eng.wait_ge(dve_cb, 2 * g + 1)
                if k == PPG - 1 and not last:
                    eng.wait_ge(dve_convbc, 6 * (g + 1) + 3)
                project(ps_z[:], win_hi[:, r2, KT * P:], win_lo[:, r2, KT * P:], pe_gate)
                if not (first and k < 2):
                    project_out(s, g, k)
                eng.wait_ge(act_hid, s + 1)
                if k == 0:
                    eng.wait_ge(dve_cb, 2 * g + 2)
                if k == 1 and not first:
                    eng.wait_ge(dve_ms, g)
                for t in range(TT):
                    done = tr(ps_t[:, t * P:(t + 1) * P], hidT[:, r2, t * P:(t + 1) * P])
                done.then_inc(pe_tr, 1)
                if k >= PPG - 2 and not last:
                    which = k - (PPG - 2)
                    eng.wait_ge(low_wbc, g + 2)
                    eng.wait_ge(act_gate, s + 1)
                    project(ps_z[:], wbc_hi[:, which * KT * P:(which + 1) * KT * P],
                            wbc_lo[:, which * KT * P:(which + 1) * KT * P], pe_bc)

            def scan_heads(s, k):
                q2 = (k - 1) % 2
                eng.wait_ge(dve_hiddt, s)
                eng.wait_ge(dve_m, s)
                if late(s - 1):
                    eng.wait_ge(dve_v, s - 1)
                for h in range(2):
                    for b in range(B):
                        out = ps_y[h * HD:(h + 1) * HD, b * S:(b + 1) * S]
                        mm(out, hid_dt[:, q2, 2 * b, h * HD:(h + 1) * HD], decay[:, q2, b, h, 0:S],
                           start=True, stop=False)
                        done = mm(out[:, P:S], hid_dt[:, q2, 2 * b + 1, h * HD:(h + 1) * HD],
                                  decay[:, q2, b, h, S:MJ], start=False, stop=True)
                done.then_inc(pe_y, 1)

            def project_out(s, g, k):
                pair, q2, q4 = (k - 2) % PPG, (k - 2) % 2, (k - 2) % 4
                eng.wait_ge(dve_ylo, s - 1)
                for t in range(TT):
                    if k == 2 and late(TT * g):
                        eng.wait_ge(dve_acc, TT * (g - 1) + t + 1)
                    for n, (y, w) in enumerate(((y_hi, wout_hi), (y_hi, wout_lo), (y_lo, wout_hi))):
                        done = mm(ps_out[:, t, :], y[:, q2, t * P:(t + 1) * P], w[:, q4, :],
                                  start=pair == 0 and n == 0, stop=pair == PPG - 1 and n == 2)
                done.then_inc(pe_out, 1)

            def sum_channels(g):
                eng.wait_ge(pool_sq, (PPG - 1) * (g + 1))
                for t in range(TT):
                    done = mm(ps_t[:, t:t + 1], sqacc[:, t * P:(t + 1) * P], ones[:, 0:1], start=True, stop=True)
                done.then_inc(pe_ss, 1)

            slots(eng, slot)
            scan_heads(PAIRS, 0)
            project_out(PAIRS, GROUPS, 0)
            sum_channels(GROUPS - 1)
            project_out(PAIRS + 1, GROUPS, 1)

            def products(out, w, lower, upper, t, cols=P):
                n = 0
                for x, part in ((xT_hi, upper), (xT_hi, lower), (xT_lo, upper)):
                    for k in range(KT):
                        done = mm(out, x[:, t, k * P:(k + 1) * P], part(k), start=n == 0, stop=n == 3 * KT - 1)
                        n += 1
                return done

            def turn_rounded(t):
                eng.wait_ge(q_round, t + 1)
                eng.wait_ge(dve_acc, TT * (GROUPS - 1) + t + 1)
                bank = ps_out[:, t, :].bitcast(bf16)
                for k in range(KT):
                    done = nc.tensor.transpose(bank[:, k * P:(k + 1) * P], qround[:, t, k * P:(k + 1) * P], identb[:])
                done.then_inc(q_tr, 1)

            def cross(t):
                b = t // 2
                eng.wait_ge(q_lo, t + 1)
                if b:
                    eng.wait_ge(ctxlo1_done, KT)
                else:
                    eng.wait_ge(ctxlo_done, 1)
                eng.wait_ge(dve_ms, GROUPS)
                products(work[t][:], None, lambda k: ctx_lo[b][:, k, :], lambda k: ctx_hi[b][:, k, :],
                         t).then_inc(x_mm, 1)

            def turn_normed(t):
                eng.wait_ge(ln_out, TT + t + 1)
                eng.wait_ge(q_value, t + 1)
                for k in range(KT):
                    done = tr(ps_out[:, t, k * P:(k + 1) * P], normed[:, t, k * P:(k + 1) * P])
                done.then_inc(n_tr, 1)

            def gate_columns(t):
                eng.wait_ge(n_lo, t + 1)
                eng.wait_ge(gate_low, 1)
                n = 0
                for w, x in ((gate_hi, xT_hi), (gate_hi, xT_lo), (gate_lo, xT_hi)):
                    for k in range(KT):
                        done = mm(ps_out[0:GATE, t, 0:P], w[:, k, :], x[:, t, k * P:(k + 1) * P], start=n == 0,
                                  stop=n == 3 * KT - 1)
                        n += 1
                done.then_inc(g_mm, 1)

            def ffn(t):
                eng.wait_ge(x_add, t + 1)
                eng.wait_ge(low_wbc, GROUPS + 2)
                if t == TT - 1:
                    eng.wait_ge(mix_dve, 2)
                products(work[t][:], None, lambda k: wffn(k, True), lambda k: wffn(k, False), t).then_inc(h_mm, 1)

            for t in range(TT):
                turn_rounded(t)
                if t >= 2:
                    cross(t - 2)
            cross(TT - 2)
            turn_normed(0)
            cross(TT - 1)
            turn_normed(1)
            gate_columns(0)
            ffn(0)
            turn_normed(2)
            gate_columns(1)
            turn_normed(3)
            gate_columns(2)
            ffn(1)
            gate_columns(3)
            eng.wait_ge(g_copy, TT)
            eng.wait_ge(x_add, TT)
            for t in range(TT):
                tr_out = ps_t[:, t * EXPERTS:(t + 1) * EXPERTS]
                done = nc.tensor.transpose(tr_out, zh[RANK:GATE, t * P:(t + 1) * P], ident[RANK:GATE, RANK:GATE])
            done.then_inc(h_turned, 1)
            eng.wait_ge(h_turned, 1)
            for t in range(TT):
                done = mm(ps_t[:, 64 + t * EXPERTS:64 + (t + 1) * EXPERTS], zh[0:RANK, t * P:(t + 1) * P], limesT[:],
                          start=True, stop=True)
            done.then_inc(mix_pe, 1)
            ffn(3)
            eng.wait_ge(mix_dve, MIX_WT)
            for t in range(TT):
                done = tr(ps_y[0:EXPERTS, t * P:(t + 1) * P], ffn_small[:, 7, t, :])
            done.then_inc(mix_pe, 1)
            eng.wait_ge(mix_act, 3)
            anchors = wT.rearrange("e (a two) -> e a two", two=2)[:, :, 1:2].broadcast_to([EXPERTS, T // 2, 2])
            mm(ps_out[0:RANK, 0, :], limes[:], anchors, start=True, stop=True).then_inc(mix_pe, 1)
            ffn(2)
            eng.wait_ge(mix_dve, MIX_ZP + 1)
            eng.wait_ge(mix_act, 5)
            eng.wait_ge(bstlo_done, 1)
            eng.wait_ge(bst_done, 2)
            for t in range(TT):
                mm(work[t][:], zst[:, t * P:(t + 1) * P], bst, start=False, stop=True,
                   skip_group_check=True).then_inc(d_mm, 1)


DVE_VAR = 2 * TT + 1
DVE_MS = DVE_VAR + 4
DVE_H = DVE_MS + 2 * TT
DVE_HT = DVE_H + KT
DVE_V = DVE_HT + 2
DVE_ABS = DVE_V + 1
DVE_ONEP = DVE_ABS + 2
DVE_CS = DVE_ONEP + 4 + B
PE_DT = KT + 1
PE_TOK = PE_DT + 2
ACT_TOK = KT + 6
MIX_ABS = 7
MIX_LOGITS = MIX_ABS + 7
MIX_THRESH = MIX_LOGITS + 3 + TT + 1
MIX_WT = MIX_THRESH + 7
MIX_ZP = MIX_WT + 1


def lay_out(i):
    import numpy as np

    a = {k: np.asarray(x) for k, x in i.items()}

    def by_width(w):
        return w.T.reshape(KT, P, -1).transpose(1, 0, 2)

    win, conv_w, conv_b = a["L0_attn_in_proj_w"], a["L0_attn_conv_w"], a["L0_attn_conv_b"]
    gates, hidden = win[:INNER], win[INNER:2 * INNER]
    gn = GROUPS * P
    rows_b, rows_c = win[2 * INNER:2 * INNER + gn], win[2 * INNER + gn:2 * INNER + 2 * gn]
    rows_dt = win[2 * INNER + 2 * gn:]
    wout = a["L0_attn_out_proj_w"].T
    d_ch = np.repeat(a["L0_attn_Dp"], HD)
    gnorm = a["L0_attn_gnorm_w"]
    wmain = np.zeros((PAIRS, P, W_ROW), np.float32)
    for s in range(PAIRS):
        c = slice(s * P, (s + 1) * P)
        wmain[s, :, 0:KT * P] = by_width(hidden[c]).reshape(P, -1)
        wmain[s, :, KT * P:W_IN] = by_width(gates[c]).reshape(P, -1)
        wmain[s, :, W_IN:W_ALL] = wout[c]
        wmain[s, :, W_ALL:W_ALL + TAPS] = conv_w[c]
        wmain[s, :, W_ALL + 4] = conv_b[c]
        wmain[s, :, W_ALL + 5] = d_ch[c]
        wmain[s, :, W_ALL + 6] = gnorm[c]
    wbc = np.zeros((GROUPS, P, BC_ROW), np.float32)
    for g in range(GROUPS):
        c = slice(g * P, (g + 1) * P)
        for n, rows in enumerate((rows_b, rows_c)):
            at = BC_W + n * (TAPS + 1)
            cc = slice(INNER + n * gn + g * P, INNER + n * gn + (g + 1) * P)
            wbc[g, :, n * KT * P:(n + 1) * KT * P] = by_width(rows[c]).reshape(P, -1)
            wbc[g, :, at:at + TAPS] = conv_w[cc]
            wbc[g, :, at + TAPS] = conv_b[cc]
    return {
        "x": a["x"], "ctx": a["ctx_4096"],
        "wdt": by_width(rows_dt).reshape(P, -1),
        "dtpar": np.stack([a["L0_attn_dt_bias"], a["L0_attn_A_log"]], 1),
        "normw": a["L0_attn_norm_w"].reshape(KT, P).T,
        "wmain": wmain, "wbc": wbc,
        "quant": np.stack([a["L0_xattn_x1_scale"], a["L0_xattn_x1_zp"], a["L0_xattn_x2_scale"],
                           a["L0_xattn_x2_zp"]], 0),
        "wffn": by_width(a["L0_ffn_W"]).reshape(P, -1), "ffnb": a["L0_ffn_b"].reshape(1, D),
        "gate": np.concatenate([a["L0_ffn_A"], a["L0_ffn_W"][:EXPERTS].T], 1).reshape(KT, P, GATE).transpose(1, 0, 2),
        "bmat": a["L0_ffn_Bmat"], "limes": a["L0_ffn_LiMEs"], "limest": a["L0_ffn_LiMEs"].T,
    }


def kernel(**inputs):
    import numpy as np
    import concourse.bacc as bacc
    from concourse import mybir as mb
    from concourse.bass_utils import run_bass_kernel_spmd

    nc = bacc.Bacc("TRN2", target_bir_lowering=False, num_devices=1)
    arrays, args = {}, []
    for name, a in lay_out(inputs).items():
        a = np.ascontiguousarray(a)
        arrays[f"in_{name}"] = a
        args.append(nc.dram_tensor(f"in_{name}", a.shape, mb.dt.from_np(a.dtype), kind="ExternalInput").ap())
    args.append(nc.dram_tensor("out_x", (B, S, D), mb.dt.float32, kind="ExternalOutput").ap())
    build(nc, *args)
    r = run_bass_kernel_spmd(nc, [arrays], core_ids=[0])
    return r.results[0]["out_x"]
```

```python
import concourse.bass as bass
from concourse import mybir
from contextlib import ExitStack

D = 512
B, S = 2, 256
T = B * S
P = 128
TT = T // P
KT = D // P
HEADS, HD, GROUPS = 128, 64, 8
INNER = HEADS * HD
PAIRS = INNER // P
PPG = PAIRS // GROUPS
TAPS = 4
W_IN = 2 * KT * P
W_ALL = W_IN + D
N_PAR = 8
W_ROW = W_ALL + N_PAR
BC_W = 2 * KT * P
BC_ROW = BC_W + 2 * (TAPS + 1)
CTX = 512
EXPERTS, RANK = 8, 32
GATE = RANK + EXPERTS
MJ = S + P
EPS, EPS_RMS, EPS_G = 1e-5, 1e-5, 1e-5
CENTRE = 128.0
ROUND = 1.5 * 2.0 ** 23
OUT_SCALE = 16.0 / RANK


WARM_UP = 40


def late(count):
    return not isinstance(count, int) or count > 0


def build(nc, x_d, ctx_d, wdt_d, dtpar_d, normw_d, wmain_d, wbc_d, quant_d, wffn_d, ffnb_d,
          gate_d, bmat_d, limes_d, limest_d, out_d):
    f32, f32r, bf16 = mybir.dt.float32, mybir.dt.float32r, mybir.dt.bfloat16
    ALU, ACT, AX = mybir.AluOpType, mybir.ActivationFunctionType, mybir.AxisListType
    ds = bass.ds

    with ExitStack() as ctx:
        def sb(name, shape, dt=f32):
            return ctx.enter_context(nc.sbuf_tensor(name, shape, dt))

        def sem(name):
            return ctx.enter_context(nc.semaphore(name))

        cs_dram = nc.dram_tensor("cs_rows", [HEADS, T], f32).ap()

        acc = sb("acc", [P, TT, D])
        hT_hi = sb("hT_hi", [P, KT, T], f32r)
        hT_lo = sb("hT_lo", [P, KT, T], f32r)
        dt_tok = sb("dt_tok", [P, TT, HEADS])
        cs_tok = sb("cs_tok", [P, TT, HEADS])
        w_raw = sb("w_raw", [P, 4, W_ROW])
        win_hi = sb("win_hi", [P, 2, W_IN], f32r)
        win_lo = sb("win_lo", [P, 2, W_IN], f32r)
        wout_hi = sb("wout_hi", [P, 4, D], f32r)
        wout_lo = sb("wout_lo", [P, 4, D], f32r)
        bc_raw = sb("bc_raw", [P, BC_ROW])
        wbc_hi = sb("wbc_hi", [P, BC_W], f32r)
        wbc_lo = sb("wbc_lo", [P, BC_W], f32r)
        csb = sb("csb", [P, 4, 2, T])
        decay = sb("decay", [P, 2, B, 2, MJ])
        cs_own = sb("cs_own", [P, 2, TT, 2])
        cbm = sb("cbm", [P, B, MJ])
        conv = sb("conv", [P, T])
        conv_bc = sb("conv_bc", [P, T])
        hidT = sb("hidT", [P, 2, T])
        gate = sb("gate", [P, 2, T])
        bcT = sb("bcT", [P, 2, T])
        hid_dt = sb("hid_dt", [P, 2, TT, P])
        v = sb("v", [P, T])
        yg = sb("yg", [P, 2, T])
        y_hi = sb("y_hi", [P, 2, T], f32r)
        y_lo = sb("y_lo", [P, 2, T], f32r)
        sq = sb("sq", [P, 2, T])
        sqacc = sb("sqacc", [P, T])
        ms = sb("ms", [P, TT])
        rstd = sb("rstd", [P, TT])
        ident = sb("ident", [P, P])
        causal = sb("causal", [P, MJ])
        ones = sb("ones", [P, 1])
        onesb = sb("onesb", [P, P], bf16)
        half_neg = sb("half_neg", [P, TT])
        dtpar = sb("dtpar", [P, 2])
        negA = sb("negA", [P, 1])
        normw = sb("normw", [P, KT])
        stats = sb("stats", [P, TT, 6])
        mv = sb("mv", [P, TT, 2])
        qpar = sb("qpar", [P, 4])
        qinv = sb("qinv", [P, 2])
        qcon = sb("qcon", [P, 4])
        rowsum = sb("rowsum", [P, TT])
        ctx_raw = sb("ctx_raw", [P, B * CTX // P, D])
        ctx_first = sb("ctx_first", [P, D], bf16)
        wffn_hi = sb("wffn_hi", [P, 2 * D], f32r)
        wffn_lo = sb("wffn_lo", [P, 2 * D], f32r)
        gate_raw = sb("gate_raw", [P, KT, GATE])
        gate_hi = sb("gate_hi", [P, KT, GATE], f32r)
        gate_lo = sb("gate_lo", [P, KT, GATE], f32r)
        lnv = sb("lnv", [P, 2, TT])
        lnr = sb("lnr", [P, 2, TT])
        biasb = sb("biasb", [P, D])
        odd = sb("odd", [P, 1])
        limes = sb("limes", [EXPERTS, RANK])
        limesT = sb("limesT", [RANK, EXPERTS])
        ffn_small = sb("ffn_small", [P, 9, TT, EXPERTS])
        ffn_one = sb("ffn_one", [P, 8, TT])

        normed = decay[:].rearrange("p r b h m -> p (r b h m)")[:, 0:TT * D].rearrange("p (t d) -> p t d", t=TT)
        hnorm = w_raw[:, 2:4].rearrange("p r w -> p (r w)")[:, 0:TT * D].rearrange("p (t d) -> p t d", t=TT)
        wdt = csb[:, 0].rearrange("p h t -> p (h t)")[:, 0:KT * P]
        residual = (yg[:, 0, :], yg[:, 1, :], sq[:, 0, :], sq[:, 1, :])
        wdt_hi, wdt_lo = y_hi[:, 0, :], y_lo[:, 0, :]
        dtT, csT = csb[:, 1, 0, :], csb[:, 1, 1, :]
        tmpA, tmpB, tmpC, onesT = csb[:, 2, 0, :], csb[:, 2, 1, :], csb[:, 3, 0, :], csb[:, 3, 1, :]
        qscaled = csb[:].rearrange("p r h t -> p (r h t)")[:, 0:TT * D].rearrange("p (t d) -> p t d", t=TT)
        ctxsum = csb[:].rearrange("p r h t -> p (r h t)")[:, TT * D:(TT + B) * D].rearrange("p (b d) -> p b d", b=B)
        qT = hidT[:].rearrange("p r t -> p (r t)").bitcast(bf16).rearrange("p (t d) -> p t d", t=TT)
        qround = gate[:].rearrange("p r t -> p (r t)").bitcast(bf16).rearrange("p (t d) -> p t d", t=TT)
        identb = sb("identb", [P, P], bf16)
        xT_hi, xT_lo = wout_hi, wout_lo
        zh = v[0:GATE, :]
        zp = conv[0:RANK, :]
        wT = conv_bc[0:EXPERTS, :]
        bmat = sqacc[0:RANK, :]
        zst = y_hi[0:3 * RANK, 0, :]
        bst = y_lo[0:3 * RANK, 0, :]

        def ctxq(n):
            return ctx_raw[:, n - 1, :].bitcast(bf16)[:, 0:D] if n else ctx_first[:]

        def wffn(k, lower):
            if k < 2:
                return (wbc_lo if lower else wbc_hi)[:, k * D:(k + 1) * D]
            return (wffn_lo if lower else wffn_hi)[:, (k - 2) * D:(k - 1) * D]

        ps_out = ctx.enter_context(nc.psum_tensor("ps_out", [P, TT, D], f32))
        ps_h = ctx.enter_context(nc.psum_tensor("ps_h", [P, T], f32))
        ps_z = ctx.enter_context(nc.psum_tensor("ps_z", [P, T], f32))
        ps_y = ctx.enter_context(nc.psum_tensor("ps_y", [P, T], f32))
        ps_t = ctx.enter_context(nc.psum_tensor("ps_t", [P, T], f32))
        work = (ps_h, ps_z, ps_y, ps_t)

        x_in = [sem(f"x_in{t}") for t in range(TT)]
        wdt_in, pre_in, qpar_in, ctx_in = sem("wdt_in"), sem("pre_in"), sem("qpar_in"), sem("ctx_in")
        cs_out = sem("cs_out")
        w_in = [sem(f"w_in{i}") for i in range(4)]
        csb_in = [sem(f"csb_in{i}") for i in range(4)]
        bc_in, ffn_in, bmat_in, stored = sem("bc_in"), sem("ffn_in"), sem("bmat_in"), sem("stored")
        pre_dve, pre_act, pre_pool, pre_pe = sem("pre_dve"), sem("pre_act"), sem("pre_pool"), sem("pre_pe")
        pe_hid, pe_gate, pe_bc, pe_cb = sem("pe_hid"), sem("pe_gate"), sem("pe_bc"), sem("pe_cb")
        pe_tr, pe_y, pe_out, pe_ss = sem("pe_tr"), sem("pe_y"), sem("pe_out"), sem("pe_ss")
        act_tap, act_hid, act_gate = sem("act_tap"), sem("act_hid"), sem("act_gate")
        act_tapbc, act_bc, act_exp = sem("act_tapbc"), sem("act_bc"), sem("act_exp")
        act_yhi, act_sq = sem("act_yhi"), sem("act_sq")
        dve_conv, dve_convbc, dve_hiddt = sem("dve_conv"), sem("dve_convbc"), sem("dve_hiddt")
        low_win, low_wout, low_wbc, dve_cb = sem("low_win"), sem("low_wout"), sem("low_wbc"), sem("dve_cb")
        dve_m, dve_v, dve_yg, dve_ylo = sem("dve_m"), sem("dve_v"), sem("dve_yg"), sem("dve_ylo")
        dve_ms, dve_acc, dve_sub = sem("dve_ms"), sem("dve_acc"), sem("dve_sub")
        pool_win, pool_wout, pool_wbc = sem("pool_win"), sem("pool_wout"), sem("pool_wbc")
        pool_own, pool_sq, pool_rstd = sem("pool_own"), sem("pool_sq"), sem("pool_rstd")
        act_ctx, dve_ctx, dve_half = sem("act_ctx"), sem("dve_ctx"), sem("dve_half")
        c_mm, c_sum, r_sum, r_add = sem("c_mm"), sem("c_sum"), sem("r_sum"), sem("r_add")
        bst_done, bstlo_done, gate_split, gate_low = sem("bst_done"), sem("bstlo_done"), sem("gate_split"), sem("gate_low")
        ln_step, ln_var, ln_root, ln_out = sem("ln_step"), sem("ln_var"), sem("ln_root"), sem("ln_out")
        q_scaled, q_step, q_round = sem("q_scaled"), sem("q_step"), sem("q_round")
        q_tr, q_copy, x_shift = sem("q_tr"), sem("q_copy"), sem("x_shift")
        x_mm, x_add, n_tr, n_hi, n_lo = sem("x_mm"), sem("x_add"), sem("n_tr"), sem("n_hi"), sem("n_lo")
        g_mm, g_copy, bias_add = sem("g_mm"), sem("g_copy"), sem("bias_add")
        mix_dve, mix_act, mix_pool, mix_pe = sem("mix_dve"), sem("mix_act"), sem("mix_pool"), sem("mix_pe")
        d_mm, y_done, h_turned = sem("d_mm"), sem("y_done"), sem("h_turned")

        def slots(eng, slot):
            for k in range(PPG):
                slot(eng, k, 0, k, True, False)
            with eng.Fori(1, GROUPS - 1) as g:
                for k in range(PPG):
                    slot(eng, PPG * g + k, g, k, False, False)
            for k in range(PPG):
                slot(eng, PPG * (GROUPS - 1) + k, GROUPS - 1, k, False, True)

        block = ctx.enter_context(nc.Block())

        @block.sync
        def _(eng):
            for t in range(TT):
                eng.dma_start(acc[:, t, :], x_d[t // 2, (t % 2) * P:(t % 2 + 1) * P, :]).then_inc(x_in[t], 16)
            eng.dma_start(wdt, wdt_d).then_inc(wdt_in, 16)
            eng.dma_start(normw[:], normw_d).then_inc(pre_in, 16)
            eng.dma_start(dtpar[:], dtpar_d).then_inc(pre_in, 16)
            eng.dma_start(bc_raw[:], wbc_d[0]).then_inc(bc_in, 16)
            eng.dma_start(w_raw[:, 0, :], wmain_d[0]).then_inc(w_in[0], 16)
            eng.dma_start(w_raw[:, 1, :], wmain_d[1]).then_inc(w_in[1], 16)
            eng.dma_start(qpar[:], quant_d.rearrange("a n -> (a n)").partition_broadcast(P)).then_inc(qpar_in, 16)
            eng.dma_start(ctx_raw[:], ctx_d.rearrange("b (k p) d -> p (b k) d", p=P)).then_inc(ctx_in, 16)
            eng.dma_start(biasb[:], ffnb_d.rearrange("a n -> (a n)").partition_broadcast(P)).then_inc(ffn_in, 16)
            eng.dma_start(gate_raw[:], gate_d).then_inc(ffn_in, 16)
            eng.dma_start(limes[:], limes_d).then_inc(ffn_in, 16)
            eng.dma_start(limesT[:], limest_d).then_inc(ffn_in, 16)
            eng.wait_ge(pre_dve, DVE_CS)
            eng.dma_start(cs_dram, csT).then_inc(cs_out, 16)
            eng.wait_ge(cs_out, 16)

            def slot(eng, s, g, k, first, last):
                r = k % 4
                if not (first and k < 2):
                    if late(s - 3):
                        eng.wait_ge(dve_ylo, s - 3)
                    eng.dma_start(w_raw[:, r, :], wmain_d[s]).then_inc(w_in[r], 16)
                if first and k == 1:
                    eng.wait_ge(pre_pe, PE_TOK)
                if late(s - 3):
                    eng.wait_ge(dve_sub, 8 * s - 24)
                eng.dma_start(csb[:, r].rearrange("p h t -> p (h t)"),
                              cs_dram[ds(2 * s, 2), :].rearrange("h t -> (h t)").partition_broadcast(P)
                              ).then_inc(csb_in[r], 16)
                if k == 1:
                    eng.wait_ge(act_bc, 2 * g + 2)
                    if last:
                        eng.dma_start(bc_raw[:, 0:BC_W], wffn_d[:, 0:2 * D]).then_inc(bc_in, 16)
                    else:
                        eng.dma_start(bc_raw[:], wbc_d[g + 1]).then_inc(bc_in, 16)
                if last and k == 6:
                    eng.wait_ge(low_wbc, GROUPS + 1)
                    eng.dma_start(bc_raw[:, 0:BC_W], wffn_d[:, 2 * D:]).then_inc(bc_in, 16)

            slots(eng, slot)
            eng.wait_ge(pe_ss, GROUPS)
            eng.dma_start(bmat, bmat_d).then_inc(bmat_in, 16)
            for t in range(TT):
                eng.wait_ge(y_done, t + 1)
                eng.dma_start(out_d[t // 2, (t % 2) * P:(t % 2 + 1) * P, :], acc[:, t, :]).then_inc(stored, 16)
            eng.wait_ge(stored, 16 * TT)

        @block.gpsimd
        def _(eng):
            eng.memset(ident[:], 0.0).then_inc(pre_pool, 1)
            eng.memset(causal[:], 1.0).then_inc(pre_pool, 1)
            eng.memset(onesb[:], 1.0).then_inc(pre_pool, 1)
            eng.memset(half_neg[:], -0.5).then_inc(pre_pool, 1)
            eng.memset(ones[:], 1.0).then_inc(pre_pool, 1)
            eng.wait_ge(pre_pool, 5)
            eng.affine_select(out=ident[:], in_=ident[:], compare_op=ALU.not_equal, fill=1.0, base=0,
                              pattern=[[-1, P]], channel_multiplier=1).then_inc(pre_pool, 1)
            eng.affine_select(out=causal[:, 0:P], in_=causal[:, 0:P], compare_op=ALU.is_ge, fill=0.0,
                              base=0, pattern=[[1, P]], channel_multiplier=-1).then_inc(pre_pool, 1)
            eng.affine_select(out=causal[:, S:S + P], in_=causal[:, S:S + P], compare_op=ALU.is_ge, fill=0.0,
                              base=0, pattern=[[1, P]], channel_multiplier=-1).then_inc(pre_pool, 1)
            eng.wait_ge(pre_pool, 8)
            eng.tensor_scalar(identb[:], ident[:], 1.0, 0.0, ALU.mult, ALU.add).then_inc(pre_pool, 1)
            eng.wait_ge(pre_dve, DVE_VAR)
            eng.tensor_tensor(lnr[:, 0, :], lnv[:, 0, :], half_neg[:], ALU.pow).then_inc(pre_pool, 1)
            eng.tensor_tensor(rstd[:], ms[:], half_neg[:], ALU.pow).then_inc(pre_pool, 1)

            def split_in(r4, r2):
                eng.tensor_scalar(win_hi[:, r2, :], w_raw[:, r4, 0:W_IN], 1.0, 0.0, ALU.mult,
                                  ALU.add).then_inc(pool_win, 1)

            def split_out(r4):
                eng.tensor_scalar(wout_hi[:, r4, :], w_raw[:, r4, W_IN:W_ALL], 1.0, 0.0,
                                  ALU.mult, ALU.add).then_inc(pool_wout, 1)

            def lower_in(r4, r2, n):
                eng.wait_ge(pool_win, n)
                eng.tensor_tensor(win_lo[:, r2, :], w_raw[:, r4, 0:W_IN], win_hi[:, r2, :].bitcast(f32),
                                  ALU.subtract).then_inc(low_win, 1)

            def lower_out(r4, n):
                eng.wait_ge(pool_wout, n)
                eng.tensor_tensor(wout_lo[:, r4, :], w_raw[:, r4, W_IN:W_ALL], wout_hi[:, r4, :].bitcast(f32),
                                  ALU.subtract).then_inc(low_wout, 1)

            def lower_bc(n):
                eng.wait_ge(pool_wbc, n)
                eng.tensor_tensor(wbc_lo[:], bc_raw[:, 0:BC_W], wbc_hi[:].bitcast(f32),
                                  ALU.subtract).then_inc(low_wbc, 1)

            eng.wait_ge(bc_in, 16)
            eng.tensor_scalar(wbc_hi[:], bc_raw[:, 0:BC_W], 1.0, 0.0, ALU.mult, ALU.add).then_inc(pool_wbc, 1)
            eng.wait_ge(w_in[0], 16)
            split_in(0, 0)
            split_out(0)
            lower_bc(1)
            lower_in(0, 0, 1)
            lower_out(0, 1)

            for t in range(TT):
                eng.wait_ge(pre_dve, DVE_HT + t + 1)
                eng.tensor_tensor(acc[:, t, :], acc[:, t, :], residual[t], ALU.add).then_inc(pre_pool, 1)
            eng.wait_ge(pre_act, ACT_TOK)

            def own_sums(s, r2):
                eng.tensor_copy(cs_own[:, r2], cs_tok[:, :, ds(2 * s, 2)]).then_inc(pool_own, 1)

            own_sums(0, 0)

            def slot(eng, s, g, k, first, last):
                r2, r4 = k % 2, k % 4
                n4 = (k + 1) % 4
                if not (last and k == PPG - 1):
                    eng.wait_ge(w_in[n4], 16 * (2 * g + (k + 1) // 4 + 1))
                    if first and 0 < k < 3:
                        eng.wait_ge(pe_gate, s)
                    if late(s - 2):
                        eng.wait_ge(pe_out, s - 2)
                if k == 4:
                    eng.wait_ge(bc_in, 16 * (g + 2))
                    eng.wait_ge(pe_bc, 2 * g + 2)
                if not (last and k == PPG - 1):
                    if late(s):
                        eng.wait_ge(dve_sub, 8 * s)
                    own_sums(s + 1, 1 - r2)
                if not (last and k == PPG - 1):
                    split_in(n4, (k + 1) % 2)
                    split_out(n4)
                    lower_in(n4, (k + 1) % 2, s + 2)
                    lower_out(n4, s + 2)
                if k == 4:
                    eng.tensor_scalar(wbc_hi[:], bc_raw[:, 0:BC_W], 1.0, 0.0, ALU.mult, ALU.add).then_inc(pool_wbc, 1)
                    lower_bc(g + 2)
                sum_squares(s, g, k, first)
                if k == 1 and not first:
                    eng.wait_ge(dve_ms, g)
                    eng.tensor_tensor(rstd[:], ms[:], half_neg[:], ALU.pow).then_inc(pool_rstd, 1)

            def sum_squares(s, g, k, first):
                if k == 1 or (first and k == 0):
                    return
                eng.wait_ge(act_sq, s)
                if k == 2:
                    if late(g):
                        eng.wait_ge(pe_ss, g)
                    eng.tensor_tensor(sqacc[:], sq[:, 0, :], sq[:, 1, :], ALU.add).then_inc(pool_sq, 1)
                else:
                    eng.wait_ge(pool_sq, (PPG - 1) * g + k - 2 if k else (PPG - 1) * (g - 1) + PPG - 2)
                    eng.tensor_tensor(sqacc[:], sqacc[:], sq[:, (k - 1) % 2, :], ALU.add).then_inc(pool_sq, 1)

            slots(eng, slot)
            eng.wait_ge(bc_in, 16 * (GROUPS + 2))
            eng.tensor_scalar(wffn_hi[:], bc_raw[:, 0:BC_W], 1.0, 0.0, ALU.mult, ALU.add).then_inc(pool_wbc, 1)
            eng.wait_ge(dve_ms, GROUPS)
            eng.tensor_tensor(rstd[:], ms[:], half_neg[:], ALU.pow).then_inc(pool_rstd, 1)

            def root(r, t):
                eng.wait_ge(ln_var, TT * r + t + 1)
                eng.tensor_tensor(lnr[:, r, t:t + 1], lnv[:, r, t:t + 1], half_neg[:, 0:1],
                                  ALU.pow).then_inc(ln_root, 1)

            def shift(t):
                eng.wait_ge(c_sum, 2)
                eng.wait_ge(r_add, t + 1)
                eng.tensor_tensor(qscaled[:, t, :], qscaled[:, t, :], ctxsum[:, t // 2, :], ALU.add).then_inc(x_shift, 1)

            def add_bias(t):
                eng.wait_ge(ffn_in, 64)
                eng.wait_ge(ln_out, TT + t + 1)
                eng.tensor_tensor(acc[:, t, :], acc[:, t, :], biasb[:], ALU.add).then_inc(bias_add, 1)

            for t in range(TT):
                root(0, t)
            eng.wait_ge(pool_wbc, GROUPS + 2)
            eng.tensor_tensor(wffn_lo[:], bc_raw[:, 0:BC_W], wffn_hi[:].bitcast(f32), ALU.subtract).then_inc(low_wbc, 1)
            eng.wait_ge(gate_split, 1)
            eng.tensor_tensor(gate_lo[:], gate_raw[:], gate_hi[:].bitcast(f32), ALU.subtract).then_inc(gate_low, 1)
            shift(0)
            shift(1)
            root(1, 0)
            shift(2)
            root(1, 1)
            shift(3)
            root(1, 2)
            root(1, 3)
            for t in range(TT):
                add_bias(t)
            eng.wait_ge(mix_dve, MIX_ABS)
            eng.partition_all_reduce(ffn_one[:, 1, 0:2], ffn_one[:, 0, 0:2], P,
                                     bass.bass_isa.ReduceOp.max).then_inc(mix_pool, 1)

        @block.scalar
        def _(eng):
            eng.wait_ge(wdt_in, 16)
            eng.activation(wdt_hi, wdt, ACT.Copy).then_inc(pre_act, 1)
            eng.wait_ge(pre_in, 32)
            for k in range(KT):
                eng.wait_ge(pre_pe, k + 1)
                eng.activation(hT_hi[:, k, :], ps_out[:, k, :], ACT.Identity, scale=normw[:, k:k + 1]).then_inc(pre_act, 1)
            eng.wait_ge(pre_dve, DVE_ABS)
            eng.activation(tmpA, tmpA, ACT.Exp, scale=-1.0).then_inc(pre_act, 1)
            eng.activation(negA[:], dtpar[:, 1:2], ACT.Exp).then_inc(pre_act, 1)

            def tap_bc(which, g, bank, out):
                base = BC_W + which * (TAPS + 1)
                eng.wait_ge(pe_bc, 2 * g + which + 1)
                if late(2 * g):
                    eng.wait_ge(act_bc, 2 * g + which)
                eng.activation(out, bank[:], ACT.Identity, bias=bc_raw[:, base + TAPS:base + TAPS + 1],
                               scale=bc_raw[:, base + TAPS - 1:base + TAPS]).then_inc(act_tapbc, 1)

            def silu_bc(which, g, src):
                eng.wait_ge(dve_convbc, 6 * g + 3 * which + 3)
                if late(2 * g):
                    eng.wait_ge(pe_cb, 2 * g)
                eng.activation(bcT[:, which, :], src, ACT.Silu).then_inc(act_bc, 1)

            def tap(s, g, k):
                r4 = k % 4
                eng.wait_ge(pe_hid, s + 1)
                eng.wait_ge(w_in[r4], 16 * (2 * g + k // 4 + 1))
                if late(s):
                    eng.wait_ge(act_hid, s)
                eng.activation(conv[:], ps_h[:], ACT.Identity, bias=w_raw[:, r4, W_ALL + 4:W_ALL + 5],
                               scale=w_raw[:, r4, W_ALL + 3:W_ALL + 4]).then_inc(act_tap, 1)

            eng.wait_ge(pre_dve, DVE_ONEP)
            eng.activation(tmpC, tmpB, ACT.Ln).then_inc(pre_act, 1)
            tap_bc(0, 0, ps_z, conv_bc[:])
            tap_bc(1, 0, ps_y, gate[:, 1, :])
            tap(0, 0, 0)
            silu_bc(0, 0, conv_bc[:])

            def slot(eng, s, g, k, first, last):
                if k == 0 and first:
                    eng.wait_ge(pre_pe, PE_TOK - 1)
                    eng.activation(dt_tok[:].rearrange("p t h -> p (t h)"), ps_out[:, 0, :], ACT.Copy).then_inc(pre_act, 1)
                    eng.wait_ge(pre_pe, PE_TOK)
                    eng.activation(cs_tok[:].rearrange("p t h -> p (t h)"), ps_out[:, 1, :], ACT.Copy).then_inc(pre_act, 1)
                    silu_bc(1, g, gate[:, 1, :])
                    hidden(s, k)
                    gates(s, k)
                    decays(s, k)
                    return
                if k == 0:
                    tap_bc(1, g, ps_z, conv_bc[:])
                    silu_bc(1, g, conv_bc[:])
                if k == PPG - 1 and not last:
                    tap_bc(0, g + 1, ps_z, conv_bc[:])
                    silu_bc(0, g + 1, conv_bc[:])
                tap(s, g, k)
                decays(s, k)
                hidden(s, k)
                gates(s, k)
                finish_y(s, g, k, first)
                if first:
                    scale_context(k - 1)
                if last and k == 4:
                    scale_context(PPG - 1)

            def decays(s, k):
                eng.wait_ge(dve_sub, 8 * s + 8)
                eng.activation(decay[:, k % 2].rearrange("p b h m -> p (b h m)"),
                               decay[:, k % 2].rearrange("p b h m -> p (b h m)"), ACT.Exp).then_inc(act_exp, 1)

            def hidden(s, k):
                eng.wait_ge(dve_conv, 3 * s + 3)
                if late(s - 1):
                    eng.wait_ge(dve_v, s - 1)
                eng.activation(hidT[:, k % 2, :], conv[:], ACT.Silu).then_inc(act_hid, 1)

            def gates(s, k):
                eng.wait_ge(pe_gate, s + 1)
                if late(s - 1):
                    eng.wait_ge(dve_yg, s - 1)
                eng.activation(gate[:, k % 2, :], ps_z[:], ACT.Silu).then_inc(act_gate, 1)

            def scale_context(k):
                if k == 0:
                    eng.wait_ge(ctx_in, 16)
                    eng.wait_ge(dve_half, 6)
                eng.activation(ctx_raw[:, k, :], ctx_raw[:, k, :], ACT.Identity, bias=qpar[:, 3:4],
                               scale=qinv[:, 1:2]).then_inc(act_ctx, 1)

            def finish_y(s, g, k, first):
                q2, q4 = (k - 1) % 2, (k - 1) % 4
                eng.wait_ge(dve_yg, s)
                if late(s - 2):
                    eng.wait_ge(pe_out, s - 2)
                eng.activation(y_hi[:, q2, :], yg[:, q2, :], ACT.Copy,
                               scale=w_raw[:, q4, W_ALL + 6:W_ALL + 7]).then_inc(act_yhi, 1)
                if not (first and k < 3):
                    gs, ks = (g, k - 3) if k >= 3 else (g - 1, k - 3 + PPG)
                    eng.wait_ge(pool_sq, (PPG - 1) * gs + max(ks, 1))
                eng.activation(sq[:, q2, :], yg[:, q2, :], ACT.Square).then_inc(act_sq, 1)

            slots(eng, slot)
            finish_y(PAIRS, GROUPS, 0, False)

            eng.wait_ge(ffn_in, 64)
            eng.activation(gate_hi[:], gate_raw[:], ACT.Copy).then_inc(gate_split, 1)

            def column_sums(b):
                eng.wait_ge(c_mm, b + 1)
                eng.wait_ge(dve_sub, 8 * PAIRS)
                eng.activation(ctxsum[:, b, :], work[2 + b][:], ACT.Identity, bias=qcon[:, 3:4],
                               scale=qcon[:, 0:1]).then_inc(c_sum, 1)

            def shifted(t):
                eng.wait_ge(x_mm, t + 1)
                eng.activation(rowsum[:, t:t + 1], ps_out[:, t, D // 2:D // 2 + 1], ACT.Copy,
                               scale=qcon[:, 1:2]).then_inc(r_sum, 1)
                eng.wait_ge(r_sum, t + 1)
                eng.wait_ge(q_round, t + 1)
                eng.activation(qscaled[:, t, :], work[t][:], ACT.Identity, bias=rowsum[:, t:t + 1]).then_inc(r_add, 1)

            def scaled(t):
                eng.wait_ge(ln_out, t + 1)
                eng.wait_ge(dve_sub, 8 * PAIRS)
                eng.activation(qscaled[:, t, :], normed[:, t, :], ACT.Identity, bias=qpar[:, 1:2],
                               scale=qinv[:, 0:1]).then_inc(q_scaled, 1)

            def q_turned(t):
                eng.wait_ge(q_tr, t + 1)
                eng.wait_ge(dve_v, PAIRS)
                eng.activation(qT[:, t, :], ps_out[:, t, :].bitcast(bf16)[:, 0:D], ACT.Copy).then_inc(q_copy, 1)

            def n_upper(t):
                eng.wait_ge(n_tr, t + 1)
                eng.activation(xT_hi[:, t, :], ps_out[:, t, :], ACT.Copy).then_inc(n_hi, 1)

            column_sums(0)
            column_sums(1)
            scaled(0)
            scaled(1)
            q_turned(0)
            scaled(2)
            q_turned(1)
            shifted(0)
            scaled(3)
            q_turned(2)
            shifted(1)
            q_turned(3)
            shifted(2)
            shifted(3)
            n_upper(0)
            n_upper(1)
            eng.wait_ge(bmat_in, 16)
            eng.wait_ge(dve_ylo, PAIRS)
            eng.wait_ge(pe_out, PAIRS)
            eng.activation(bst[0:RANK, :], bmat, ACT.Copy).then_inc(bst_done, 1)
            eng.activation(bst[2 * RANK:3 * RANK, :], bmat, ACT.Copy).then_inc(bst_done, 1)

            def gate_copy(t):
                eng.wait_ge(g_mm, t + 1)
                eng.activation(zh[:, t * P:(t + 1) * P], ps_out[0:GATE, t, 0:P], ACT.Copy).then_inc(g_copy, 1)

            gate_copy(0)
            n_upper(2)
            gate_copy(1)
            n_upper(3)
            gate_copy(2)
            gate_copy(3)
            eng.wait_ge(mix_dve, MIX_LOGITS)
            eng.activation(ffn_small[:, 3], ffn_small[:, 2], ACT.Exp).then_inc(mix_act, 1)
            eng.wait_ge(mix_dve, MIX_THRESH)
            eng.activation(ffn_small[:, 6], ffn_small[:, 5], ACT.Exp, scale=-2.0).then_inc(mix_act, 1)
            eng.wait_ge(mix_pe, 2)
            eng.activation(wT, ps_out[0:EXPERTS, 1, :], ACT.Copy).then_inc(mix_act, 1)
            eng.wait_ge(mix_dve, MIX_ZP)
            eng.activation(zst[0:RANK, :], zp, ACT.Copy).then_inc(mix_act, 1)
            eng.activation(zst[RANK:2 * RANK, :], zp, ACT.Copy).then_inc(mix_act, 1)

        @block.vector
        def _(eng):
            n_pre = [0]

            def pre(ins):
                n_pre[0] += 1
                ins.then_inc(pre_dve, 1)

            for t in range(TT):
                eng.wait_ge(x_in[t], 16)
                pre(eng.bn_stats(stats[:, t, :], acc[:, t, :]))
            for t in range(TT):
                eng.wait_ge(pre_dve, t + 1)
                pre(eng.bn_aggr(mv[:, t, :], stats[:, t, :]))
            eng.wait_ge(pre_dve, n_pre[0])
            pre(eng.tensor_scalar(lnv[:, 0, :], mv[:, :, 1], 1.0 + EPS_RMS, EPS * EPS_RMS, ALU.mult, ALU.add))
            pre(eng.tensor_scalar(ms[:], mv[:, :, 1], EPS, None, ALU.add))
            assert n_pre[0] == DVE_VAR
            eng.wait_ge(pre_act, 1)
            pre(eng.tensor_tensor(wdt_lo, wdt, wdt_hi.bitcast(f32), ALU.subtract))
            eng.wait_ge(pre_pool, 10)
            for t in range(TT):
                pre(eng.tensor_scalar(hnorm[:, t, :], acc[:, t, :], mv[:, t, 0:1], lnr[:, 0, t:t + 1],
                                      ALU.subtract, ALU.mult))
            assert n_pre[0] == DVE_H
            for k in range(KT):
                eng.wait_ge(pre_act, 2 + k)
                pre(eng.scalar_tensor_tensor(out=hT_lo[:, k, :], in0=ps_out[:, k, :], scalar=normw[:, k:k + 1],
                                             in1=hT_hi[:, k, :].bitcast(f32), op0=ALU.mult, op1=ALU.subtract))
            assert n_pre[0] == DVE_HT
            eng.wait_ge(pre_pool, 11)
            for t in range(TT):
                pre(eng.tensor_scalar(residual[t], acc[:, t, :], mv[:, t, 0:1], rstd[:, t:t + 1],
                                      ALU.subtract, ALU.mult))
            pre(eng.memset(onesT, 1.0))
            assert n_pre[0] == DVE_R
            eng.wait_ge(pre_pe, PE_DT)
            pre(eng.tensor_scalar(dtT, ps_h[:], dtpar[:, 0:1], None, ALU.add))
            assert n_pre[0] == DVE_V
            eng.wait_ge(pre_dve, n_pre[0])
            pre(eng.scalar_tensor_tensor(out=tmpA, in0=dtT, scalar=-1.0, in1=dtT, op0=ALU.mult, op1=ALU.max))
            assert n_pre[0] == DVE_ABS
            eng.wait_ge(pre_act, 6)
            pre(eng.tensor_scalar(tmpB, tmpA, 1.0, None, ALU.add))
            assert n_pre[0] == DVE_ONEP
            eng.wait_ge(pre_dve, n_pre[0])
            pre(eng.scalar_tensor_tensor(out=tmpA, in0=tmpB, scalar=-1.0, in1=tmpA, op0=ALU.add, op1=ALU.subtract))

            def convolve(out, src, w, done, count):
                src_b = src.rearrange("p (b t) -> p b t", b=B)
                out_b = out.rearrange("p (b t) -> p b t", b=B)
                for n, back in enumerate((1, 2, 3)):
                    if n:
                        eng.wait_ge(done, count + n)
                    eng.scalar_tensor_tensor(out=out_b[:, :, back:], in0=src_b[:, :, 0:S - back],
                                             scalar=w[:, TAPS - 1 - back:TAPS - back], in1=out_b[:, :, back:],
                                             op0=ALU.mult, op1=ALU.add).then_inc(done, 1)

            def conv_group(which, g, bank, out):
                base = BC_W + which * (TAPS + 1)
                eng.wait_ge(act_tapbc, 2 * g + which + 1)
                convolve(out, bank[:], bc_raw[:, base:base + TAPS], dve_convbc, 6 * g + 3 * which)

            eng.wait_ge(pre_act, 8)
            eng.wait_ge(pre_dve, n_pre[0])
            pre(eng.tensor_tensor(tmpC, tmpC, tmpA, ALU.subtract))
            eng.wait_ge(pre_dve, n_pre[0])
            pre(eng.scalar_tensor_tensor(out=dtT, in0=dtT, scalar=0.0, in1=tmpC, op0=ALU.max, op1=ALU.add))
            eng.wait_ge(pre_dve, n_pre[0])
            eng.wait_ge(pre_act, 7)
            pre(eng.tensor_scalar(tmpA, dtT, negA[:], -1.0, ALU.mult, ALU.mult))
            eng.wait_ge(pre_dve, n_pre[0])
            for b in range(B):
                pre(eng.tensor_tensor_scan(csT[:, b * S:(b + 1) * S], onesT[:, b * S:(b + 1) * S],
                                           tmpA[:, b * S:(b + 1) * S], 0.0, ALU.mult, ALU.add))
            assert n_pre[0] == DVE_CS
            conv_group(0, 0, ps_z, conv_bc[:])

            def slot(eng, s, g, k, first, last):
                r2 = k % 2
                if not (first and k == 0):
                    scale_hidden(s, k)
                if k == 2 and not first:
                    add_group(g - 1)
                if k == PPG - 1 and not last:
                    conv_group(0, g + 1, ps_z, conv_bc[:])
                if k == 0:
                    conv_group(1, g, *((ps_y, gate[:, 1, :]) if first else (ps_z, conv_bc[:])))
                if first and k == 0:
                    conv_hidden(s, k)
                exponents(s, g, k)
                if k == 0:
                    if late(s):
                        eng.wait_ge(dve_m, s)
                    eng.wait_ge(pe_cb, 2 * g + 1)
                    eng.tensor_tensor(cbm[:, 1, :], (ps_y if first else ps_z)[:, 0:MJ], causal[:], ALU.mult).then_inc(dve_cb, 1)
                    eng.wait_ge(pe_cb, 2 * g + 2)
                    eng.tensor_tensor(cbm[:, 0, :], ps_t[:, 0:MJ], causal[:], ALU.mult).then_inc(dve_cb, 1)
                if not (first and k == 0):
                    conv_hidden(s, k)
                if k == 1 and not first:
                    mean_squares(g - 1)
                if first and k == 1:
                    eng.wait_ge(pre_pool, 11 + TT)
                if not (first and k == 0):
                    combine(s, k)
                eng.wait_ge(act_exp, s + 1)
                if k == 0:
                    eng.wait_ge(dve_cb, 2 * g + 2)
                eng.tensor_tensor(decay[:, r2], decay[:, r2], cbm[:].unsqueeze(2).broadcast_to([P, B, 2, MJ]),
                                  ALU.mult).then_inc(dve_m, 1)
                if not (first and k == 0):
                    lower_y(s, k)
                if first and k == 0:
                    constants()
                if first and k >= 2:
                    quantise_context(k - 2)
                if last and k in (4, 5):
                    quantise_context(k + 2)

            def conv_hidden(s, k):
                eng.wait_ge(act_tap, s + 1)
                convolve(conv[:], ps_h[:], w_raw[:, k % 4, W_ALL:W_ALL + TAPS], dve_conv, 3 * s)

            def constants():
                eng.wait_ge(qpar_in, 16)
                for n in range(2):
                    eng.reciprocal(qinv[:, n:n + 1], qpar[:, 2 * n:2 * n + 1]).then_inc(dve_half, 1)
                    eng.tensor_scalar(qcon[:, n:n + 1], qpar[:, 2 * n + 1:2 * n + 2], -1.0, CENTRE, ALU.mult,
                                      ALU.add).then_inc(dve_half, 1)
                eng.tensor_tensor(qcon[:, 2:3], qpar[:, 0:1], qpar[:, 2:3], ALU.mult).then_inc(dve_half, 1)
                eng.wait_ge(dve_half, 5)
                eng.tensor_scalar(qcon[:, 3:4], qcon[:, 0:1], qcon[:, 1:2], float(CTX), ALU.mult,
                                  ALU.mult).then_inc(dve_half, 1)

            def quantise_context(k):
                x = ctx_raw[:, k, :]
                eng.wait_ge(act_ctx, k + 1)
                eng.tensor_scalar(x, x, 0.0, 255.0, ALU.max, ALU.min).then_inc(dve_ctx, 1)
                eng.wait_ge(dve_ctx, 2 * k + 1)
                eng.tensor_scalar(ctxq(k), x, ROUND, -(ROUND + CENTRE), ALU.add, ALU.add).then_inc(dve_ctx, 1)

            def exponents(s, g, k):
                r2, r4 = k % 2, k % 4
                eng.wait_ge(csb_in[r4], 16 * (2 * g + k // 4 + 1))
                eng.wait_ge(pool_own, s + 1)
                if late(s - 1):
                    eng.wait_ge(pe_y, s - 1)
                for b in range(B):
                    for h in range(2):
                        for j, (lo, n) in enumerate(((0, S), (S, P))):
                            eng.tensor_scalar(decay[:, r2, b, h, lo:lo + n],
                                              csb[:, r4, h, (b + 1) * S - n:(b + 1) * S],
                                              cs_own[:, r2, 2 * b + j, h:h + 1], 0.0,
                                              ALU.subtract, ALU.min).then_inc(dve_sub, 1)

            def scale_hidden(s, k):
                q2 = (k - 1) % 2
                eng.wait_ge(pe_tr, s)
                if late(s - 2):
                    eng.wait_ge(pe_y, s - 2)
                own = dt_tok[:, :, ds(2 * (s - 1), 2)].unsqueeze(3).broadcast_to([P, TT, 2, HD])
                eng.tensor_tensor(hid_dt[:, q2].rearrange("p t (h c) -> p t h c", h=2),
                                  ps_t[:].rearrange("p (t h c) -> p t h c", t=TT, h=2), own,
                                  ALU.mult).then_inc(dve_hiddt, 1)

            def combine(s, k):
                q2, q4 = (k - 1) % 2, (k - 1) % 4
                eng.wait_ge(pe_y, s)
                eng.wait_ge(act_hid, s)
                if late(s - 1):
                    eng.wait_ge(dve_yg, s - 1)
                eng.scalar_tensor_tensor(out=v[:], in0=hidT[:, q2, :], scalar=w_raw[:, q4, W_ALL + 5:W_ALL + 6],
                                         in1=ps_y[:], op0=ALU.mult, op1=ALU.add).then_inc(dve_v, 1)
                eng.wait_ge(act_gate, s)
                if late(s - 2):
                    eng.wait_ge(dve_ylo, s - 2)
                eng.wait_ge(dve_v, s)
                eng.tensor_tensor(yg[:, q2, :], v[:], gate[:, q2, :], ALU.mult).then_inc(dve_yg, 1)

            def lower_y(s, k):
                q2, q4 = (k - 1) % 2, (k - 1) % 4
                eng.wait_ge(act_yhi, s)
                eng.scalar_tensor_tensor(out=y_lo[:, q2, :], in0=yg[:, q2, :],
                                         scalar=w_raw[:, q4, W_ALL + 6:W_ALL + 7],
                                         in1=y_hi[:, q2, :].bitcast(f32), op0=ALU.mult,
                                         op1=ALU.subtract).then_inc(dve_ylo, 1)

            def mean_squares(g):
                eng.wait_ge(pe_ss, g + 1)
                eng.tensor_scalar(ms[:], ps_t[:, 0:TT], 1.0 / (INNER // GROUPS), EPS_G, ALU.mult,
                                  ALU.add).then_inc(dve_ms, 1)

            def add_group(g):
                eng.wait_ge(pool_rstd, g + 1)
                eng.wait_ge(pe_out, PPG * (g + 1))
                for t in range(TT):
                    add_tile(t)

            def add_tile(t):
                eng.scalar_tensor_tensor(out=acc[:, t, :], in0=ps_out[:, t, :], scalar=rstd[:, t:t + 1],
                                         in1=acc[:, t, :], op0=ALU.mult, op1=ALU.add).then_inc(dve_acc, 1)

            slots(eng, slot)
            scale_hidden(PAIRS, 0)
            combine(PAIRS, 0)
            lower_y(PAIRS, 0)
            eng.wait_ge(pe_ss, GROUPS)
            eng.tensor_reduce(ms[:], ps_t[:, 0:2 * TT].rearrange("p (n t) -> p t n", t=TT), AX.X, ALU.add).then_inc(dve_half, 1)
            eng.wait_ge(dve_half, 7)
            eng.tensor_scalar(ms[:], ms[:], 1.0 / (INNER // GROUPS), EPS_G, ALU.mult, ALU.add).then_inc(dve_ms, 1)
            eng.tensor_reduce(odd[:], ident[:].rearrange("p (n two) -> p n two", two=2)[:, :, 1], AX.X,
                              ALU.add).then_inc(dve_half, 1)
            eng.wait_ge(pool_rstd, GROUPS)
            eng.wait_ge(pe_out, PAIRS)

            def variance(r, t):
                eng.bn_stats(stats[:, t, :], acc[:, t, :]).then_inc(ln_step, 1)
                eng.wait_ge(ln_step, 2 * (TT * r + t) + 1)
                eng.bn_aggr(mv[:, t, :], stats[:, t, :]).then_inc(ln_step, 1)
                eng.wait_ge(ln_step, 2 * (TT * r + t) + 2)
                eng.tensor_scalar(lnv[:, r, t:t + 1], mv[:, t, 1:2], EPS, None, ALU.add).then_inc(ln_var, 1)

            def norm(r, t):
                eng.wait_ge(ln_root, TT * r + t + 1)
                if r:
                    eng.wait_ge(q_scaled, t + 1)
                eng.tensor_scalar(normed[:, t, :], acc[:, t, :], mv[:, t, 0:1], lnr[:, r, t:t + 1],
                                  ALU.subtract, ALU.mult).then_inc(ln_out, 1)

            def last_group(t):
                add_tile(t)
                eng.wait_ge(dve_acc, TT * (GROUPS - 1) + t + 1)
                variance(0, t)

            def quantise(t):
                eng.wait_ge(q_scaled, t + 1)
                eng.tensor_scalar(qscaled[:, t, :], qscaled[:, t, :], 0.0, 255.0, ALU.max, ALU.min).then_inc(q_step, 1)
                eng.wait_ge(q_step, t + 1)
                eng.tensor_scalar(qround[:, t, :], qscaled[:, t, :], ROUND, -(ROUND + CENTRE), ALU.add,
                                  ALU.add).then_inc(q_round, 1)

            def cross(t):
                eng.wait_ge(x_shift, t + 1)
                eng.scalar_tensor_tensor(out=acc[:, t, :], in0=qscaled[:, t, :], scalar=qcon[:, 2:3],
                                         in1=acc[:, t, :], op0=ALU.mult, op1=ALU.add).then_inc(x_add, 1)
                eng.wait_ge(x_add, t + 1)
                variance(1, t)

            def n_lower(t):
                eng.wait_ge(n_hi, t + 1)
                eng.tensor_tensor(xT_lo[:, t, :], ps_out[:, t, :], xT_hi[:, t, :].bitcast(f32),
                                  ALU.subtract).then_inc(n_lo, 1)

            last_group(0)
            last_group(1)
            norm(0, 0)
            last_group(2)
            norm(0, 1)
            quantise(0)
            last_group(3)
            norm(0, 2)
            quantise(1)
            norm(0, 3)
            quantise(2)
            quantise(3)
            cross(0)
            cross(1)
            norm(1, 0)
            cross(2)
            norm(1, 1)
            n_lower(0)
            cross(3)
            norm(1, 2)
            n_lower(1)
            norm(1, 3)
            n_lower(2)
            eng.wait_ge(bst_done, 1)
            eng.tensor_tensor(bst[RANK:2 * RANK, :], bmat, bst[0:RANK, :].bitcast(f32), ALU.subtract).then_inc(bstlo_done, 1)
            n_lower(3)

            n_mix = [0]

            def mix(ins):
                n_mix[0] += 1
                ins.then_inc(mix_dve, 1)

            def settle():
                eng.wait_ge(mix_dve, n_mix[0])

            hs, dl, lg, ex, pr, df, sg, wt, ab = (ffn_small[:, i] for i in range(9))
            wide = [P, TT, EXPERTS]
            eng.wait_ge(mix_pe, 1)
            eng.wait_ge(h_turned, 1)
            mix(eng.tensor_tensor(hs, ps_out[:, 2, 0:TT * EXPERTS].rearrange("p (t e) -> p t e", t=TT),
                                  biasb[:, 0:EXPERTS].unsqueeze(1).broadcast_to(wide), ALU.add))
            mix(eng.tensor_copy(dl, ps_out[:, 3, 0:TT * EXPERTS].rearrange("p (t e) -> p t e", t=TT)))
            settle()
            for n, src in enumerate((hs, dl)):
                mix(eng.scalar_tensor_tensor(out=(ab, wt)[n], in0=src, scalar=-1.0, in1=src, op0=ALU.mult, op1=ALU.max))
            settle()
            for n in range(2):
                mix(eng.tensor_reduce(ffn_one[:, 2, n:n + 1], (ab, wt)[n], AX.XY, ALU.max))
            settle()
            eng.wait_ge(dve_half, 8)
            mix(eng.tensor_scalar(ffn_one[:, 0, 0:2], ffn_one[:, 2, 0:2], odd[:], None, ALU.mult))
            assert n_mix[0] == MIX_ABS
            eng.wait_ge(mix_pool, 1)
            mix(eng.tensor_scalar(ffn_one[:, 3, 0:2], ffn_one[:, 1, 0:2], 1e-6, None, ALU.max))
            settle()
            mix(eng.reciprocal(ffn_one[:, 4, 0:2], ffn_one[:, 3, 0:2]))
            settle()
            mix(eng.tensor_scalar(hs, hs, ffn_one[:, 4, 0:1], 0.5, ALU.mult, ALU.mult))
            mix(eng.tensor_scalar(dl, dl, ffn_one[:, 4, 1:2], 0.5, ALU.mult, ALU.mult))
            settle()
            mix(eng.tensor_tensor(hs, hs, dl, ALU.add))
            settle()
            mix(eng.tensor_reduce(ffn_one[:, 5, :], hs, AX.X, ALU.max))
            settle()
            mix(eng.tensor_tensor(lg, hs, ffn_one[:, 5, :].unsqueeze(2).broadcast_to(wide), ALU.subtract))
            assert n_mix[0] == MIX_LOGITS
            eng.wait_ge(mix_act, 1)
            mix(eng.tensor_reduce(ffn_one[:, 6, :], ex, AX.X, ALU.add))
            settle()
            mix(eng.reciprocal(ffn_one[:, 7, :], ffn_one[:, 6, :]))
            settle()
            mix(eng.tensor_tensor(pr, ex, ffn_one[:, 7, :].unsqueeze(2).broadcast_to(wide), ALU.mult))
            settle()
            for t in range(TT):
                mix(eng.max(ab[:, t, :], pr[:, t, :]))
            settle()
            mix(eng.tensor_tensor(df, pr, ab[:, :, 1:2].broadcast_to(wide), ALU.subtract))
            assert n_mix[0] == MIX_THRESH
            eng.wait_ge(mix_act, 2)
            mix(eng.tensor_scalar(sg, sg, 1.0, None, ALU.add))
            settle()
            mix(eng.reciprocal(sg, sg))
            settle()
            mix(eng.tensor_tensor(wt, pr, sg, ALU.mult))
            settle()
            mix(eng.tensor_reduce(ffn_one[:, 5, :], wt, AX.X, ALU.add))
            settle()
            mix(eng.tensor_scalar(ffn_one[:, 5, :], ffn_one[:, 5, :], 1e-9, None, ALU.add))
            settle()
            mix(eng.reciprocal(ffn_one[:, 6, :], ffn_one[:, 5, :]))
            settle()
            mix(eng.tensor_tensor(wt, wt, ffn_one[:, 6, :].unsqueeze(2).broadcast_to(wide), ALU.mult))
            assert n_mix[0] == MIX_WT
            eng.wait_ge(mix_pe, 3)
            mix(eng.scalar_tensor_tensor(out=zp, in0=zh[0:RANK, :], scalar=OUT_SCALE, in1=ps_out[0:RANK, 0, :],
                                         op0=ALU.mult, op1=ALU.mult))
            assert n_mix[0] == MIX_ZP
            eng.wait_ge(mix_act, 4)
            mix(eng.tensor_tensor(zst[2 * RANK:3 * RANK, :], zp, zst[0:RANK, :].bitcast(f32), ALU.subtract))
            for t in range(TT):
                eng.wait_ge(d_mm, t + 1)
                eng.wait_ge(bias_add, t + 1)
                eng.tensor_tensor(acc[:, t, :], acc[:, t, :], work[t][:], ALU.add).then_inc(y_done, 1)

        @block.tensor
        def _(eng):
            mm = nc.tensor.matmul

            def tr(out, src, n=P):
                return nc.tensor.transpose(out, src, ident[:n, :n])

            def keep_up(bank, n):
                for _ in range(n):
                    mm(bank[:, 0:P], identb[:], identb[:], start=True, stop=True)

            eng.wait_ge(pre_pool, 9)
            keep_up(ps_t, WARM_UP)
            for t in range(TT):
                eng.wait_ge(pre_dve, DVE_H - TT + t + 1)
                for k in range(KT):
                    last = tr(ps_out[:, k, t * P:(t + 1) * P], hnorm[:, t, k * P:(k + 1) * P])
                    if t == TT - 1:
                        last.then_inc(pre_pe, 1)

            def project(out, w_hi, w_lo, done):
                n = 0
                for w, h in ((w_hi, hT_hi), (w_hi, hT_lo), (w_lo, hT_hi)):
                    for k in range(KT):
                        last = mm(out, w[:, k * P:(k + 1) * P], h[:, k, :], start=n == 0, stop=n == 3 * KT - 1)
                        n += 1
                last.then_inc(done, 1)

            for k in range(KT):
                eng.wait_ge(pre_act, 2 + k)
                mm(ps_h[:], wdt_hi[:, k * P:(k + 1) * P], hT_hi[:, k, :], start=k == 0, stop=False)
            eng.wait_ge(pre_dve, DVE_H)
            for k in range(KT):
                mm(ps_h[:], wdt_lo[:, k * P:(k + 1) * P], hT_hi[:, k, :], start=False, stop=False)
            for k in range(KT):
                eng.wait_ge(pre_dve, DVE_H + k + 1)
                last = mm(ps_h[:], wdt_hi[:, k * P:(k + 1) * P], hT_lo[:, k, :], start=False, stop=k == KT - 1)
            last.then_inc(pre_pe, 1)
            eng.wait_ge(low_wbc, 1)
            project(ps_z[:], wbc_hi[:, 0:KT * P], wbc_lo[:, 0:KT * P], pe_bc)

            def start_up():
                project(ps_y[:], wbc_hi[:, KT * P:], wbc_lo[:, KT * P:], pe_bc)
                eng.wait_ge(pre_dve, DVE_CS)
                for n, src in enumerate((dtT, csT)):
                    for t in range(TT):
                        last = tr(ps_out[:, n, t * P:(t + 1) * P], src[:, t * P:(t + 1) * P])
                    last.then_inc(pre_pe, 1)
                eng.wait_ge(dve_convbc, 3)
                project(ps_z[:], win_hi[:, 0, KT * P:], win_lo[:, 0, KT * P:], pe_gate)

            def slot(eng, s, g, k, first, last):
                r2 = k % 2
                eng.wait_ge(low_win, s + 1)
                if late(3 * s):
                    eng.wait_ge(dve_conv, 3 * s)
                if first and k == 0:
                    eng.wait_ge(pre_dve, DVE_V)
                project(ps_h[:], win_hi[:, r2, 0:KT * P], win_lo[:, r2, 0:KT * P], pe_hid)
                if first and k == 0:
                    start_up()
                if not (first and k == 0):
                    scan_heads(s, k)
                if k == 0:
                    eng.wait_ge(act_bc, 2 * g + 2)
                    if late(s):
                        eng.wait_ge(act_gate, s)
                    for b, bank in ((1, ps_y if first else ps_z), (0, ps_t)):
                        q = b * S
                        mm(bank[:, 0:S], bcT[:, 0, q:q + P], bcT[:, 1, q:q + S], start=True, stop=True)
                        mm(bank[:, S:MJ], bcT[:, 0, q + P:q + S], bcT[:, 1, q + P:q + S], start=True,
                           stop=True).then_inc(pe_cb, 1)
                if k == 1 and not first:
                    sum_channels(g - 1)
                if not (first and k == 0):
                    eng.wait_ge(act_gate, s)
                    if k == 0:
                        eng.wait_ge(dve_cb, 2 * g + 1)
                    if k == PPG - 1 and not last:
                        eng.wait_ge(dve_convbc, 6 * (g + 1) + 3)
                    project(ps_z[:], win_hi[:, r2, KT * P:], win_lo[:, r2, KT * P:], pe_gate)
                if not (first and k < 2):
                    project_out(s, g, k)
                eng.wait_ge(act_hid, s + 1)
                if k == 0:
                    eng.wait_ge(dve_cb, 2 * g + 2)
                if k == 1 and not first:
                    eng.wait_ge(dve_ms, g)
                for t in range(TT):
                    done = tr(ps_t[:, t * P:(t + 1) * P], hidT[:, r2, t * P:(t + 1) * P])
                done.then_inc(pe_tr, 1)
                if k >= PPG - 2 and not last:
                    which = k - (PPG - 2)
                    eng.wait_ge(low_wbc, g + 2)
                    eng.wait_ge(act_gate, s + 1)
                    project(ps_z[:], wbc_hi[:, which * KT * P:(which + 1) * KT * P],
                            wbc_lo[:, which * KT * P:(which + 1) * KT * P], pe_bc)

            def scan_heads(s, k):
                q2 = (k - 1) % 2
                eng.wait_ge(dve_hiddt, s)
                eng.wait_ge(dve_m, s)
                if late(s - 1):
                    eng.wait_ge(dve_v, s - 1)
                for h in range(2):
                    for b in range(B):
                        out = ps_y[h * HD:(h + 1) * HD, b * S:(b + 1) * S]
                        mm(out, hid_dt[:, q2, 2 * b, h * HD:(h + 1) * HD], decay[:, q2, b, h, 0:S],
                           start=True, stop=False)
                        done = mm(out[:, P:S], hid_dt[:, q2, 2 * b + 1, h * HD:(h + 1) * HD],
                                  decay[:, q2, b, h, S:MJ], start=False, stop=True)
                done.then_inc(pe_y, 1)

            def project_out(s, g, k):
                pair, q2, q4 = (k - 2) % PPG, (k - 2) % 2, (k - 2) % 4
                eng.wait_ge(dve_ylo, s - 1)
                for t in range(TT):
                    if k == 2 and late(TT * g):
                        eng.wait_ge(dve_acc, TT * (g - 1) + t + 1)
                    for n, (y, w) in enumerate(((y_hi, wout_hi), (y_hi, wout_lo), (y_lo, wout_hi))):
                        done = mm(ps_out[:, t, :], y[:, q2, t * P:(t + 1) * P], w[:, q4, :],
                                  start=pair == 0 and n == 0, stop=pair == PPG - 1 and n == 2)
                done.then_inc(pe_out, 1)

            def sum_channels(g):
                eng.wait_ge(pool_sq, (PPG - 1) * (g + 1))
                for t in range(TT):
                    done = mm(ps_t[:, t:t + 1], sqacc[:, t * P:(t + 1) * P], ones[:], start=True, stop=True)
                done.then_inc(pe_ss, 1)

            slots(eng, slot)
            scan_heads(PAIRS, 0)
            project_out(PAIRS, GROUPS, 0)
            eng.wait_ge(pool_sq, (PPG - 1) * GROUPS - 1)
            eng.wait_ge(dve_hiddt, PAIRS)
            for t in range(TT):
                mm(ps_t[:, t:t + 1], sqacc[:, t * P:(t + 1) * P], ones[:], start=True, stop=True)
            eng.wait_ge(low_wout, PAIRS)
            project_out(PAIRS + 1, GROUPS, 1)
            eng.wait_ge(act_sq, PAIRS)
            for t in range(TT):
                done = mm(ps_t[:, TT + t:TT + t + 1], sq[:, (PAIRS - 1) % 2, t * P:(t + 1) * P], ones[:],
                          start=True, stop=True)
            done.then_inc(pe_ss, 1)
            eng.wait_ge(dve_ctx, 2 * PPG)
            eng.wait_ge(dve_v, PAIRS)
            eng.wait_ge(dve_ms, GROUPS)
            for b in range(B):
                for k in range(KT):
                    done = mm(work[2 + b][:], onesb[:], ctxq(b * KT + k), start=k == 0, stop=k == KT - 1)
                done.then_inc(c_mm, 1)

            def products(out, lower, upper, t, passes=(0, 1, 2)):
                for n in passes:
                    x, part = ((xT_hi, upper), (xT_hi, lower), (xT_lo, upper))[n]
                    for k in range(KT):
                        mm(out, x[:, t, k * P:(k + 1) * P], part(k), start=n == 0 and k == 0,
                           stop=n == 2 and k == KT - 1)

            def turn_rounded(t):
                eng.wait_ge(q_round, t + 1)
                eng.wait_ge(dve_acc, TT * (GROUPS - 1) + t + 1)
                bank = ps_out[:, t, :].bitcast(bf16)
                for k in range(KT):
                    done = nc.tensor.transpose(bank[:, k * P:(k + 1) * P], qround[:, t, k * P:(k + 1) * P], identb[:])
                done.then_inc(q_tr, 1)

            def cross(t):
                eng.wait_ge(q_copy, t + 1)
                for k in range(KT):
                    turned = qT[:, t, k * P:(k + 1) * P]
                    mm(work[t][:], turned, ctxq(t // 2 * KT + k), start=k == 0, stop=k == KT - 1)
                    done = mm(ps_out[:, t, D // 2:D // 2 + 1], turned, onesb[:, 0:1], start=k == 0, stop=k == KT - 1)
                done.then_inc(x_mm, 1)

            def turn_normed(t):
                eng.wait_ge(ln_out, TT + t + 1)
                for k in range(KT):
                    done = tr(ps_out[:, t, k * P:(k + 1) * P], normed[:, t, k * P:(k + 1) * P])
                done.then_inc(n_tr, 1)

            def gate_columns(t):
                eng.wait_ge(n_lo, t + 1)
                eng.wait_ge(gate_low, 1)
                n = 0
                for w, x in ((gate_hi, xT_hi), (gate_hi, xT_lo), (gate_lo, xT_hi)):
                    for k in range(KT):
                        done = mm(ps_out[0:GATE, t, 0:P], w[:, k, :], x[:, t, k * P:(k + 1) * P], start=n == 0,
                                  stop=n == 3 * KT - 1)
                        n += 1
                done.then_inc(g_mm, 1)

            def ffn(t, passes=(0, 1, 2)):
                eng.wait_ge(x_add, t + 1)
                eng.wait_ge(low_wbc, GROUPS + 2)
                products(work[t][:], lambda k: wffn(k, True), lambda k: wffn(k, False), t, passes)

            keep_up(work[0], 2 * WARM_UP)
            for t in range(TT):
                turn_rounded(t)
                if t >= 2:
                    eng.wait_ge(c_sum, t - 1)
                keep_up(work[t], WARM_UP // 5)
                cross(t)
            eng.wait_ge(r_add, 1)
            keep_up(work[0], WARM_UP // 3)
            turn_normed(0)
            keep_up(work[0], WARM_UP // 3)
            turn_normed(1)
            gate_columns(0)
            ffn(0, (0,))
            turn_normed(2)
            gate_columns(1)
            turn_normed(3)
            gate_columns(2)
            ffn(0, (1,))
            gate_columns(3)
            eng.wait_ge(g_copy, TT)
            for t in range(TT):
                done = nc.tensor.transpose(ps_out[:, 2, t * EXPERTS:(t + 1) * EXPERTS], zh[RANK:GATE, t * P:(t + 1) * P],
                                           ident[RANK:GATE, RANK:GATE])
            done.then_inc(h_turned, 1)
            for t in range(TT):
                done = mm(ps_out[:, 3, t * EXPERTS:(t + 1) * EXPERTS], zh[0:RANK, t * P:(t + 1) * P], limesT[:],
                          start=True, stop=True)
            done.then_inc(mix_pe, 1)
            ffn(0, (2,))
            ffn(1)
            ffn(2)
            ffn(3, (0,))
            eng.wait_ge(mix_dve, MIX_WT)
            for t in range(TT):
                done = tr(ps_out[0:EXPERTS, 1, t * P:(t + 1) * P], ffn_small[:, 7, t, :])
            done.then_inc(mix_pe, 1)
            eng.wait_ge(mix_act, 3)
            anchors = wT.rearrange("e (a two) -> e a two", two=2)[:, :, 1:2].broadcast_to([EXPERTS, T // 2, 2])
            mm(ps_out[0:RANK, 0, :], limes[:], anchors, start=True, stop=True).then_inc(mix_pe, 1)
            ffn(3, (1, 2))
            eng.wait_ge(mix_dve, MIX_ZP + 1)
            eng.wait_ge(mix_act, 5)
            eng.wait_ge(bstlo_done, 1)
            eng.wait_ge(bst_done, 2)
            for t in range(TT):
                mm(work[t][:], zst[:, t * P:(t + 1) * P], bst, start=False, stop=True,
                   skip_group_check=True).then_inc(d_mm, 1)


DVE_VAR = 2 * TT + 2
DVE_H = DVE_VAR + 1 + TT
DVE_HT = DVE_H + KT
DVE_R = DVE_HT + TT + 1
DVE_V = DVE_R + 1
DVE_ABS = DVE_V + 1
DVE_ONEP = DVE_ABS + 1
DVE_CS = DVE_ONEP + 4 + B
PE_DT = KT + 1
PE_TOK = PE_DT + 2
ACT_TOK = KT + 6
MIX_ABS = 7
MIX_LOGITS = MIX_ABS + 7
MIX_THRESH = MIX_LOGITS + 3 + TT + 1
MIX_WT = MIX_THRESH + 7
MIX_ZP = MIX_WT + 1


def lay_out(i):
    import numpy as np

    a = {k: np.asarray(x) for k, x in i.items()}

    def by_width(w):
        return w.T.reshape(KT, P, -1).transpose(1, 0, 2)

    win, conv_w, conv_b = a["L0_attn_in_proj_w"], a["L0_attn_conv_w"], a["L0_attn_conv_b"]
    gates, hidden = win[:INNER], win[INNER:2 * INNER]
    gn = GROUPS * P
    rows_b, rows_c = win[2 * INNER:2 * INNER + gn], win[2 * INNER + gn:2 * INNER + 2 * gn]
    rows_dt = win[2 * INNER + 2 * gn:]
    wout = a["L0_attn_out_proj_w"].T
    d_ch = np.repeat(a["L0_attn_Dp"], HD)
    gnorm = a["L0_attn_gnorm_w"]
    wmain = np.zeros((PAIRS, P, W_ROW), np.float32)
    for s in range(PAIRS):
        c = slice(s * P, (s + 1) * P)
        wmain[s, :, 0:KT * P] = by_width(hidden[c]).reshape(P, -1)
        wmain[s, :, KT * P:W_IN] = by_width(gates[c]).reshape(P, -1)
        wmain[s, :, W_IN:W_ALL] = wout[c]
        wmain[s, :, W_ALL:W_ALL + TAPS] = conv_w[c]
        wmain[s, :, W_ALL + 4] = conv_b[c]
        wmain[s, :, W_ALL + 5] = d_ch[c]
        wmain[s, :, W_ALL + 6] = gnorm[c]
    wbc = np.zeros((GROUPS, P, BC_ROW), np.float32)
    for g in range(GROUPS):
        c = slice(g * P, (g + 1) * P)
        for n, rows in enumerate((rows_b, rows_c)):
            at = BC_W + n * (TAPS + 1)
            cc = slice(INNER + n * gn + g * P, INNER + n * gn + (g + 1) * P)
            wbc[g, :, n * KT * P:(n + 1) * KT * P] = by_width(rows[c]).reshape(P, -1)
            wbc[g, :, at:at + TAPS] = conv_w[cc]
            wbc[g, :, at + TAPS] = conv_b[cc]
    return {
        "x": a["x"], "ctx": a["ctx_4096"],
        "wdt": by_width(rows_dt).reshape(P, -1),
        "dtpar": np.stack([a["L0_attn_dt_bias"], a["L0_attn_A_log"]], 1),
        "normw": a["L0_attn_norm_w"].reshape(KT, P).T,
        "wmain": wmain, "wbc": wbc,
        "quant": np.stack([a["L0_xattn_x1_scale"], a["L0_xattn_x1_zp"], a["L0_xattn_x2_scale"],
                           a["L0_xattn_x2_zp"]], 0),
        "wffn": by_width(a["L0_ffn_W"]).reshape(P, -1), "ffnb": a["L0_ffn_b"].reshape(1, D),
        "gate": np.concatenate([a["L0_ffn_A"], a["L0_ffn_W"][:EXPERTS].T], 1).reshape(KT, P, GATE).transpose(1, 0, 2),
        "bmat": a["L0_ffn_Bmat"], "limes": a["L0_ffn_LiMEs"], "limest": a["L0_ffn_LiMEs"].T,
    }


def kernel(**inputs):
    import numpy as np
    import concourse.bacc as bacc
    from concourse import mybir as mb
    from concourse.bass_utils import run_bass_kernel_spmd

    nc = bacc.Bacc("TRN2", target_bir_lowering=False, num_devices=1)
    arrays, args = {}, []
    for name, a in lay_out(inputs).items():
        a = np.ascontiguousarray(a)
        arrays[f"in_{name}"] = a
        args.append(nc.dram_tensor(f"in_{name}", a.shape, mb.dt.from_np(a.dtype), kind="ExternalInput").ap())
    args.append(nc.dram_tensor("out_x", (B, S, D), mb.dt.float32, kind="ExternalOutput").ap())
    build(nc, *args)
    r = run_bass_kernel_spmd(nc, [arrays], core_ids=[0])
    return r.results[0]["out_x"]
```
